# Optimizing a Trainium2 kernel written in Bass

```python
import numpy as np
import jax
import jax.numpy as jnp

def _softmax(x, axis=-1):
    return jax.nn.softmax(x, axis=axis)

def _gelu(x):
    return jax.nn.gelu(x, approximate=True)

def _silu(x):
    return jax.nn.silu(x)

def _sigmoid(x):
    return jax.nn.sigmoid(x)

def _layernorm(x, axis=-1, eps=1e-05):
    m = jnp.mean(x, axis=axis, keepdims=True)
    v = jnp.var(x, axis=axis, keepdims=True)
    return (x - m) / jnp.sqrt(v + eps)

def _scatter_add(tgt, idx, src, axis=0):
    return tgt.at[idx].add(src)

def _segment_sum(src, seg, n):
    return jax.ops.segment_sum(src, seg, n)
kernel_name = 'mk_seq_postln_d2_jaxref_r8_11f098'

def setup_inputs(seed: int=0):
    np.random.seed(seed)
    _w = jnp.asarray

    def _L0_attn_setup():
        import jax, jax.numpy as jnp
        import numpy as np
        D_MODEL = 128
        D_HIDDEN = 32
        key = jax.random.key(seed)
        ks = jax.random.split(key, 10)
        B, T = (4, 512)
        s = lambda fan_in: 1.0 / np.sqrt(fan_in)
        return {'x': jax.random.normal(ks[0], (B, T, D_MODEL), dtype=jnp.float32), 'A': jnp.log(jnp.arange(1, D_HIDDEN + 1, dtype=jnp.float32)), 'Wb': jax.random.uniform(ks[1], (D_MODEL, D_HIDDEN), jnp.float32, -s(D_MODEL), s(D_MODEL)), 'bb': jax.random.uniform(ks[2], (D_HIDDEN,), jnp.float32, -s(D_MODEL), s(D_MODEL)), 'Wc': jax.random.uniform(ks[3], (D_HIDDEN, D_MODEL), jnp.float32, -s(D_HIDDEN), s(D_HIDDEN)), 'bc': jax.random.uniform(ks[4], (D_MODEL,), jnp.float32, -s(D_HIDDEN), s(D_HIDDEN)), 'Wd': jax.random.uniform(ks[5], (D_MODEL, D_MODEL), jnp.float32, -s(D_MODEL), s(D_MODEL)), 'bd': jax.random.uniform(ks[6], (D_MODEL,), jnp.float32, -s(D_MODEL), s(D_MODEL)), 'Wdelta': jax.random.uniform(ks[7], (D_MODEL, D_HIDDEN), jnp.float32, -s(D_MODEL), s(D_MODEL)), 'bdelta': jax.random.uniform(ks[8], (D_HIDDEN,), jnp.float32, -s(D_MODEL), s(D_MODEL))}
    _L0_attn_in = _L0_attn_setup()

    def _L0_ffn_setup():
        import jax, jax.numpy as jnp
        import numpy as np
        DIM = 128

        def _reference_tuple_inner(x, W_r, W_k, W_v, mu_r, mu_k):
            B, T, C = x.shape
            x_prev = jnp.concatenate([jnp.zeros((B, 1, C), x.dtype), x[:, :-1, :]], axis=1)
            xr = mu_r * x + (1.0 - mu_r) * x_prev
            xk = mu_k * x + (1.0 - mu_k) * x_prev
            r = jax.nn.sigmoid(jnp.einsum('btc,dc->btd', xr, W_r))
            k = jnp.einsum('btc,dc->btd', xk, W_k)
            k_act = jnp.square(jax.nn.relu(k))
            out = r * jnp.einsum('btc,dc->btd', k_act, W_v)
            new_state = x[:, -1, :]
            return (out, new_state)
        key = jax.random.key(seed)
        ks = jax.random.split(key, 6)
        B, T, C = (8, 256, DIM)
        x = jax.random.normal(ks[0], (B, T, C), dtype=jnp.float32)
        s = 1.0 / np.sqrt(C)
        W_r = jax.random.uniform(ks[1], (C, C), jnp.float32, -s, s)
        W_k = jax.random.uniform(ks[2], (C, C), jnp.float32, -s, s)
        W_v = jax.random.uniform(ks[3], (C, C), jnp.float32, -s, s)
        mu_r = jax.random.uniform(ks[4], (C,), jnp.float32)
        mu_k = jax.random.uniform(ks[5], (C,), jnp.float32)
        return {'x': x, 'W_r': W_r, 'W_k': W_k, 'W_v': W_v, 'mu_r': mu_r, 'mu_k': mu_k}
    _L0_ffn_in = _L0_ffn_setup()

    def _L1_attn_setup():
        import jax, jax.numpy as jnp
        import numpy as np
        DIM = 128
        NUM_HEADS = 16
        HEAD_DIM = DIM // NUM_HEADS
        TAU = 2.0
        V_TH = 1.0
        BN_EPS = 1e-05

        def _branch(x, W, gamma, beta):
            B, N, D = x.shape
            h = jnp.einsum('bnd,ed->bne', x, W)
            hf = h.reshape(B * N, D)
            mean = jnp.mean(hf, axis=0)
            var = jnp.var(hf, axis=0)
            hn = (hf - mean) * jax.lax.rsqrt(var + BN_EPS) * gamma + beta
            hn = hn.reshape(B, N, D)
            return jax.nn.sigmoid(4.0 * (hn - V_TH))

        def _heads(x):
            B, N, D = x.shape
            return x.reshape(B, N, NUM_HEADS, HEAD_DIM).transpose(0, 2, 1, 3)
        key = jax.random.key(seed)
        ks = jax.random.split(key, 12)
        B, N, D = (8, 512, DIM)
        s = 0.02
        return {'x': jax.random.normal(ks[0], (B, N, D), dtype=jnp.float32), 'Wq': jax.random.normal(ks[1], (D, D), dtype=jnp.float32) * s, 'gq': jnp.ones((D,), jnp.float32), 'bq': jnp.zeros((D,), jnp.float32), 'Wk': jax.random.normal(ks[2], (D, D), dtype=jnp.float32) * s, 'gk': jnp.ones((D,), jnp.float32), 'bk': jnp.zeros((D,), jnp.float32), 'Wv': jax.random.normal(ks[3], (D, D), dtype=jnp.float32) * s, 'gv': jnp.ones((D,), jnp.float32), 'bv': jnp.zeros((D,), jnp.float32), 'Wp': jax.random.normal(ks[4], (D, D), dtype=jnp.float32) * s, 'bp': jnp.zeros((D,), jnp.float32)}
    _L1_attn_in = _L1_attn_setup()

    def _L1_ffn_setup():
        import jax, jax.numpy as jnp
        import numpy as np
        HIDDEN = 128
        MOE_INTER = 64
        SHARED_INTER = 256
        N_EXPERTS = 32
        TOP_K = 6
        N_GROUP = 8
        TOPK_GROUP = 4
        ROUTED_SCALE = 2.5

        def _relu2(x):
            return jnp.square(jax.nn.relu(x))

        def _router(x, gate_w, e_bias):
            T = x.shape[0]
            logits = x.astype(jnp.float32) @ gate_w.astype(jnp.float32).T
            scores = jax.nn.sigmoid(logits)
            sc = scores + e_bias[None, :]
            g = sc.reshape(T, N_GROUP, N_EXPERTS // N_GROUP)
            group_scores = jax.lax.top_k(g, 2)[0].sum(-1)
            group_idx = jax.lax.top_k(group_scores, TOPK_GROUP)[1]
            group_mask = jnp.zeros_like(group_scores).at[jnp.arange(T)[:, None], group_idx].set(1.0)
            score_mask = jnp.repeat(group_mask, N_EXPERTS // N_GROUP, axis=1)
            masked = jnp.where(score_mask > 0, sc, 0.0)
            topk_idx = jax.lax.stop_gradient(jax.lax.top_k(masked, TOP_K)[1])
            topk_w = jnp.take_along_axis(scores, topk_idx, axis=1)
            topk_w = topk_w / (topk_w.sum(-1, keepdims=True) + 1e-20)
            topk_w = topk_w * ROUTED_SCALE
            return (topk_idx, topk_w)
        if __name__ == '__main__':
            out = reference(**setup_inputs())
            print(out.shape, out.dtype)
        key = jax.random.key(seed)
        ks = jax.random.split(key, 6)
        s = 0.02
        return {'hidden_states': jax.random.normal(ks[0], (2, 128, HIDDEN), jnp.float32), 'gate_w': jax.random.normal(ks[1], (N_EXPERTS, HIDDEN), jnp.float32) * s, 'e_bias': jnp.zeros((N_EXPERTS,), jnp.float32), 'up_w': jax.random.normal(ks[2], (N_EXPERTS, MOE_INTER, HIDDEN), jnp.float32) * s, 'down_w': jax.random.normal(ks[3], (N_EXPERTS, HIDDEN, MOE_INTER), jnp.float32) * s, 'shared_up_w': jax.random.normal(ks[4], (SHARED_INTER, HIDDEN), jnp.float32) * s, 'shared_down_w': jax.random.normal(ks[5], (HIDDEN, SHARED_INTER), jnp.float32) * s}
    _L1_ffn_in = _L1_ffn_setup()
    _d = {'L0_attn_x': _L0_attn_in['x'], 'L0_attn_A': _L0_attn_in['A'], 'L0_attn_Wb': _L0_attn_in['Wb'], 'L0_attn_bb': _L0_attn_in['bb'], 'L0_attn_Wc': _L0_attn_in['Wc'], 'L0_attn_bc': _L0_attn_in['bc'], 'L0_attn_Wd': _L0_attn_in['Wd'], 'L0_attn_bd': _L0_attn_in['bd'], 'L0_attn_Wdelta': _L0_attn_in['Wdelta'], 'L0_attn_bdelta': _L0_attn_in['bdelta'], 'L0_ffn_W_r': _L0_ffn_in['W_r'], 'L0_ffn_W_k': _L0_ffn_in['W_k'], 'L0_ffn_W_v': _L0_ffn_in['W_v'], 'L0_ffn_mu_r': _L0_ffn_in['mu_r'], 'L0_ffn_mu_k': _L0_ffn_in['mu_k'], 'L1_attn_Wq': _L1_attn_in['Wq'], 'L1_attn_gq': _L1_attn_in['gq'], 'L1_attn_bq': _L1_attn_in['bq'], 'L1_attn_Wk': _L1_attn_in['Wk'], 'L1_attn_gk': _L1_attn_in['gk'], 'L1_attn_bk': _L1_attn_in['bk'], 'L1_attn_Wv': _L1_attn_in['Wv'], 'L1_attn_gv': _L1_attn_in['gv'], 'L1_attn_bv': _L1_attn_in['bv'], 'L1_attn_Wp': _L1_attn_in['Wp'], 'L1_attn_bp': _L1_attn_in['bp'], 'L1_ffn_gate_w': _L1_ffn_in['gate_w'], 'L1_ffn_e_bias': _L1_ffn_in['e_bias'], 'L1_ffn_up_w': _L1_ffn_in['up_w'], 'L1_ffn_down_w': _L1_ffn_in['down_w'], 'L1_ffn_shared_up_w': _L1_ffn_in['shared_up_w'], 'L1_ffn_shared_down_w': _L1_ffn_in['shared_down_w']}
    _x0 = _d['L0_attn_x']
    _d['L0_attn_x'] = jax.random.normal(jax.random.fold_in(jax.random.key(seed), 1), (32, 256, 128), dtype=_x0.dtype)
    del _x0
    return _d

def reference(L0_attn_x, L0_attn_A, L0_attn_Wb, L0_attn_bb, L0_attn_Wc, L0_attn_bc, L0_attn_Wd, L0_attn_bd, L0_attn_Wdelta, L0_attn_bdelta, L0_ffn_W_r, L0_ffn_W_k, L0_ffn_W_v, L0_ffn_mu_r, L0_ffn_mu_k, L1_attn_Wq, L1_attn_gq, L1_attn_bq, L1_attn_Wk, L1_attn_gk, L1_attn_bk, L1_attn_Wv, L1_attn_gv, L1_attn_bv, L1_attn_Wp, L1_attn_bp, L1_ffn_gate_w, L1_ffn_e_bias, L1_ffn_up_w, L1_ffn_down_w, L1_ffn_shared_up_w, L1_ffn_shared_down_w):

    def _L0_attn_ref(x, A, Wb, bb, Wc, bc, Wd, bd, Wdelta, bdelta):
        import jax, jax.numpy as jnp
        import numpy as np
        D_MODEL = 128
        D_HIDDEN = 32
        delta = jax.nn.softplus(jnp.einsum('btc,ch->bth', x, Wdelta) + bdelta)
        A_log = -jax.nn.softplus(A)
        A_bar_log = delta * A_log
        B_bar = delta * (jnp.einsum('btc,ch->bth', x, Wb) + bb)
        A_log_cum = jnp.clip(jnp.cumsum(A_bar_log, axis=1), -20.0, 20.0)
        A_log_cum_shifted = jnp.concatenate([jnp.zeros_like(A_log_cum[:, :1, :]), A_log_cum[:, :-1, :]], axis=1)
        B_shift = B_bar * jnp.exp(-A_log_cum_shifted)
        h = jnp.exp(A_log_cum) * jnp.cumsum(B_shift, axis=1)
        out = jnp.einsum('bth,hc->btc', h, Wc) + bc + jnp.einsum('btc,cd->btd', x, Wd) + bd
        return out

    def _L0_ffn_ref(x, W_r, W_k, W_v, mu_r, mu_k):
        import jax, jax.numpy as jnp
        import numpy as np
        DIM = 128

        def _reference_tuple_inner(x, W_r, W_k, W_v, mu_r, mu_k):
            B, T, C = x.shape
            x_prev = jnp.concatenate([jnp.zeros((B, 1, C), x.dtype), x[:, :-1, :]], axis=1)
            xr = mu_r * x + (1.0 - mu_r) * x_prev
            xk = mu_k * x + (1.0 - mu_k) * x_prev
            r = jax.nn.sigmoid(jnp.einsum('btc,dc->btd', xr, W_r))
            k = jnp.einsum('btc,dc->btd', xk, W_k)
            k_act = jnp.square(jax.nn.relu(k))
            out = r * jnp.einsum('btc,dc->btd', k_act, W_v)
            new_state = x[:, -1, :]
            return (out, new_state)
        return _reference_tuple_inner(x, W_r, W_k, W_v, mu_r, mu_k)[0]

    def _L1_attn_ref(x, Wq, gq, bq, Wk, gk, bk, Wv, gv, bv, Wp, bp):
        import jax, jax.numpy as jnp
        import numpy as np
        DIM = 128
        NUM_HEADS = 16
        HEAD_DIM = DIM // NUM_HEADS
        TAU = 2.0
        V_TH = 1.0
        BN_EPS = 1e-05

        def _branch(x, W, gamma, beta):
            B, N, D = x.shape
            h = jnp.einsum('bnd,ed->bne', x, W)
            hf = h.reshape(B * N, D)
            mean = jnp.mean(hf, axis=0)
            var = jnp.var(hf, axis=0)
            hn = (hf - mean) * jax.lax.rsqrt(var + BN_EPS) * gamma + beta
            hn = hn.reshape(B, N, D)
            return jax.nn.sigmoid(4.0 * (hn - V_TH))

        def _heads(x):
            B, N, D = x.shape
            return x.reshape(B, N, NUM_HEADS, HEAD_DIM).transpose(0, 2, 1, 3)
        B, N, D = x.shape
        scale = HEAD_DIM ** (-0.5)
        q = _branch(x, Wq, gq, bq)
        k = _branch(x, Wk, gk, bk)
        v = _branch(x, Wv, gv, bv)
        qk = _heads(q * k) * scale
        v_h = _heads(v)
        vv = jnp.einsum('bhnd,bhne->bhde', v_h, v_h)
        out = jnp.einsum('bhnd,bhde->bhne', qk, vv)
        out = out.transpose(0, 2, 1, 3).reshape(B, N, D)
        return jnp.einsum('bnd,ed->bne', out, Wp) + bp

    def _L1_ffn_ref(hidden_states, gate_w, e_bias, up_w, down_w, shared_up_w, shared_down_w):
        import jax, jax.numpy as jnp
        import numpy as np
        HIDDEN = 128
        MOE_INTER = 64
        SHARED_INTER = 256
        N_EXPERTS = 32
        TOP_K = 6
        N_GROUP = 8
        TOPK_GROUP = 4
        ROUTED_SCALE = 2.5

        def _relu2(x):
            return jnp.square(jax.nn.relu(x))

        def _router(x, gate_w, e_bias):
            T = x.shape[0]
            logits = x.astype(jnp.float32) @ gate_w.astype(jnp.float32).T
            scores = jax.nn.sigmoid(logits)
            sc = scores + e_bias[None, :]
            g = sc.reshape(T, N_GROUP, N_EXPERTS // N_GROUP)
            group_scores = jax.lax.top_k(g, 2)[0].sum(-1)
            group_idx = jax.lax.top_k(group_scores, TOPK_GROUP)[1]
            group_mask = jnp.zeros_like(group_scores).at[jnp.arange(T)[:, None], group_idx].set(1.0)
            score_mask = jnp.repeat(group_mask, N_EXPERTS // N_GROUP, axis=1)
            masked = jnp.where(score_mask > 0, sc, 0.0)
            topk_idx = jax.lax.stop_gradient(jax.lax.top_k(masked, TOP_K)[1])
            topk_w = jnp.take_along_axis(scores, topk_idx, axis=1)
            topk_w = topk_w / (topk_w.sum(-1, keepdims=True) + 1e-20)
            topk_w = topk_w * ROUTED_SCALE
            return (topk_idx, topk_w)
        if __name__ == '__main__':
            out = reference(**setup_inputs())
            print(out.shape, out.dtype)
        B, S, H = hidden_states.shape
        x = hidden_states.reshape(-1, H)
        T = x.shape[0]
        topk_idx, topk_w = _router(x, gate_w, e_bias)
        combine = jnp.zeros((T, N_EXPERTS), topk_w.dtype).at[jnp.arange(T)[:, None], topk_idx].add(topk_w)
        h = _relu2(jnp.einsum('th,eih->tei', x, up_w))
        h = h * combine[:, :, None]
        moe_out = jnp.einsum('tei,ehi->th', h, down_w)
        shared = _relu2(x @ shared_up_w.T) @ shared_down_w.T
        return (moe_out + shared).reshape(B, S, H)
    x = L0_attn_x
    x = _layernorm(x + _L0_attn_ref(x, L0_attn_A, L0_attn_Wb, L0_attn_bb, L0_attn_Wc, L0_attn_bc, L0_attn_Wd, L0_attn_bd, L0_attn_Wdelta, L0_attn_bdelta), axis=-1)
    x = _layernorm(x + _L0_ffn_ref(x, L0_ffn_W_r, L0_ffn_W_k, L0_ffn_W_v, L0_ffn_mu_r, L0_ffn_mu_k), axis=-1)
    x = _layernorm(x + _L1_attn_ref(x, L1_attn_Wq, L1_attn_gq, L1_attn_bq, L1_attn_Wk, L1_attn_gk, L1_attn_bk, L1_attn_Wv, L1_attn_gv, L1_attn_bv, L1_attn_Wp, L1_attn_bp), axis=-1)
    x = _layernorm(x + _L1_ffn_ref(x, L1_ffn_gate_w, L1_ffn_e_bias, L1_ffn_up_w, L1_ffn_down_w, L1_ffn_shared_up_w, L1_ffn_shared_down_w), axis=-1)
    return x

_drawn_inputs = setup_inputs


def setup_inputs(seed=0):
    import zlib

    import numpy as np

    out = dict(_drawn_inputs(seed))
    spreads = {'L1_attn_gq': (1.0, 0.2),
     'L1_attn_bq': (0.0, 0.1),
     'L1_attn_gk': (1.0, 0.2),
     'L1_attn_bk': (0.0, 0.1),
     'L1_attn_gv': (1.0, 0.2),
     'L1_attn_bv': (0.0, 0.1),
     'L1_attn_bp': (0.0, 0.1),
     'L1_ffn_e_bias': (0.0, 0.769)}
    factors = {'L0_attn_bd': 2.827,
     'L0_ffn_mu_r': 8.0,
     'L1_ffn_gate_w': 8.0,
     'L1_ffn_up_w': 6.123,
     'L1_ffn_down_w': 5.818,
     'L1_ffn_shared_up_w': 3.115}
    for name, (base, spread) in spreads.items():
        noise = np.random.default_rng([zlib.crc32(name.encode()), seed]).standard_normal(out[name].shape)
        drawn = base * np.exp(spread * noise) if base else spread * noise
        out[name] = jnp.asarray(drawn.astype(out[name].dtype))
    for name, factor in factors.items():
        out[name] = (out[name] * factor).astype(out[name].dtype)
    return out
```

```python
from contextlib import ExitStack

import numpy as np
import concourse.bass as bass
from concourse import mybir

F32 = mybir.dt.float32
F32R = mybir.dt.float32r
BF16 = mybir.dt.bfloat16
ALU = mybir.AluOpType
ACT = mybir.ActivationFunctionType
AX = mybir.AxisListType

P = 128
B, T, D = 32, 256, 128
NTOK = B * T
CH = 512
NCH = NTOK // CH
TT = CH // P
BC = CH // T
HID = 32
NE, INTER, SHARED = 32, 64, 256
NG, GE = 8, 4
TOPG, TOPK = 4, 6
ROUTED_SCALE = 2.5
NRB = NE * INTER // P
NB = NRB + SHARED // P
EPS = 1e-5
NEG = -3.0e38
TAKEN = 3.0e38
HD = 8
V_TH = 1.0

ROWS = ["bc", "bd", "mu_r", "mu_k", "gq", "bq", "gk", "bk", "gv", "bv", "bp", "A", "bdelta", "bb"]
COL = {n: i for i, n in enumerate(ROWS)}
SQ = ["W_r", "W_k", "W_v", "Wq", "Wk", "Wv", "Wp"]


def need(eng, sem, n):
    if isinstance(n, int) and n <= 0:
        return
    eng.wait_ge(sem, n)


def pipeline(eng, stages, n, depth):
    first = depth + 2 + depth % 2
    last = n - n % 2

    def step(s, parity):
        for delay, fn in stages:
            c = s - delay
            if isinstance(s, int) and not 0 <= c < n:
                continue
            fn(c, (parity - delay) % 2)

    for s in range(first):
        step(s, s % 2)
    with eng.Fori(first // 2, last // 2) as i:
        for parity in (0, 1):
            step(2 * i + parity, parity)
    for s in range(last, n + depth):
        step(s, s % 2)


def build(nc, t, out):
    with ExitStack() as ctx:
        def sb(name, shape, dt=F32):
            return ctx.enter_context(nc.sbuf_tensor(name, shape, dt))

        m = {}
        m["act"] = sb("act_ch", [P, NTOK])
        m["tok"] = sb("x2_tok", [P, NTOK // P, D])
        m["hT"] = sb("scan_h", [P, NTOK // 4])
        m["cT"] = sb("combine_ch", [3 * NE, NTOK], BF16)
        for n in ("up_hi", "up_lo", "dn_hi", "dn_lo"):
            m[n] = sb(n, [P, NB, P], F32R)
        m["sqT"] = sb("square_T", [P, len(SQ), P])
        m["wv_nat"] = sb("wv_natural", [P, P])
        m["wdI"] = sb("wd_plus_identity", [P, P])
        m["wc_pad"] = sb("wc_padded", [P, 4, P])
        m["wdelta_pad"] = sb("wdelta_padded", [P, 4, P])
        m["wb_pad"] = sb("wb_padded", [P, 4, P])
        m["gateT"] = sb("gate_T", [P, NE])
        m["ebias"] = sb("e_bias_rows", [P, NE])
        m["cols"] = sb("channel_columns", [P, len(ROWS)])
        m["aux"] = sb("derived_columns", [P, 16])
        m["ident"] = sb("identity", [P, P])
        m["identb"] = sb("identity_bf16", [P, P], BF16)
        m["identr"] = sb("identity_f32r", [P, P], F32R)
        m["ones"] = sb("ones", [P, P])
        m["onesb"] = sb("ones_bf16", [3, P], BF16)
        m["headmask"] = sb("head_mask", [P, P])
        m["sel"] = sb("expert_select", [3 * NE, NRB, P], BF16)
        m["gram"] = sb("gram", [P, P + 1])
        m["wvT"] = sb("wv_scaled_T", [P, P])
        m["vb3"] = sb("v_bias_rows", [3, TT, P], BF16)
        m["bp3"] = sb("bp_rows", [3, TT, P], BF16)
        m["brow"] = sb("bias_columns", [P, 2])

        prepare(nc, t, m)
        scan_block(nc, t, m)
        first_block(nc, t, m)
        fold_block(nc, t, m)
        second_block(nc, t, m)
        experts_block(nc, t, m, out)


def prepare(nc, t, m):
    with ExitStack() as ctx:
        sb = lambda n, s, d=F32: ctx.enter_context(nc.sbuf_tensor(n, s, d))
        sem = lambda n: ctx.enter_context(nc.semaphore(n))
        bank = [ctx.enter_context(nc.psum_tensor(f"prep{i}", [P, 4, P], F32)) for i in range(4)]
        up_raw = sb("up_raw", [P, NB, P])
        dn_raw = sb("down_raw", [P, NB, P])
        sq_raw = sb("square_raw", [P, len(SQ), P])
        gate_raw = sb("gate_raw", [NE, P])
        rows = sb("vector_rows", [len(ROWS), P])
        eb_row = sb("e_bias_row", [1, NE])
        wide = sb("select_wide", [3 * NE, NRB * P])
        zero_done, ident_done, small_in, big_in = sem("zero_done"), sem("ident_done"), sem("small_in"), sem("big_in")
        turned, evac_act, evac_dve, masks = sem("turned"), sem("evac_act"), sem("evac_dve"), sem("masks_step")
        row_in = sem("row_in")

        jobs = [("cols", 0), ("gate", 0), ("ebias", 0)]
        jobs += [("sq", i) for i in range(len(SQ))]
        jobs += [("up", j) for j in range(NB)] + [("dn", j) for j in range(NB)]
        single, groups = jobs[:3], []
        for kind, n in (("sq", len(SQ)), ("up", NB), ("dn", NB)):
            for a in range(0, n, 4):
                groups.append((kind, a, min(4, n - a)))
        order = [(k, 0, 1) for k, _ in single] + groups
        dve_n, act_n, dn_, an_ = [], [], 0, 0
        for kind, a, n in order:
            if kind in ("up", "dn"):
                an_ += 1
            dn_ += 1
            act_n.append(an_)
            dve_n.append(dn_)

        block = ctx.enter_context(nc.Block())

        @block.sync
        def _(e):
            for r, name in enumerate(ROWS):
                src = t[name]
                if name in ("A", "bdelta", "bb"):
                    for k in range(4):
                        e.dma_start(rows[r:r + 1, HID * k:HID * (k + 1)],
                                    src.rearrange("(a c) -> a c", a=1)).then_inc(row_in, 16)
                else:
                    e.dma_start(rows[r:r + 1, :], src.rearrange("(a c) -> a c", a=1)).then_inc(row_in, 16)
            e.dma_start(eb_row[:, :], t["e_bias"].rearrange("(a c) -> a c", a=1)).then_inc(row_in, 16)
            e.dma_start(gate_raw[:, :], t["gate_w"]).then_inc(row_in, 16)
            for i, name in enumerate(SQ):
                e.dma_start(sq_raw[:, i, :], t[name]).then_inc(small_in, 16)
            e.dma_start(m["wdI"][:, :], t["Wd"]).then_inc(small_in, 16)
            e.dma_start(m["wv_nat"][:, :], t["Wv"]).then_inc(small_in, 16)
            e.wait_ge(zero_done, 3)
            for k in range(4):
                e.dma_start(m["wc_pad"][HID * k:HID * (k + 1), k, :], t["Wc"]).then_inc(small_in, 16)
                e.dma_start(m["wdelta_pad"][:, k, HID * k:HID * (k + 1)], t["Wdelta"]).then_inc(small_in, 16)
                e.dma_start(m["wb_pad"][:, k, HID * k:HID * (k + 1)], t["Wb"]).then_inc(small_in, 16)

        @block.scalar
        def _(e):
            e.dma_start(up_raw[:, 0:NRB, :], t["up_w"].rearrange("(j e) i h -> (e i) j h", e=2)).then_inc(big_in, 16)
            e.dma_start(up_raw[:, NRB:NB, :], t["shared_up_w"].rearrange("(j p) h -> p j h", p=P)).then_inc(big_in, 16)
            for ee in range(2):
                e.dma_start(dn_raw[:, 0:NRB, INTER * ee:INTER * (ee + 1)],
                            t["down_w"].rearrange("(j e) h i -> e h j i", e=2)[ee]).then_inc(big_in, 16)
            e.dma_start(dn_raw[:, NRB:NB, :], t["shared_down_w"].rearrange("h (j p) -> h j p", p=P)).then_inc(big_in, 16)
            for g, (kind, a, n) in enumerate(order):
                if kind in ("up", "dn"):
                    e.wait_ge(turned, g + 1)
                    e.activation(m[kind + "_hi"][:, a:a + n, :], bank[g % 4][:, 0:n, :], ACT.Copy).then_inc(evac_act, 1)

        @block.gpsimd
        def _(e):
            e.memset(m["ident"][:, :], 0.0).then_inc(masks, 1)
            e.memset(m["ones"][:, :], 1.0).then_inc(masks, 1)
            e.wait_ge(masks, 2)
            e.affine_select(out=m["ident"][:, :], in_=m["ident"][:, :], compare_op=ALU.not_equal, fill=1.0,
                            base=0, pattern=[[-1, P]], channel_multiplier=1).then_inc(ident_done, 1)
            e.affine_select(out=m["headmask"][:, :].rearrange("p (a b) -> p a b", b=HD),
                            in_=m["ones"][:, :].rearrange("p (a b) -> p a b", b=HD),
                            compare_op=ALU.is_ge, fill=0.0, base=0, pattern=[[-HD, P // HD], [0, HD]],
                            channel_multiplier=1).then_inc(masks, 1)
            e.wait_ge(masks, 3)
            e.affine_select(out=m["headmask"][:, :].rearrange("p (a b) -> p a b", b=HD),
                            in_=m["headmask"][:, :].rearrange("p (a b) -> p a b", b=HD),
                            compare_op=ALU.is_ge, fill=0.0, base=HD - 1, pattern=[[HD, P // HD], [0, HD]],
                            channel_multiplier=-1).then_inc(masks, 1)
            e.memset(wide[:, :], 0.0).then_inc(masks, 1)
            for part in range(3):
                e.wait_ge(masks, 5 + part)
                w = wide[:, :].rearrange("p (j c) -> p j c", c=INTER)
                e.affine_select(out=w, in_=w, compare_op=ALU.not_equal, fill=1.0, base=-NE * part,
                                pattern=[[-1, NE], [0, INTER]], channel_multiplier=1).then_inc(masks, 1)

        @block.tensor
        def _(e):
            e.wait_ge(ident_done, 1)
            for g, (kind, a, n) in enumerate(order):
                if g == 0:
                    e.wait_ge(row_in, 16 * (len(ROWS) + 9 + 2))
                if kind == "sq":
                    e.wait_ge(small_in, 16 * (len(SQ) + 14))
                if kind in ("up", "dn"):
                    e.wait_ge(big_in, 16 * 5)
                if g >= 4:
                    need(e, evac_act, act_n[g - 4])
                    need(e, evac_dve, dve_n[g - 4])
                bk = bank[g % 4]
                if kind == "cols":
                    last = e.transpose(bk[:, 0, 0:len(ROWS)], rows[:, :], m["ident"][0:len(ROWS), 0:len(ROWS)])
                elif kind == "gate":
                    last = e.transpose(bk[:, 0, 0:NE], gate_raw[:, :], m["ident"][0:NE, 0:NE])
                elif kind == "ebias":
                    last = e.matmul(bk[:, 0, 0:NE], m["ones"][0:1, :], eb_row[:, :], start=True, stop=True)
                else:
                    raw = {"sq": sq_raw, "up": up_raw, "dn": dn_raw}[kind]
                    for k in range(n):
                        last = e.transpose(bk[:, k, :], raw[:, a + k, :], m["ident"][:, :])
                last.then_inc(turned, 1)

        @block.vector
        def _(e):
            for name in ("wc_pad", "wdelta_pad", "wb_pad"):
                e.memset(m[name][:, :, :], 0.0).then_inc(zero_done, 1)
            e.memset(m["onesb"][:, :], 1.0)
            e.wait_ge(ident_done, 1)
            e.tensor_copy(m["identb"][:, :], m["ident"][:, :])
            e.tensor_copy(m["identr"][:, :], m["ident"][:, :])
            e.wait_ge(masks, 8)
            e.tensor_copy(m["sel"][:, :, :].rearrange("p j c -> p (j c)"), wide[:, :])
            for g, (kind, a, n) in enumerate(order):
                e.wait_ge(turned, g + 1)
                bk = bank[g % 4]
                if kind == "cols":
                    e.tensor_copy(m["cols"][:, :], bk[:, 0, 0:len(ROWS)]).then_inc(evac_dve, 1)
                elif kind == "gate":
                    e.tensor_copy(m["gateT"][:, :], bk[:, 0, 0:NE]).then_inc(evac_dve, 1)
                elif kind == "ebias":
                    e.tensor_copy(m["ebias"][:, :], bk[:, 0, 0:NE]).then_inc(evac_dve, 1)
                elif kind == "sq":
                    e.tensor_copy(m["sqT"][:, a:a + n, :], bk[:, 0:n, :]).then_inc(evac_dve, 1)
                else:
                    e.wait_ge(evac_act, act_n[g])
                    e.tensor_tensor(m[kind + "_lo"][:, a:a + n, :], bk[:, 0:n, :],
                                    m[kind + "_hi"][:, a:a + n, :].bitcast(F32), ALU.subtract).then_inc(evac_dve, 1)
            e.wait_ge(small_in, 16 * (len(SQ) + 14))
            e.tensor_tensor(m["wdI"][:, :], m["wdI"][:, :], m["ident"][:, :], ALU.add).then_inc(evac_dve, 1)
            c = m["cols"]
            e.tensor_tensor(m["aux"][:, 0:1], c[:, COL["bc"]:COL["bc"] + 1], c[:, COL["bd"]:COL["bd"] + 1],
                            ALU.add).then_inc(evac_dve, 1)


def scan_block(nc, t, m):
    with ExitStack() as ctx:
        sb = lambda n, s, d=F32: ctx.enter_context(nc.sbuf_tensor(n, s, d))
        sem = lambda n: ctx.enter_context(nc.semaphore(n))
        ps = lambda n: ctx.enter_context(nc.psum_tensor(n, [P, 512], F32))
        NI = 4
        GT = 4 * T
        xin = [sb(f"x_in{k}", [P, GT // P, D]) for k in range(2)]
        PT = [ps(f"xT{k}") for k in range(4)]
        PD, PB = ps("delta_pre"), ps("b_pre")
        absd, expd, lnd, pos, delta = (sb(n, [P, 512]) for n in ("absd", "expd", "lnd", "posd", "delta"))
        alog, cum = sb("a_bar_log", [P, 512]), sb("cum", [P, 512])
        clip = sb("cum_clipped", [P, 2, T + 1])
        en, ep, bbar, bsh, bcum = (sb(n, [P, 512]) for n in ("exp_neg", "exp_pos", "b_bar", "b_shift", "b_cum"))
        ones = sb("ones_scan", [P, T])
        acol = sb("a_columns", [P, 4])
        x_in = [sem("x_in_0"), sem("x_in_1")]
        xt, xe_act, xe_dve, db = sem("x_turned"), sem("x_evac_act"), sem("x_evac_dve"), sem("delta_b_ready")
        s_abs, s_exp, s_ln, s_pos, s_delta = sem("abs_done"), sem("exp_done"), sem("ln_done"), sem("pos_done"), sem("delta_done")
        s_alog, s_cum, s_clip, s_en, s_ep = sem("alog_done"), sem("cum_done"), sem("clip_done"), sem("exp_neg_done"), sem("exp_pos_done")
        s_bbar, s_bsh, s_bcum, s_h, setup = sem("bbar_done"), sem("bshift_done"), sem("bcum_done"), sem("h_done"), sem("scan_setup")
        s_a = sem("a_softplus")
        xf = t["x"].rearrange("b t c -> (b t) c")
        A, hT, cols = m["act"], m["hT"], m["cols"]
        ca = lambda n: cols[:, COL[n]:COL[n] + 1]
        block = ctx.enter_context(nc.Block())

        def over(eng, fn):
            fn(0)
            with eng.Fori(1, NI) as i:
                fn(i)

        @block.sync
        def _(e):
            def load(i):
                for k in range(2):
                    need(e, xt, 4 * (i - 1) + 2 * k + 2)
                    src = xf[bass.ds((2 * i + k) * GT, GT), :].rearrange("(a p) c -> p a c", p=P)
                    e.dma_start(xin[k][:, :, :], src).then_inc(x_in[k], 16)
            over(e, load)

        @block.tensor
        def _(e):
            def work(i):
                for k in range(4):
                    if k % 2 == 0:
                        e.wait_ge(x_in[k // 2], 16 * (i + 1))
                    need(e, xe_act if k < 2 else xe_dve, 2 * (i - 1) + k % 2 + 1)
                    for a in range(4):
                        last = e.transpose(PT[k][:, a * P:(a + 1) * P], xin[k // 2][:, 4 * (k % 2) + a, :],
                                           m["ident"][:, :])
                    last.then_inc(xt, 1)
                e.wait_ge(xe_act, 2 * (i + 1))
                e.wait_ge(xe_dve, 2 * (i + 1))
                need(e, s_pos, i)
                need(e, s_abs, i)
                need(e, s_bbar, i)
                for dst, w in ((PD, m["wdelta_pad"]), (PB, m["wb_pad"])):
                    for g in range(2):
                        for k in range(4):
                            last = e.matmul(dst[:, g * T:(g + 1) * T], w[:, k, :],
                                            A[:, bass.ds((2 * i + g) * GT + k * T, T)],
                                            start=(k == 0), stop=(k == 3))
                    last.then_inc(db, 1)
            over(e, work)

        @block.scalar
        def _(e):
            e.activation(acol[:, 0:1], ca("A"), ACT.Abs).then_inc(s_a, 1)
            e.wait_ge(s_a, 1)
            e.activation(acol[:, 1:2], acol[:, 0:1], ACT.Exp, scale=-1.0).then_inc(s_a, 1)
            e.wait_ge(s_a, 2)
            e.activation(acol[:, 2:3], acol[:, 1:2], ACT.Ln, bias=1.0).then_inc(s_a, 1)

            def work(i):
                for k in range(2):
                    e.wait_ge(xt, 4 * i + k + 1)
                    e.activation(A[:, bass.ds(2 * i * GT + k * 512, 512)], PT[k][:, :], ACT.Copy).then_inc(xe_act, 1)
                e.wait_ge(db, 2 * i + 1)
                e.activation(absd[:, :], PD[:, :], ACT.Abs, bias=ca("bdelta")).then_inc(s_abs, 1)
                e.wait_ge(s_abs, i + 1)
                e.activation(expd[:, :], absd[:, :], ACT.Exp, scale=-1.0).then_inc(s_exp, 1)
                e.wait_ge(s_exp, i + 1)
                need(e, s_delta, i)
                e.activation(lnd[:, :], expd[:, :], ACT.Ln, bias=1.0).then_inc(s_ln, 1)
                e.wait_ge(s_clip, i + 1)
                need(e, s_bsh, i)
                e.activation(en[:, :].rearrange("p (g t) -> p g t", g=2), clip[:, :, 0:T], ACT.Exp, scale=-1.0).then_inc(s_en, 1)
                need(e, s_h, i)
                e.activation(ep[:, :].rearrange("p (g t) -> p g t", g=2), clip[:, :, 1:T + 1], ACT.Exp).then_inc(s_ep, 1)
            over(e, work)

        @block.vector
        def _(e):
            e.memset(ones[:, :], 1.0).then_inc(setup, 1)
            e.memset(clip[:, :, 0:1], 0.0).then_inc(setup, 1)
            e.wait_ge(s_a, 3)
            e.tensor_scalar(acol[:, 3:4], ca("A"), 0.0, None, ALU.max).then_inc(setup, 1)
            e.wait_ge(setup, 3)
            e.tensor_tensor(acol[:, 3:4], acol[:, 3:4], acol[:, 2:3], ALU.add).then_inc(setup, 1)
            e.wait_ge(setup, 4)
            e.tensor_scalar(acol[:, 3:4], acol[:, 3:4], -1.0, None, ALU.mult).then_inc(setup, 1)
            e.wait_ge(setup, 5)

            def work(i):
                for k in range(2):
                    e.wait_ge(xt, 4 * i + k + 3)
                    e.tensor_copy(A[:, bass.ds(2 * i * GT + (k + 2) * 512, 512)], PT[2 + k][:, :]).then_inc(xe_dve, 1)
                e.wait_ge(s_abs, i + 1)
                e.tensor_scalar(pos[:, :], PD[:, :], ca("bdelta"), 0.0, ALU.add, ALU.max).then_inc(s_pos, 1)
                e.wait_ge(s_pos, i + 1)
                e.wait_ge(s_ln, i + 1)
                e.tensor_tensor(delta[:, :], pos[:, :], lnd[:, :], ALU.add).then_inc(s_delta, 1)
                e.wait_ge(s_delta, i + 1)
                e.tensor_scalar(alog[:, :], delta[:, :], acol[:, 3:4], None, ALU.mult).then_inc(s_alog, 1)
                e.wait_ge(s_alog, i + 1)
                for g in range(2):
                    e.tensor_tensor_scan(cum[:, g * T:(g + 1) * T], ones[:, :], alog[:, g * T:(g + 1) * T], 0.0,
                                         ALU.mult, ALU.add).then_inc(s_cum, 1)
                e.wait_ge(s_cum, 2 * i + 2)
                need(e, s_en, i)
                need(e, s_ep, i)
                e.tensor_scalar(clip[:, :, 1:T + 1], cum[:, :].rearrange("p (g t) -> p g t", g=2), -20.0, 20.0,
                                ALU.max, ALU.min).then_inc(s_clip, 1)
                e.wait_ge(db, 2 * i + 2)
                need(e, s_bsh, i)
                e.scalar_tensor_tensor(out=bbar[:, :], in0=PB[:, :], scalar=ca("bb"), in1=delta[:, :],
                                       op0=ALU.add, op1=ALU.mult).then_inc(s_bbar, 1)
                e.wait_ge(s_bsh, i + 1)
                need(e, s_h, i)
                for g in range(2):
                    e.tensor_tensor_scan(bcum[:, g * T:(g + 1) * T], ones[:, :], bsh[:, g * T:(g + 1) * T], 0.0,
                                         ALU.mult, ALU.add).then_inc(s_bcum, 1)
            over(e, work)

        @block.gpsimd
        def _(e):
            def work(i):
                e.wait_ge(s_bbar, i + 1)
                e.wait_ge(s_en, i + 1)
                need(e, s_bcum, 2 * i)
                e.tensor_tensor(bsh[:, :], bbar[:, :], en[:, :], ALU.mult).then_inc(s_bsh, 1)
                e.wait_ge(s_bcum, 2 * i + 2)
                e.wait_ge(s_ep, i + 1)
                e.tensor_tensor(hT[:, bass.ds(i * 512, 512)], bcum[:, :], ep[:, :], ALU.mult).then_inc(s_h, 1)
            over(e, work)


class Norm:

    def __init__(self, ctx, nc, name):
        sb = lambda n, s: ctx.enter_context(nc.sbuf_tensor(f"{name}_{n}", s, F32))
        sem = lambda n: ctx.enter_context(nc.semaphore(f"{name}_{n}"))
        self.parts = [sb(f"parts{k}", [P, TT, 6]) for k in range(2)]
        self.mv = [sb(f"mv{k}", [P, TT, 2]) for k in range(2)]
        self.ve = [sb(f"ve{k}", [P, TT]) for k in range(2)]
        self.rstd = [sb(f"rstd{k}", [P, TT]) for k in range(2)]
        self.power, self.eps = sb("power", [P, TT]), sb("eps", [P, TT])
        self.stats_done, self.mv_done = sem("stats_done"), sem("mv_done")
        self.ve_done, self.rstd_done, self.normed = sem("ve_done"), sem("rstd_done"), sem("normed")
        self.power_set, self.gate = sem("power_set"), sem("gate")

    def setup(self, pool):
        pool.memset(self.power[:, :], -0.5).then_inc(self.power_set, 1)
        pool.memset(self.eps[:, :], EPS).then_inc(self.power_set, 1)
        pool.wait_ge(self.power_set, 2)

    def stats(self, dve, c, par, src):
        for k in range(TT):
            dve.bn_stats(self.parts[par][:, k, :], src[:, k, :]).then_inc(self.stats_done, 1)
        dve.wait_ge(self.stats_done, TT * (c + 1))
        need(dve, self.normed, TT * c)
        dve.sem_inc(self.gate, 1)
        for k in range(TT):
            dve.bn_aggr(self.mv[par][:, k, :], self.parts[par][:, k, :]).then_inc(self.mv_done, 1)

    def root(self, pool, c, par):
        pool.wait_ge(self.mv_done, TT * (c + 1))
        pool.tensor_tensor(self.ve[par][:, :], self.mv[par][:, :, 1], self.eps[:, :], ALU.add).then_inc(self.ve_done, 1)
        pool.wait_ge(self.ve_done, c + 1)
        need(pool, self.normed, TT * c)
        pool.tensor_tensor(self.rstd[par][:, :], self.ve[par][:, :], self.power[:, :], ALU.pow).then_inc(self.rstd_done, 1)

    def apply(self, dve, c, par, dst, src):
        dve.wait_ge(self.mv_done, TT * (c + 1))
        dve.wait_ge(self.rstd_done, c + 1)
        for k in range(TT):
            dve.tensor_scalar(dst[:, k, 0:D], src[:, k, :], self.mv[par][:, k, 0:1], self.rstd[par][:, k:k + 1],
                              ALU.subtract, ALU.mult).then_inc(self.normed, 1)


def first_block(nc, t, m):
    with ExitStack() as ctx:
        sb = lambda n, s, d=F32: ctx.enter_context(nc.sbuf_tensor(n, s, d))
        sem = lambda n: ctx.enter_context(nc.semaphore(n))
        ps = lambda n: ctx.enter_context(nc.psum_tensor(n, [P, CH], F32))
        two = lambda n, s=(P, CH): [sb(f"{n}{k}", list(s)) for k in range(2)]
        YT, YK, X1, RP, KP, ZK, X2, GP = (ps(n) for n in ("y_ch", "y_tok", "x1_ch", "r_pre", "k_pre", "z_tok", "x2_ch", "gram_sum"))
        VP = YT
        yT, x1k = two("y_sb"), two("x1_tok", (P, TT, D))
        x1T = two("x1T", (P, BC, T + 1))
        diff, xr, xk, rr, kr, k2, vr, zT = (two(n) for n in ("diff", "xr", "xk", "r", "k_relu", "k_sq", "v_r", "zT"))
        x2k = two("x2_stage", (P, TT, D + 1))
        n1, n2 = Norm(ctx, nc, "norm1"), Norm(ctx, nc, "norm2")
        zrow = sb("zero_row", [1, P + 1])
        A, hT, aux, cols = m["act"], m["hT"], m["aux"], m["cols"]
        cc = lambda n: cols[:, COL[n]:COL[n] + 1]
        bv = lambda ap: ap.rearrange("p (b t) -> p b t", b=BC)
        tv = lambda ap: ap.rearrange("p (k c) -> p k c", k=TT)

        y_mm, y_sb, y_tok, x1_turned, x1_copied = sem("y_mm"), sem("y_sb_done"), sem("y_turned"), sem("x1_turned"), sem("x1_copied")
        s_diff, s_xr, s_xk, r_mm, k_mm = sem("diff_done"), sem("xr_done"), sem("xk_done"), sem("r_mm"), sem("k_mm")
        s_r, s_kr, s_k2, v_mm, s_vr, s_z = sem("r_done"), sem("krelu_done"), sem("ksq_done"), sem("v_mm"), sem("vr_done"), sem("z_done")
        z_turned, x2_turned, x2_copied, gram_mm, stored = sem("z_turned"), sem("x2_turned"), sem("x2_copied"), sem("gram_mm"), [sem("x2_stored0"), sem("x2_stored1")]
        setup, gram_out, zeroed = sem("first_setup"), sem("gram_out"), sem("gram_zeroed")
        block = ctx.enter_context(nc.Block())

        D1, D2, D3, D4 = 0, 1, 2, 3

        @block.tensor
        def _(e):
            e.wait_ge(setup, 6)
            e.matmul(GP[:, 0:P + 1], m["ones"][0:1, :], zrow[0:1, :], start=True, stop=False).then_inc(zeroed, 1)

            def attn(c, p):
                need(e, y_sb, c)
                need(e, s_vr, c - 1)
                e.matmul(YT[:, :], m["wdI"][:, :], A[:, bass.ds(c * CH, CH)], start=True, stop=False)
                for b in range(BC):
                    last = e.matmul(YT[:, b * T:(b + 1) * T], m["wc_pad"][:, BC * p + b, :],
                                    hT[:, bass.ds((c - p) * (T // 2), T)], start=False, stop=(b == BC - 1))
                last.then_inc(y_mm, 1)
                e.wait_ge(y_sb, c + 1)
                need(e, n1.normed, TT * c)
                for k in range(TT):
                    last = e.transpose(YK[:, k * P:(k + 1) * P], yT[p][:, k * P:(k + 1) * P], m["ident"][:, :])
                last.then_inc(y_tok, 1)

            def mix(c, p):
                e.wait_ge(n1.normed, TT * (c + 1))
                need(e, x1_copied, c)
                for k in range(TT):
                    last = e.transpose(X1[:, k * P:(k + 1) * P], x1k[p][:, k, :], m["ident"][:, :])
                last.then_inc(x1_turned, 1)
                e.wait_ge(s_xk, c + 1)
                need(e, s_kr, c)
                need(e, s_k2, c)
                e.matmul(KP[:, :], m["sqT"][:, SQ.index("W_k"), :], xk[p][:, :], start=True, stop=True).then_inc(k_mm, 1)
                e.wait_ge(s_xr, c + 1)
                need(e, s_r, c)
                e.matmul(RP[:, :], m["sqT"][:, SQ.index("W_r"), :], xr[p][:, :], start=True, stop=True).then_inc(r_mm, 1)

            def value(c, p):
                e.wait_ge(s_k2, c + 1)
                need(e, y_sb, c + 2 if not isinstance(c, int) else min(c + 2, NCH))
                e.matmul(VP[:, :], m["sqT"][:, SQ.index("W_v"), :], k2[p][:, :], start=True, stop=True).then_inc(v_mm, 1)
                e.wait_ge(s_z, c + 1)
                need(e, n2.normed, TT * c)
                for k in range(TT):
                    last = e.transpose(ZK[:, k * P:(k + 1) * P], zT[p][:, k * P:(k + 1) * P], m["ident"][:, :])
                last.then_inc(z_turned, 1)

            def emit(c, p):
                e.wait_ge(n2.normed, TT * (c + 1))
                need(e, x2_copied, c)
                for k in range(TT):
                    last = e.transpose(X2[:, k * P:(k + 1) * P], x2k[p][:, k, 0:D], m["ident"][:, :])
                last.then_inc(x2_turned, 1)
                for k in range(TT):
                    last = e.matmul(GP[:, 0:D + 1], x2k[p][:, k, 0:D], x2k[p][:, k, :], start=False,
                                    stop=False, skip_group_check=True)
                last.then_inc(gram_mm, 1)

            pipeline(e, [(D4, emit), (D3, value), (D2, mix), (D1, attn)], NCH, 3)
            e.matmul(GP[:, 0:P + 1], m["ones"][0:1, :], zrow[0:1, :], start=False, stop=True).then_inc(zeroed, 1)

        @block.scalar
        def _(e):
            def attn(c, p):
                e.wait_ge(y_mm, c + 1)
                need(e, y_tok, c - 1)
                e.activation(yT[p][:, :], YT[:, :], ACT.Identity, bias=aux[:, 0:1]).then_inc(y_sb, 1)

            def mix(c, p):
                e.wait_ge(x1_turned, c + 1)
                need(e, s_z, c - 1)
                need(e, s_xr, c - 1)
                need(e, s_xk, c - 1)
                e.activation(x1T[p][:, :, 1:T + 1], bv(X1[:, :]), ACT.Copy).then_inc(x1_copied, 1)
                e.wait_ge(k_mm, c + 1)
                need(e, s_k2, c - 1)
                e.activation(kr[p][:, :], KP[:, :], ACT.Relu).then_inc(s_kr, 1)
                e.wait_ge(r_mm, c + 1)
                need(e, s_vr, c - 1)
                e.activation(rr[p][:, :], RP[:, :], ACT.Sigmoid).then_inc(s_r, 1)

            def emit(c, p):
                e.wait_ge(x2_turned, c + 1)
                e.activation(A[:, bass.ds(c * CH, CH)], X2[:, :], ACT.Copy).then_inc(x2_copied, 1)

            pipeline(e, [(D4, emit), (D2, mix), (D1, attn)], NCH, 3)

        @block.vector
        def _(e):
            e.memset(zrow[:, :], 0.0).then_inc(setup, 1)
            for k in range(2):
                e.memset(x1T[k][:, :, 0:1], 0.0).then_inc(setup, 1)
                e.memset(x2k[k][:, :, D:D + 1], 1.0).then_inc(setup, 1)
            e.memset(aux[:, 1:2], 0.0).then_inc(setup, 1)

            def attn(c, p):
                e.wait_ge(y_tok, c + 1)
                n1.stats(e, c, p, tv(YK[:, :]))
                need(e, x1_turned, c - 1)
                n1.apply(e, c, p, x1k[p], tv(YK[:, :]))

            def mix(c, p):
                e.wait_ge(s_diff, c + 1)
                for mu, dst, done, used in (("mu_k", xk, s_xk, k_mm), ("mu_r", xr, s_xr, r_mm)):
                    need(e, used, c - 1)
                    e.scalar_tensor_tensor(out=bv(dst[p][:, :]), in0=bv(diff[p][:, :]), scalar=cc(mu),
                                           in1=x1T[p][:, :, 0:T], op0=ALU.mult, op1=ALU.add).then_inc(done, 1)
                e.wait_ge(s_kr, c + 1)
                need(e, v_mm, c - 1)
                e.scalar_tensor_tensor(out=k2[p][:, :], in0=KP[:, :], scalar=0.0, in1=kr[p][:, :],
                                       op0=ALU.max, op1=ALU.mult).then_inc(s_k2, 1)

            def value(c, p):
                e.wait_ge(v_mm, c + 1)
                e.wait_ge(s_r, c + 1)
                need(e, s_z, c - 1)
                e.tensor_tensor(vr[p][:, :], VP[:, :], rr[p][:, :], ALU.mult).then_inc(s_vr, 1)
                e.wait_ge(z_turned, c + 1)
                n2.stats(e, c, p, tv(ZK[:, :]))
                need(e, x2_turned, c - 1)
                need(e, gram_mm, c - 1)
                need(e, stored[p], 8 * (c - p))
                n2.apply(e, c, p, x2k[p], tv(ZK[:, :]))

            pipeline(e, [(D3, value), (D2, mix), (D1, attn)], NCH, 3)
            e.wait_ge(zeroed, 2)
            e.tensor_scalar(m["gram"][:, :], GP[:, 0:P + 1], 1.0 / NTOK, None, ALU.mult).then_inc(gram_out, 1)

        @block.gpsimd
        def _(e):
            n1.setup(e)
            n2.setup(e)
            e.wait_ge(setup, 6)

            def attn(c, p):
                n1.root(e, c, p)

            def mix(c, p):
                e.wait_ge(x1_copied, c + 1)
                need(e, s_xr, c - 1)
                need(e, s_xk, c - 1)
                e.tensor_tensor(bv(diff[p][:, :]), x1T[p][:, :, 1:T + 1], x1T[p][:, :, 0:T], ALU.subtract).then_inc(s_diff, 1)

            def value(c, p):
                e.wait_ge(s_vr, c + 1)
                need(e, z_turned, c - 1)
                e.tensor_tensor(bv(zT[p][:, :]), bv(vr[p][:, :]), x1T[p][:, :, 1:T + 1], ALU.add).then_inc(s_z, 1)
                n2.root(e, c, p)

            pipeline(e, [(D3, value), (D2, mix), (D1, attn)], NCH, 3)

        @block.sync
        def _(e):
            def emit(c, p):
                e.wait_ge(n2.normed, TT * (c + 1))
                e.dma_start(m["tok"][:, bass.ds(c * TT, TT), :], x2k[p][:, :, 0:D]).then_inc(stored[p], 16)

            pipeline(e, [(D4, emit)], NCH, 3)
            for s in stored:
                e.wait_ge(s, 8 * NCH)


def fold_block(nc, t, m):
    with ExitStack() as ctx:
        sb = lambda n, s, d=F32: ctx.enter_context(nc.sbuf_tensor(n, s, d))
        sem = lambda n: ctx.enter_context(nc.semaphore(n))
        ps = lambda n, d=F32: ctx.enter_context(nc.psum_tensor(n, [P, 512], d))
        GW, ST, TR, TB = ps("gram_w"), ps("bn_sums"), ps("v_turned"), ps("rows_turned", BF16)
        prod = sb("w_gram_w", [P, 3, P])
        st = sb("bn_columns", [P, 8, 3])
        half = sb("half_power", [P, 3])
        parts = sb("row_parts", [P, 2, 3], BF16)
        rest = sb("row_rest", [P, 2, 2])
        mm, dv, pw, pl = sem("fold_mm"), sem("fold_dve"), sem("fold_power"), sem("fold_pool")
        block = ctx.enter_context(nc.Block())
        WT = m["sqT"][:, SQ.index("Wq"):SQ.index("Wq") + 3, :]
        aux, cols = m["aux"], m["cols"]
        gam = cols[:, COL["gq"]:COL["gq"] + 6].rearrange("p (b k) -> p k b", k=2)

        @block.tensor
        def _(e):
            e.matmul(GW[:, 0:3 * P], m["gram"][:, 0:P], WT, start=True, stop=True).then_inc(mm, 1)
            e.wait_ge(dv, 1)
            for b in range(3):
                e.matmul(ST[:, b:b + 1], WT[:, b, :], m["gram"][:, P:P + 1], start=(b == 0), stop=True,
                         skip_group_check=True)
            for b in range(3):
                last = e.matmul(ST[:, 4 + b:5 + b], prod[:, b, :], m["ones"][:, 0:1], start=False, stop=True,
                                skip_group_check=True)
            last.then_inc(mm, 1)
            e.wait_ge(dv, 7)
            e.transpose(TR[:, 0:P], m["wv_nat"][:, :], m["ident"][:, :]).then_inc(mm, 1)
            e.wait_ge(dv, 12)
            e.transpose(TB[0:3, 0:P], parts[:, 0, :], m["identb"][:, :])
            e.transpose(TB[0:3, P:2 * P], parts[:, 1, :], m["identb"][:, :]).then_inc(mm, 1)

        @block.gpsimd
        def _(e):
            e.memset(half[:, :], -0.5).then_inc(pl, 1)
            e.wait_ge(pl, 1)
            e.wait_ge(dv, 4)
            e.tensor_tensor(st[:, 5, :], st[:, 4, :], half[:, :], ALU.pow).then_inc(pw, 1)

        @block.vector
        def _(e):
            n = [0]

            def done(ins):
                ins.then_inc(dv, 1)
                n[0] += 1
                e.wait_ge(dv, n[0])

            e.wait_ge(mm, 1)
            done(e.tensor_tensor(prod[:, :, :], GW[:, 0:3 * P].rearrange("p (b c) -> p b c", b=3), WT, ALU.mult))
            e.wait_ge(mm, 2)
            e.tensor_copy(st[:, 1, :], ST[:, 4:7])
            done(e.tensor_copy(st[:, 0, :], ST[:, 0:3]))
            done(e.tensor_tensor(st[:, 2, :], st[:, 0, :], st[:, 0, :], ALU.mult))
            e.scalar_tensor_tensor(out=st[:, 3, :], in0=st[:, 2, :], scalar=-1.0, in1=ST[:, 4:7],
                                   op0=ALU.mult, op1=ALU.add).then_inc(pl, 1)
            e.wait_ge(pl, 2)
            done(e.tensor_scalar(st[:, 4, :], st[:, 3, :], 0.0, EPS, ALU.max, ALU.add))
            e.wait_ge(pw, 1)
            done(e.scalar_tensor_tensor(out=st[:, 6, :], in0=st[:, 5, :], scalar=4.0, in1=gam[:, 0, :],
                                        op0=ALU.mult, op1=ALU.mult))
            done(e.tensor_tensor(st[:, 7, :], st[:, 0, :], st[:, 6, :], ALU.mult))
            e.tensor_copy(aux[:, 2:5], st[:, 6, :])
            done(e.tensor_scalar(m["wv_nat"][:, :], m["wv_nat"][:, :], st[:, 6, 2:3], None, ALU.mult))
            done(e.tensor_scalar(aux[:, 5:8], gam[:, 1, :], -V_TH, 4.0, ALU.add, ALU.mult))
            done(e.tensor_tensor(aux[:, 5:8], aux[:, 5:8], st[:, 7, :], ALU.subtract))
            src = m["brow"]
            e.tensor_copy(src[:, 0:1], aux[:, 7:8])
            done(e.tensor_copy(src[:, 1:2], cols[:, COL["bp"]:COL["bp"] + 1]))
            e.tensor_copy(parts[:, :, 0], src[:, :]).then_inc(pl, 1)
            e.wait_ge(pl, 3)
            e.tensor_tensor(rest[:, :, 0], src[:, :], parts[:, :, 0], ALU.subtract).then_inc(pl, 1)
            e.wait_ge(pl, 4)
            done(e.tensor_copy(parts[:, :, 1], rest[:, :, 0]))
            e.tensor_tensor(rest[:, :, 1], rest[:, :, 0], parts[:, :, 1], ALU.subtract).then_inc(pl, 1)
            e.wait_ge(pl, 5)
            done(e.tensor_copy(parts[:, :, 2], rest[:, :, 1]))
            e.wait_ge(mm, 3)
            done(e.tensor_copy(m["wvT"][:, :], TR[:, 0:P]))
            e.wait_ge(mm, 4)
            for k in range(TT):
                done(e.tensor_copy(m["vb3"][:, k, :], TB[0:3, 0:P]))
                done(e.tensor_copy(m["bp3"][:, k, :], TB[0:3, P:2 * P]))


def second_block(nc, t, m):
    with ExitStack() as ctx:
        sb = lambda n, s, d=F32: ctx.enter_context(nc.sbuf_tensor(n, s, d))
        sem = lambda n: ctx.enter_context(nc.semaphore(n))
        ps = lambda n, d=F32, w=CH: ctx.enter_context(nc.psum_tensor(n, [P, w], d))
        two = lambda n, s=(P, CH), d=F32: [sb(f"{n}{k}", list(s), d) for k in range(2)]
        QP, KP, VP, GM, MP, OP, X3, LG = (ps(n) for n in ("q_pre", "k2_pre", "v_pre", "vv_sum", "m_pre", "o_tok", "x3_ch", "logits"))
        CT = GM[:, :].bitcast(BF16)
        x2s, q, k_, qk = two("x2_static"), two("q"), two("k"), two("qk")
        v = two("v_tok", (P, TT, D))
        vvm, mp = two("vv_masked", (P, BC, P)), two("m_mix", (P, BC, P))
        z, x3k, x3s = two("z_attn", (P, TT, D)), two("x3_tok", (P, TT, D)), two("x3_static")
        S = two("scores", (P, TT, NE))
        sc = sb("biased", [P, TT, NE])
        hi2, lo2 = sb("pair_max", [P, TT * NE // 2]), sb("pair_min", [P, TT * NE // 2])
        g1, g2, g3 = (sb(n, [P, TT * NG]) for n in ("top1", "pair_max_min", "low_max"))
        gpad, grep = sb("group_padded", [P, TT, NG + TOPG]), sb("group_replaced", [P, TT, NG + TOPG])
        gm8 = sb("group_top", [P, TT, 8])
        gmask = sb("group_mask", [P, TT, NG])
        epad, erep = sb("expert_padded", [P, TT, NE + 2]), sb("expert_replaced", [P, TT, NE + 2])
        em8 = sb("expert_top", [P, TT, 8])
        w, wsum, wrec = sb("chosen", [P, TT, NE]), sb("chosen_sum", [P, TT]), sb("chosen_rec", [P, TT])
        cf, c1, c2 = sb("combine", [P, TT, NE]), sb("combine_rest1", [P, TT, NE]), sb("combine_rest2", [P, TT, NE])
        cs = two("combine_parts", (P, TT, 3 * NE), BF16)
        n3 = Norm(ctx, nc, "norm3")
        A, aux = m["act"], m["aux"]
        tv = lambda ap: ap.rearrange("p (k c) -> p k c", k=TT)

        x2_in = [sem("x2_in0"), sem("x2_in1")]
        q_mm, k_mm, v_mm, s_q, s_k, s_v, s_qk = (sem(n) for n in ("q_mm", "k2_mm", "v2_mm", "q_done", "k_done", "v_done", "qk_done"))
        vv_mm, s_vvm, m_mm, s_mp, o_mm, s_zz = (sem(n) for n in ("vv_mm", "vvm_done", "m_mm", "mp_done", "o_mm", "zz_done"))
        x3_turned, x3_static, x3_act, lg_mm, s_S = (sem(n) for n in ("x3_turned", "x3_static_done", "x3_act_done", "logits_mm", "scores_done"))
        gate, rt, s_cs, c_turned, c_out, setup = (sem(n) for n in ("router_gate", "router_step", "combine_done", "combine_turned", "combine_out", "second_setup"))
        block = ctx.enter_context(nc.Block())
        E1, E2, E3, E4, E5 = 0, 1, 2, 3, 4

        @block.sync
        def _(e):
            def load(c, p):
                need(e, k_mm, c - 1)
                need(e, v_mm, c - 1)
                e.dma_start(x2s[p][:, :], A[:, bass.ds(c * CH, CH)]).then_inc(x2_in[p], 16)
            pipeline(e, [(0, load)], NCH, 2)

        @block.tensor
        def _(e):
            def proj(c, p):
                e.wait_ge(x2_in[p], 8 * (c - p) + 16)
                need(e, s_q, c)
                e.matmul(QP[:, :], m["sqT"][:, SQ.index("Wq"), :], x2s[p][:, :], start=True, stop=True).then_inc(q_mm, 1)
                need(e, s_k, c)
                e.matmul(KP[:, :], m["sqT"][:, SQ.index("Wk"), :], x2s[p][:, :], start=True, stop=True).then_inc(k_mm, 1)
                need(e, s_v, c)
                e.matmul(VP[:, :], m["onesb"][:, :], m["vb3"][:, :, :].rearrange("p k c -> p (k c)"), start=True, stop=False)
                for k in range(TT):
                    last = e.matmul(VP[:, k * P:(k + 1) * P], x2s[p][:, k * P:(k + 1) * P], m["wvT"][:, :],
                                    start=False, stop=(k == TT - 1))
                last.then_inc(v_mm, 1)

            def attend(c, p):
                e.wait_ge(s_v, c + 1)
                need(e, s_vvm, c)
                need(e, c_out, c - E5 + E2 + 1 if not isinstance(c, int) else min(c - E5 + E2 + 1, NCH))
                for b in range(BC):
                    for k in range(2):
                        last = e.matmul(GM[:, b * P:(b + 1) * P], v[p][:, 2 * b + k, :], v[p][:, 2 * b + k, :],
                                        start=(k == 0), stop=(k == 1))
                last.then_inc(vv_mm, 1)
                e.wait_ge(s_vvm, c + 1)
                need(e, s_mp, c)
                for b in range(BC):
                    last = e.matmul(MP[:, b * P:(b + 1) * P], vvm[p][:, b, :], m["sqT"][:, SQ.index("Wp"), :],
                                    start=True, stop=True)
                last.then_inc(m_mm, 1)
                e.wait_ge(s_mp, c + 1)
                e.wait_ge(s_qk, c + 1)
                need(e, s_zz, c)
                e.matmul(OP[:, :], m["onesb"][:, :], m["bp3"][:, :, :].rearrange("p k c -> p (k c)"), start=True, stop=False)
                for k in range(TT):
                    last = e.matmul(OP[:, k * P:(k + 1) * P], qk[p][:, k * P:(k + 1) * P], mp[p][:, k // 2, :],
                                    start=False, stop=(k == TT - 1))
                last.then_inc(o_mm, 1)

            def turn(c, p):
                e.wait_ge(n3.normed, TT * (c + 1))
                need(e, x3_static, c)
                need(e, x3_act, c)
                for k in range(TT):
                    last = e.transpose(X3[:, k * P:(k + 1) * P], x3k[p][:, k, :], m["ident"][:, :])
                last.then_inc(x3_turned, 1)
                e.wait_ge(x3_static, c + 1)
                need(e, s_S, c)
                for k in range(TT):
                    last = e.matmul(LG[:, k * NE:(k + 1) * NE], x3s[p][:, k * P:(k + 1) * P], m["gateT"][:, :],
                                    start=True, stop=True)
                last.then_inc(lg_mm, 1)

            def experts(c, p):
                e.wait_ge(s_cs, c + 1)
                need(e, c_out, c)
                need(e, s_vvm, c + E5 - E2 if not isinstance(c, int) else min(c + E5 - E2, NCH))
                for k in range(TT):
                    last = e.transpose(CT[0:3 * NE, k * P:(k + 1) * P], cs[p][:, k, :], m["identb"][:, :])
                last.then_inc(c_turned, 1)

            pipeline(e, [(E5, experts), (E3, turn), (E2, attend), (E1, proj)], NCH, 4)

        @block.scalar
        def _(e):
            def proj(c, p):
                e.wait_ge(q_mm, c + 1)
                need(e, s_qk, c - 1)
                e.activation(q[p][:, :], QP[:, :], ACT.Sigmoid, bias=aux[:, 5:6], scale=aux[:, 2:3]).then_inc(s_q, 1)
                e.wait_ge(k_mm, c + 1)
                e.activation(k_[p][:, :], KP[:, :], ACT.Sigmoid, bias=aux[:, 6:7], scale=aux[:, 3:4]).then_inc(s_k, 1)
                e.wait_ge(v_mm, c + 1)
                need(e, vv_mm, c - 1)
                e.activation(v[p][:, :, :], tv(VP[:, :]), ACT.Sigmoid).then_inc(s_v, 1)

            def attend(c, p):
                e.wait_ge(m_mm, c + 1)
                need(e, o_mm, c - 1)
                e.activation(mp[p][:, :, :], MP[:, 0:BC * P].rearrange("p (b c) -> p b c", b=BC), ACT.Copy).then_inc(s_mp, 1)

            def turn(c, p):
                e.wait_ge(x3_turned, c + 1)
                need(e, lg_mm, c - 1)
                e.activation(x3s[p][:, :], X3[:, :], ACT.Copy).then_inc(x3_static, 1)
                e.activation(A[:, bass.ds(c * CH, CH)], X3[:, :], ACT.Copy).then_inc(x3_act, 1)
                e.wait_ge(lg_mm, c + 1)
                need(e, s_cs, c - 1)
                e.activation(S[p][:, :, :], LG[:, 0:TT * NE].rearrange("p (k c) -> p k c", k=TT), ACT.Sigmoid).then_inc(s_S, 1)

            def experts(c, p):
                e.wait_ge(c_turned, c + 1)
                e.activation(m["cT"][:, bass.ds(c * CH, CH)], CT[0:3 * NE, 0:CH], ACT.Copy).then_inc(c_out, 1)

            pipeline(e, [(E5, experts), (E3, turn), (E2, attend), (E1, proj)], NCH, 4)

        @block.gpsimd
        def _(e):
            n3.setup(e)

            def proj(c, p):
                e.wait_ge(s_q, c + 1)
                e.wait_ge(s_k, c + 1)
                need(e, o_mm, c - 1)
                e.tensor_tensor(qk[p][:, :], q[p][:, :], k_[p][:, :], ALU.mult).then_inc(s_qk, 1)

            def attend(c, p):
                n3.root(e, c, p)

            pipeline(e, [(E2, attend), (E1, proj)], NCH, 4)

        @block.vector
        def _(e):
            e.memset(gpad[:, :, NG:], NEG).then_inc(setup, 1)
            e.memset(epad[:, :, NE:], NEG).then_inc(setup, 1)
            e.wait_ge(setup, 2)
            RT = 23

            def attend(c, p):
                e.wait_ge(vv_mm, c + 1)
                need(e, m_mm, c - 1)
                for b in range(BC):
                    last = e.scalar_tensor_tensor(out=vvm[p][:, b, :], in0=GM[:, b * P:(b + 1) * P],
                                                  scalar=float(HD) ** -0.5, in1=m["headmask"][:, :],
                                                  op0=ALU.mult, op1=ALU.mult)
                last.then_inc(s_vvm, 1)
                e.wait_ge(o_mm, c + 1)
                need(e, n3.normed, TT * (c - 1))
                e.tensor_tensor(z[p][:, :, :], tv(OP[:, :]), m["tok"][:, bass.ds(c * TT, TT), :], ALU.add).then_inc(s_zz, 1)
                e.wait_ge(s_zz, c + 1)
                n3.stats(e, c, p, z[p])
                need(e, x3_turned, c - 1)
                n3.apply(e, c, p, x3k[p], z[p])

            def router(c, p):
                n = [0]

                def chain(ins, fixed=False):
                    ins.then_inc(rt, 1)
                    n[0] += 1
                    e.wait_ge(rt, c * RT + n[0])
                    if fixed:
                        e.sem_inc(gate, 1)

                e.wait_ge(s_S, c + 1)
                chain(e.tensor_tensor(sc[:, :, :], S[p][:, :, :],
                                      m["ebias"][:, :].rearrange("p (a c) -> p a c", a=1).broadcast_to([P, TT, NE]), ALU.add))
                pair = sc[:, :, :].rearrange("p k (g two) -> p (k g) two", two=2)
                e.tensor_tensor(hi2[:, :], pair[:, :, 0], pair[:, :, 1], ALU.max)
                chain(e.tensor_tensor(lo2[:, :], pair[:, :, 0], pair[:, :, 1], ALU.min))
                ph = hi2[:, :].rearrange("p (g two) -> p g two", two=2)
                pl = lo2[:, :].rearrange("p (g two) -> p g two", two=2)
                e.tensor_tensor(g1[:, :], ph[:, :, 0], ph[:, :, 1], ALU.max)
                e.tensor_tensor(g2[:, :], ph[:, :, 0], ph[:, :, 1], ALU.min)
                chain(e.tensor_tensor(g3[:, :], pl[:, :, 0], pl[:, :, 1], ALU.max))
                chain(e.tensor_tensor(g2[:, :], g2[:, :], g3[:, :], ALU.max))
                chain(e.tensor_tensor(gpad[:, :, 0:NG], g1[:, :].rearrange("p (k g) -> p k g", k=TT),
                                      g2[:, :].rearrange("p (k g) -> p k g", k=TT), ALU.add), fixed=True)
                for k in range(TT):
                    last = e.max(gm8[:, k, :], gpad[:, k, 0:NG])
                chain(last)
                chain(e.memset(gm8[:, :, TOPG:8], NEG), fixed=True)
                for k in range(TT):
                    last = e.match_replace(grep[:, k, :], gm8[:, k, :], gpad[:, k, :], TAKEN)
                chain(last)
                chain(e.tensor_scalar(gmask[:, :, :], grep[:, :, 0:NG], TAKEN, None, ALU.is_equal))
                for k in range(TT):
                    last = e.tensor_tensor(epad[:, k, 0:NE].rearrange("p (g x) -> p g x", g=NG),
                                           sc[:, k, :].rearrange("p (g x) -> p g x", g=NG),
                                           gmask[:, k, :].rearrange("p (g x) -> p g x", x=1).broadcast_to([P, NG, GE]), ALU.mult)
                chain(last, fixed=True)
                for k in range(TT):
                    last = e.max(em8[:, k, :], epad[:, k, 0:NE])
                chain(last)
                chain(e.memset(em8[:, :, TOPK:8], NEG), fixed=True)
                for k in range(TT):
                    last = e.match_replace(erep[:, k, :], em8[:, k, :], epad[:, k, :], TAKEN)
                chain(last)
                chain(e.scalar_tensor_tensor(out=w[:, :, :], in0=erep[:, :, 0:NE], scalar=TAKEN, in1=S[p][:, :, :],
                                             op0=ALU.is_equal, op1=ALU.mult))
                chain(e.tensor_reduce(wsum[:, :], w[:, :, :], AX.X, ALU.add))
                chain(e.tensor_scalar(wsum[:, :], wsum[:, :], 1e-20, None, ALU.add))
                chain(e.reciprocal(wrec[:, :], wsum[:, :]))
                chain(e.tensor_scalar(wrec[:, :], wrec[:, :], ROUTED_SCALE, None, ALU.mult))
                chain(e.tensor_tensor(cf[:, :, :], w[:, :, :],
                                      wrec[:, :].rearrange("p (k x) -> p k x", x=1).broadcast_to([P, TT, NE]), ALU.mult))
                need(e, c_turned, c - 1)
                chain(e.tensor_copy(cs[p][:, :, 0:NE], cf[:, :, :]))
                chain(e.tensor_tensor(c1[:, :, :], cf[:, :, :], cs[p][:, :, 0:NE], ALU.subtract))
                chain(e.tensor_copy(cs[p][:, :, NE:2 * NE], c1[:, :, :]))
                chain(e.tensor_tensor(c2[:, :, :], c1[:, :, :], cs[p][:, :, NE:2 * NE], ALU.subtract))
                assert n[0] == RT
                e.tensor_copy(cs[p][:, :, 2 * NE:3 * NE], c2[:, :, :]).then_inc(s_cs, 1)

            pipeline(e, [(E4, router), (E2, attend)], NCH, 4)


def experts_block(nc, t, m, out):
    with ExitStack() as ctx:
        sb = lambda n, s, d=F32: ctx.enter_context(nc.sbuf_tensor(n, s, d))
        sem = lambda n: ctx.enter_context(nc.semaphore(n))
        ps = lambda n: ctx.enter_context(nc.psum_tensor(n, [P, CH], F32))
        U, C, O = [ps(f"up{k}") for k in range(3)], [ps(f"weight{k}") for k in range(2)], [ps(f"down{k}") for k in range(2)]
        TK = ps("out_tok")
        NR = 3
        r, tt, h = ([sb(f"{n}{k}", [P, CH]) for k in range(NR)] for n in ("relu", "relu_w", "hid"))
        hh, hl = ([sb(f"{n}{k}", [P, CH], F32R) for k in range(NR)] for n in ("hid_hi", "hid_lo"))
        xh, xl = ([sb(f"{n}{k}", [P, CH], F32R) for k in range(2)] for n in ("x3_hi", "x3_lo"))
        oT = [sb(f"outT{k}", [P, CH]) for k in range(2)]
        x4 = [sb(f"x4_tok{k}", [P, TT, D]) for k in range(2)]
        n4 = Norm(ctx, nc, "norm4")
        s_xh, s_xl, u_mm, c_mm, s_r, s_t, s_h, s_hh, s_hl, d_mm, o_mm, s_o, o_turned = (
            sem(n) for n in ("x_hi_done", "x_lo_done", "up_mm", "weight_mm", "relu_done", "relu_w_done", "hid_done",
                             "hid_hi_done", "hid_lo_done", "down_mm", "out_mm", "out_copied", "out_turned"))
        stored = [sem("x4_stored0"), sem("x4_stored1")]
        A = m["act"]
        tv = lambda ap: ap.rearrange("p (k c) -> p k c", k=TT)
        of = out.rearrange("b t c -> (b t) c")
        LAG, SLAG = 4, 2
        WL = 7
        block = ctx.enter_context(nc.Block())

        def chunks(eng, body, tail):
            body(0, 0)
            body(1, 1)
            with eng.Fori(1, NCH // 2 - 1) as i:
                body(2 * i, 0)
                body(2 * i + 1, 1)
            body(NCH - 2, 0)
            body(NCH - 1, 1)
            tail()

        @block.tensor
        def _(e):
            def up(c, p, j):
                g = c * NB + j
                if j == 0:
                    e.wait_ge(s_xl, c + 1)
                need(e, s_r, g - 2)
                uk = U[j % 3]
                e.matmul(uk[:, :], m["up_hi"][:, j, :], xh[p][:, :], start=True, stop=False)
                e.matmul(uk[:, :], m["up_hi"][:, j, :], xl[p][:, :], start=False, stop=False)
                e.matmul(uk[:, :], m["up_lo"][:, j, :], xh[p][:, :], start=False, stop=True).then_inc(u_mm, 1)
                if j < NRB:
                    need(e, s_t, c * NRB + j - 1)
                    e.matmul(C[j % 2][:, :], m["sel"][:, j, :], m["cT"][:, bass.ds(c * CH, CH)],
                             start=True, stop=True).then_inc(c_mm, 1)

            def down(c, p, j):
                g = c * NB + j
                if j == 0:
                    need(e, s_o, c - 1)
                    e.matmul(O[p][:, :], m["identr"][:, :], xh[p][:, :], start=True, stop=False)
                    e.matmul(O[p][:, :], m["identr"][:, :], xl[p][:, :], start=False, stop=False)
                e.wait_ge(s_hh, g + 1)
                e.matmul(O[p][:, :], m["dn_hi"][:, j, :], hh[j % NR][:, :], start=False, stop=False)
                e.matmul(O[p][:, :], m["dn_lo"][:, j, :], hh[j % NR][:, :], start=False, stop=False)
                e.wait_ge(s_hl, g + 1)
                last = e.matmul(O[p][:, :], m["dn_hi"][:, j, :], hl[j % NR][:, :], start=False, stop=(j == NB - 1))
                last.then_inc(d_mm, 1)

            def turn(c, p):
                e.wait_ge(s_o, c + 1)
                need(e, n4.normed, TT * c)
                for k in range(TT):
                    last = e.transpose(TK[:, k * P:(k + 1) * P], oT[p][:, k * P:(k + 1) * P], m["ident"][:, :])
                last.then_inc(o_turned, 1)

            def body(c, p):
                for j in range(NB):
                    up(c, p, j)
                    if j >= LAG:
                        down(c, p, j - LAG)
                    elif not (isinstance(c, int) and c == 0):
                        down(c - 1, 1 - p, NB - LAG + j)
                    if j == WL and not (isinstance(c, int) and c == 0):
                        turn(c - 1, 1 - p)

            def tail():
                for j in range(LAG):
                    down(NCH - 1, 1, NB - LAG + j)
                turn(NCH - 1, 1)
            chunks(e, body, tail)

        @block.scalar
        def _(e):
            def split(c, p):
                need(e, d_mm, NB * (c - 2 + 1))
                e.activation(xh[p][:, :], A[:, bass.ds(c * CH, CH)], ACT.Copy).then_inc(s_xh, 1)

            def relu(c, j):
                g = c * NB + j
                e.wait_ge(u_mm, g + 1)
                need(e, s_h, g - NR + 1)
                e.activation(r[j % NR][:, :], U[j % 3][:, :], ACT.Relu).then_inc(s_r, 1)

            def hi(c, j):
                g = c * NB + j
                e.wait_ge(s_h, g + 1)
                need(e, d_mm, g - NR + 1)
                e.activation(hh[j % NR][:, :], h[j % NR][:, :], ACT.Copy).then_inc(s_hh, 1)

            def outc(c, p):
                e.wait_ge(d_mm, NB * (c + 1))
                need(e, o_turned, c)
                e.activation(oT[p][:, :], O[p][:, :], ACT.Copy).then_inc(s_o, 1)

            def body(c, p):
                first = isinstance(c, int) and c == 0
                if first:
                    split(0, 0)
                for j in range(NB):
                    relu(c, j)
                    if j >= SLAG:
                        hi(c, j - SLAG)
                    elif not first:
                        hi(c - 1, NB - SLAG + j)
                    if j == LAG and not first:
                        outc(c - 1, 1 - p)
                    if j == 9 and not (isinstance(c, int) and c == NCH - 1):
                        split(c + 1, 1 - p)

            def tail():
                for j in range(SLAG):
                    hi(NCH - 1, NB - SLAG + j)
                outc(NCH - 1, 1)
            chunks(e, body, tail)

        @block.vector
        def _(e):
            def weigh(c, j):
                if j >= NRB:
                    return
                e.wait_ge(s_r, c * NB + j + 1)
                e.wait_ge(c_mm, c * NRB + j + 1)
                need(e, s_h, c * NB + j - NR + 1)
                e.tensor_tensor(tt[j % NR][:, :], C[j % 2][:, :], r[j % NR][:, :], ALU.mult).then_inc(s_t, 1)

            def lo(c, j):
                g = c * NB + j
                e.wait_ge(s_hh, g + 1)
                need(e, d_mm, g - NR + 1)
                e.tensor_tensor(hl[j % NR][:, :], h[j % NR][:, :], hh[j % NR][:, :].bitcast(F32), ALU.subtract).then_inc(s_hl, 1)

            def split(c, p):
                e.wait_ge(s_xh, c + 1)
                e.tensor_tensor(xl[p][:, :], A[:, bass.ds(c * CH, CH)], xh[p][:, :].bitcast(F32), ALU.subtract).then_inc(s_xl, 1)

            def norm(c, p):
                e.wait_ge(o_turned, c + 1)
                n4.stats(e, c, p, tv(TK[:, :]))
                e.wait_ge(stored[p], 8 * (c - p) + 16)
                n4.apply(e, c, p, x4[p], tv(TK[:, :]))

            def body(c, p):
                first = isinstance(c, int) and c == 0
                if first:
                    split(0, 0)
                for j in range(NB):
                    weigh(c, j)
                    if j >= SLAG:
                        lo(c, j - SLAG)
                    elif not first:
                        lo(c - 1, NB - SLAG + j)
                    if j == WL + 1 and not first:
                        norm(c - 1, 1 - p)
                    if j == 11 and not (isinstance(c, int) and c == NCH - 1):
                        split(c + 1, 1 - p)

            def tail():
                for j in range(SLAG):
                    lo(NCH - 1, NB - SLAG + j)
                norm(NCH - 1, 1)
            chunks(e, body, tail)

        @block.gpsimd
        def _(e):
            n4.setup(e)

            def square(c, j):
                g = c * NB + j
                e.wait_ge(s_r, g + 1)
                need(e, s_hl, g - NR + 1)
                if j < NRB:
                    e.wait_ge(s_t, c * NRB + j + 1)
                    e.tensor_tensor(h[j % NR][:, :], tt[j % NR][:, :], r[j % NR][:, :], ALU.mult).then_inc(s_h, 1)
                else:
                    e.tensor_tensor(h[j % NR][:, :], r[j % NR][:, :], r[j % NR][:, :], ALU.mult).then_inc(s_h, 1)

            def body(c, p):
                first = isinstance(c, int) and c == 0
                for j in range(NB):
                    square(c, j)
                    if j == WL + 1 and not first:
                        n4.root(e, c - 1, 1 - p)

            def tail():
                n4.root(e, NCH - 1, 1)
            chunks(e, body, tail)

        @block.sync
        def _(e):
            def store(c, p):
                e.wait_ge(n4.normed, TT * (c + 1))
                e.dma_start(of[bass.ds(c * CH, CH), :].rearrange("(k p) c -> p k c", p=P), x4[p][:, :, :]).then_inc(stored[p], 16)
            for s in stored:
                e.sem_inc(s, 16)
            chunks(e, store, lambda: [e.wait_ge(s, 8 * NCH + 16) for s in stored])


_INS = {
    "L0_attn_x": "x", "L0_attn_A": "A", "L0_attn_Wb": "Wb", "L0_attn_bb": "bb", "L0_attn_Wc": "Wc", "L0_attn_bc": "bc",
    "L0_attn_Wd": "Wd", "L0_attn_bd": "bd", "L0_attn_Wdelta": "Wdelta", "L0_attn_bdelta": "bdelta",
    "L0_ffn_W_r": "W_r", "L0_ffn_W_k": "W_k", "L0_ffn_W_v": "W_v", "L0_ffn_mu_r": "mu_r", "L0_ffn_mu_k": "mu_k",
    "L1_attn_Wq": "Wq", "L1_attn_gq": "gq", "L1_attn_bq": "bq", "L1_attn_Wk": "Wk", "L1_attn_gk": "gk",
    "L1_attn_bk": "bk", "L1_attn_Wv": "Wv", "L1_attn_gv": "gv", "L1_attn_bv": "bv", "L1_attn_Wp": "Wp",
    "L1_attn_bp": "bp", "L1_ffn_gate_w": "gate_w", "L1_ffn_e_bias": "e_bias", "L1_ffn_up_w": "up_w",
    "L1_ffn_down_w": "down_w", "L1_ffn_shared_up_w": "shared_up_w", "L1_ffn_shared_down_w": "shared_down_w",
}


def kernel(**inputs):
    import numpy as _np
    import concourse.bacc as _bacc
    from concourse import mybir as _mybir
    from concourse.bass_utils import run_bass_kernel_spmd as _run

    nc = _bacc.Bacc("TRN2", target_bir_lowering=False, num_devices=1)
    arrays, args = {}, {}
    for name, short in _INS.items():
        a = _np.ascontiguousarray(inputs[name])
        arrays[f"in_{name}_dram"] = a
        args[short] = nc.dram_tensor(f"in_{name}_dram", a.shape, _mybir.dt.from_np(a.dtype), kind="ExternalInput").ap()
    out = nc.dram_tensor("out_0_dram", (B, T, D), _mybir.dt.float32, kind="ExternalOutput").ap()
    build(nc, args, out)
    r = _run(nc, [arrays], core_ids=[0])
    return r.results[0]["out_0_dram"]
```

```python
from contextlib import ExitStack

import numpy as np
import concourse.bass as bass
from concourse import mybir

F32 = mybir.dt.float32
F32R = mybir.dt.float32r
BF16 = mybir.dt.bfloat16
ALU = mybir.AluOpType
ACT = mybir.ActivationFunctionType
AX = mybir.AxisListType

P = 128
B, T, D = 32, 256, 128
NTOK = B * T
CH = 512
NCH = NTOK // CH
TT = CH // P
BC = CH // T
HID = 32
NE, INTER, SHARED = 32, 64, 256
NG, GE = 8, 4
TOPG, TOPK = 4, 6
ROUTED_SCALE = 2.5
NRB = NE * INTER // P
NB = NRB + SHARED // P
EPS = 1e-5
NEG = -3.0e38
TAKEN = 3.0e38
HD = 8
V_TH = 1.0

ROWS = ["bc", "bd", "mu_r", "mu_k", "gq", "bq", "gk", "bk", "gv", "bv", "bp"]
COL = {n: i for i, n in enumerate(ROWS)}
SQ = ["W_r", "W_k", "W_v", "Wq", "Wk", "Wv", "Wp"]


def need(eng, sem, n):
    if isinstance(n, int) and n <= 0:
        return
    eng.wait_ge(sem, n)


def pipeline(eng, stages, n, depth):
    first = depth + 2 + depth % 2
    last = n - n % 2

    def step(s, parity):
        for delay, fn in stages:
            c = s - delay
            if isinstance(s, int) and not 0 <= c < n:
                continue
            fn(c, (parity - delay) % 2)

    for s in range(first):
        step(s, s % 2)
    with eng.Fori(first // 2, last // 2) as i:
        for parity in (0, 1):
            step(2 * i + parity, parity)
    for s in range(last, n + depth):
        step(s, s % 2)


def build(nc, t, out):
    with ExitStack() as ctx:
        def sb(name, shape, dt=F32):
            return ctx.enter_context(nc.sbuf_tensor(name, shape, dt))

        m = {}
        m["act"] = sb("act_ch", [P, NTOK])
        m["tok"] = sb("x2_tok", [P, NTOK // P, D])
        m["hT"] = sb("scan_h", [P, NTOK // 4])
        m["cT"] = sb("combine_ch", [3 * NE, NTOK], BF16)
        for n in ("up_hi", "up_lo", "dn_hi", "dn_lo"):
            m[n] = sb(n, [P, NB, P], F32R)
        m["sqT"] = sb("square_T", [P, len(SQ), P])
        m["wv_nat"] = sb("wv_natural", [P, P])
        m["wdI"] = sb("wd_plus_identity", [P, P])
        m["wc_pad"] = sb("wc_padded", [P, 4, P])
        m["gateT"] = sb("gate_T", [P, NE])
        m["ebias"] = sb("e_bias_rows", [P, NE])
        m["cols"] = sb("channel_columns", [P, len(ROWS)])
        m["aux"] = sb("derived_columns", [P, 16])
        m["ident"] = sb("identity", [P, P])
        m["identb"] = sb("identity_bf16", [P, P], BF16)
        m["identr"] = sb("identity_f32r", [P, P], F32R)
        m["ones"] = sb("ones", [P, P])
        m["onesb"] = sb("ones_bf16", [3, P], BF16)
        m["headmask"] = sb("head_mask", [P, P])
        m["sel"] = sb("expert_select", [3 * NE, NRB, P], BF16)
        m["gram"] = sb("gram", [P, P + 1])
        m["wvT"] = sb("wv_scaled_T", [P, P])
        m["vb3"] = sb("v_bias_rows", [3, TT, P], BF16)
        m["bp3"] = sb("bp_rows", [3, TT, P], BF16)
        m["brow"] = sb("bias_columns", [P, 2])

        scan_block(nc, t, m)
        first_block(nc, t, m)
        fold_block(nc, t, m)
        second_block(nc, t, m)
        experts_block(nc, t, m, out)


def scan_block(nc, t, m):
    with ExitStack() as ctx:
        sb = lambda n, s, d=F32: ctx.enter_context(nc.sbuf_tensor(n, s, d))
        sem = lambda n: ctx.enter_context(nc.semaphore(n))
        ps = lambda n: ctx.enter_context(nc.psum_tensor(n, [P, 512], F32))
        NI = 4
        GT = 4 * T
        xin = [sb(f"x_in{k}", [P, GT // P, D]) for k in range(2)]
        PT = [ps(f"xT{k}") for k in range(4)]
        PD, PB = ps("delta_pre"), ps("b_pre")
        bank = [ps(f"weights_turned{k}") for k in range(2)]
        absd, expd, lnd, pos, delta = (sb(n, [P, 512]) for n in ("absd", "expd", "lnd", "posd", "delta"))
        alog, cum = sb("a_bar_log", [P, 512]), sb("cum", [P, 512])
        clip = sb("cum_clipped", [P, 2, T + 1])
        en, ep, bbar, bsh, bcum = (sb(n, [P, 512]) for n in ("exp_neg", "exp_pos", "b_bar", "b_shift", "b_cum"))
        ones = sb("ones_scan", [P, T])
        acol = sb("a_columns", [P, 4])
        wdelta_pad, wb_pad = sb("wdelta_padded", [P, 4, P + HID]), sb("wb_padded", [P, 4, P + HID])
        window = lambda w, k: w[:, :, :].rearrange("p k c -> p (k c)")[:, P * k:P * (k + 1)]
        later = m["tok"]
        up_raw, dn_raw = later[:, 0:NB, :], later[:, NB:2 * NB, :]
        wide = later[0:3 * NE, 2 * NB:2 * NB + NRB, :].rearrange("p a c -> p (a c)")
        sq_raw = sb("square_raw", [P, len(SQ), P])
        gate_raw = sb("gate_raw", [NE, P])
        scan_rows, rows = sb("scan_rows", [3, P]), sb("vector_rows", [len(ROWS), P])
        eb_row = sb("e_bias_row", [1, NE])

        x_in = [sem("x_in_0"), sem("x_in_1")]
        xt, xe_act, xe_dve, db = sem("x_turned"), sem("x_evac_act"), sem("x_evac_dve"), sem("delta_b_ready")
        s_abs, s_exp, s_ln, s_pos, s_delta = sem("abs_done"), sem("exp_done"), sem("ln_done"), sem("pos_done"), sem("delta_done")
        s_alog, s_cum, s_clip, s_en, s_ep = sem("alog_done"), sem("cum_done"), sem("clip_done"), sem("exp_neg_done"), sem("exp_pos_done")
        s_bbar, s_bsh, s_bcum, s_h, setup = sem("bbar_done"), sem("bshift_done"), sem("bcum_done"), sem("h_done"), sem("scan_setup")
        s_a, a_ready = sem("a_softplus"), sem("a_columns_done")
        zero_done, ident_done, masks = sem("zero_done"), sem("ident_done"), sem("masks_step")
        scan_in, row_in, sq_in, wd_in, up_in, dn_in = (sem(n) for n in ("scan_weights_in", "rows_in", "square_in", "wd_in", "up_in", "down_in"))
        turned, evac_act, evac_dve, cols_done, fixed = (sem(n) for n in ("weights_turned", "weights_hi", "weights_lo", "scan_columns_done", "wd_identity"))
        xf = t["x"].rearrange("b t c -> (b t) c")
        A, hT = m["act"], m["hT"]
        scol = sb("scan_columns", [P, 3])
        row = lambda name: t[name].rearrange("(a c) -> a c", a=1)

        jobs = [("cols", 0, 1), ("gate", 0, 1), ("ebias", 0, 1)]
        jobs += [(kind, a, min(4, n - a)) for kind, n in (("sq", len(SQ)), ("up", NB), ("dn", NB)) for a in range(0, n, 4)]
        split_at = [sum(k in ("up", "dn") for k, _, _ in jobs[:g + 1]) for g in range(len(jobs))]
        turns = [[], jobs[0:5], jobs[5:8], jobs[8:11], jobs[11:13], jobs[13:]]
        of_step, at = [], 0
        for some in turns:
            of_step.append(list(range(at, at + len(some))))
            at += len(some)
        assert at == len(jobs)

        def steps(stages, weights):
            for s in range(NI + 2):
                for delay, fn in stages:
                    if 0 <= s - delay < NI:
                        fn(s - delay)
                for g in of_step[s]:
                    weights(g, *jobs[g])

        block = ctx.enter_context(nc.Block())

        @block.sync
        def _(e):
            def load(i, k):
                need(e, xt, 4 * (i - 1) + 2 * k + 2)
                src = xf[(2 * i + k) * GT:(2 * i + k + 1) * GT, :].rearrange("(a p) c -> p a c", p=P)
                e.dma_start(xin[k][:, :, :], src).then_inc(x_in[k], 16)

            load(0, 0)
            load(0, 1)
            e.wait_ge(zero_done, 2)
            for w, name in ((wdelta_pad, "Wdelta"), (wb_pad, "Wb")):
                e.dma_start(w[:, :, 0:HID], t[name].rearrange("p (k c) -> p k c", k=1).broadcast_to([P, 4, HID])).then_inc(scan_in, 16)
            for i, name in enumerate(SQ):
                e.dma_start(sq_raw[:, i, :], t[name]).then_inc(sq_in, 16)
            load(1, 0)
            load(1, 1)
            for name in ("bc", "bd", "mu_r", "mu_k", "gq", "bq", "gk", "bk", "gv", "bv", "bp"):
                e.dma_start(rows[COL[name]:COL[name] + 1, :], row(name)).then_inc(row_in, 16)
            load(2, 0)
            load(2, 1)
            load(3, 0)
            load(3, 1)
            e.wait_ge(zero_done, 3)
            for k in range(4):
                e.dma_start(m["wc_pad"][HID * k:HID * (k + 1), k, :], t["Wc"]).then_inc(wd_in, 16)
            e.wait_ge(wd_in, 16 * 6)

        @block.scalar
        def _(e):
            for r, name in enumerate(("bdelta", "bb", "A")):
                e.dma_start(scan_rows[r:r + 1, :].rearrange("p (k c) -> p k c", k=4),
                            t[name].rearrange("(a k c) -> a k c", a=1, k=1).broadcast_to([1, 4, HID])).then_inc(scan_in, 16)
            e.dma_start(eb_row[:, :], row("e_bias")).then_inc(row_in, 16)
            e.dma_start(gate_raw[:, :], t["gate_w"]).then_inc(row_in, 16)
            e.dma_start(up_raw[:, 0:NRB, :], t["up_w"].rearrange("(j e) i h -> (e i) j h", e=2)).then_inc(up_in, 16)
            e.dma_start(up_raw[:, NRB:NB, :], t["shared_up_w"].rearrange("(j p) h -> p j h", p=P)).then_inc(up_in, 16)
            for ee in range(2):
                e.dma_start(dn_raw[:, 0:NRB, INTER * ee:INTER * (ee + 1)],
                            t["down_w"].rearrange("(j e) h i -> e h j i", e=2)[ee]).then_inc(dn_in, 16)
            e.dma_start(dn_raw[:, NRB:NB, :], t["shared_down_w"].rearrange("h (j p) -> h j p", p=P)).then_inc(dn_in, 16)
            e.dma_start(m["wdI"][:, :], t["Wd"]).then_inc(wd_in, 16)
            e.dma_start(m["wv_nat"][:, :], t["Wv"]).then_inc(wd_in, 16)

            e.wait_ge(cols_done, 2)
            e.activation(acol[:, 0:1], scol[:, 2:3], ACT.Abs).then_inc(s_a, 1)
            e.wait_ge(s_a, 1)
            e.activation(acol[:, 1:2], acol[:, 0:1], ACT.Exp, scale=-1.0).then_inc(s_a, 1)
            e.wait_ge(s_a, 2)
            e.activation(acol[:, 2:3], acol[:, 1:2], ACT.Ln, bias=1.0).then_inc(s_a, 1)

            def copy_x(i):
                for k in range(2):
                    e.wait_ge(xt, 4 * i + k + 1)
                    e.activation(A[:, 2 * i * GT + k * 512:2 * i * GT + (k + 1) * 512], PT[k][:, :], ACT.Copy).then_inc(xe_act, 1)

            def exponents(i):
                e.wait_ge(s_clip, i + 1)
                need(e, s_bsh, i)
                e.activation(en[:, :].rearrange("p (g t) -> p g t", g=2), clip[:, :, 0:T], ACT.Exp, scale=-1.0).then_inc(s_en, 1)
                need(e, s_h, i)
                e.activation(ep[:, :].rearrange("p (g t) -> p g t", g=2), clip[:, :, 1:T + 1], ACT.Exp).then_inc(s_ep, 1)

            def softplus(i):
                e.wait_ge(db, 2 * i + 1)
                e.activation(absd[:, :], PD[:, :], ACT.Abs, bias=scol[:, 0:1]).then_inc(s_abs, 1)
                e.wait_ge(s_abs, i + 1)
                e.activation(expd[:, :], absd[:, :], ACT.Exp, scale=-1.0).then_inc(s_exp, 1)
                e.wait_ge(s_exp, i + 1)
                need(e, s_delta, i)
                e.activation(lnd[:, :], expd[:, :], ACT.Ln, bias=1.0).then_inc(s_ln, 1)

            def weights(g, kind, a, n):
                if kind in ("up", "dn"):
                    e.wait_ge(turned, g + 1)
                    e.activation(m[kind + "_hi"][:, a:a + n, :], bank[g % 2][:, 0:n * P].rearrange("p (a b) -> p a b", b=P),
                                 ACT.Copy).then_inc(evac_act, 1)

            steps([(0, copy_x), (2, exponents), (1, softplus)], weights)

        @block.gpsimd
        def _(e):
            e.memset(m["ident"][:, :], 0.0).then_inc(masks, 1)
            e.wait_ge(masks, 1)
            e.affine_select(out=m["ident"][:, :], in_=m["ident"][:, :], compare_op=ALU.not_equal, fill=1.0,
                            base=0, pattern=[[-1, P]], channel_multiplier=1).then_inc(ident_done, 1)
            e.memset(m["ones"][:, :], 1.0).then_inc(masks, 1)
            e.wait_ge(masks, 2)
            e.affine_select(out=m["headmask"][:, :].rearrange("p (a b) -> p a b", b=HD),
                            in_=m["ones"][:, :].rearrange("p (a b) -> p a b", b=HD),
                            compare_op=ALU.is_ge, fill=0.0, base=0, pattern=[[-HD, P // HD], [0, HD]],
                            channel_multiplier=1).then_inc(masks, 1)
            e.wait_ge(masks, 3)
            e.affine_select(out=m["headmask"][:, :].rearrange("p (a b) -> p a b", b=HD),
                            in_=m["headmask"][:, :].rearrange("p (a b) -> p a b", b=HD),
                            compare_op=ALU.is_ge, fill=0.0, base=HD - 1, pattern=[[HD, P // HD], [0, HD]],
                            channel_multiplier=-1).then_inc(masks, 1)
            e.memset(wide[:, :], 0.0).then_inc(masks, 1)
            for part in range(3):
                e.wait_ge(masks, 5 + part)
                w = wide[:, :].rearrange("p (j c) -> p j c", c=INTER)
                e.affine_select(out=w, in_=w, compare_op=ALU.not_equal, fill=1.0, base=-NE * part,
                                pattern=[[-1, NE], [0, INTER]], channel_multiplier=1).then_inc(masks, 1)

            def shifted(i):
                e.wait_ge(s_bbar, i + 1)
                e.wait_ge(s_en, i + 1)
                need(e, s_bcum, 2 * i)
                e.tensor_tensor(bsh[:, :], bbar[:, :], en[:, :], ALU.mult).then_inc(s_bsh, 1)
                e.wait_ge(s_bcum, 2 * i + 2)
                e.wait_ge(s_ep, i + 1)
                e.tensor_tensor(hT[:, i * 512:(i + 1) * 512], bcum[:, :], ep[:, :], ALU.mult).then_inc(s_h, 1)
            for i in range(NI):
                shifted(i)

        @block.tensor
        def _(e):
            def turn_x(i):
                for k in range(4):
                    if k % 2 == 0:
                        e.wait_ge(x_in[k // 2], 16 * (i + 1))
                    need(e, xe_act if k < 2 else xe_dve, 2 * (i - 1) + k % 2 + 1)
                    for a in range(4):
                        last = e.transpose(PT[k][:, a * P:(a + 1) * P], xin[k // 2][:, 4 * (k % 2) + a, :],
                                           m["ident"][:, :])
                    last.then_inc(xt, 1)

            def delta_b(i):
                if i == 0:
                    e.wait_ge(scan_in, 16 * 5)
                e.wait_ge(xe_act, 2 * (i + 1))
                e.wait_ge(xe_dve, 2 * (i + 1))
                need(e, s_pos, i)
                need(e, s_abs, i)
                need(e, s_bbar, i)
                for dst, w in ((PD, wdelta_pad), (PB, wb_pad)):
                    for g in range(2):
                        for k in range(4):
                            at = (2 * i + g) * GT + k * T
                            last = e.matmul(dst[:, g * T:(g + 1) * T], window(w, k), A[:, at:at + T],
                                            start=(k == 0), stop=(k == 3))
                    last.then_inc(db, 1)

            def weights(g, kind, a, n):
                if kind in ("cols", "gate", "ebias"):
                    e.wait_ge(row_in, 16 * 13)
                if kind == "ebias":
                    e.wait_ge(masks, 2)
                if kind in ("sq", "up", "dn"):
                    e.wait_ge(*{"sq": (sq_in, 16 * len(SQ)), "up": (up_in, 32), "dn": (dn_in, 48)}[kind])
                if g >= 2:
                    need(e, evac_act, split_at[g - 2])
                    need(e, evac_dve, g - 1)
                bk = bank[g % 2]
                if kind == "cols":
                    last = e.transpose(bk[:, 0:len(ROWS)], rows[:, :], m["ident"][0:len(ROWS), 0:len(ROWS)])
                elif kind == "gate":
                    last = e.transpose(bk[:, 0:NE], gate_raw[:, :], m["ident"][0:NE, 0:NE])
                elif kind == "ebias":
                    last = e.matmul(bk[:, 0:NE], m["ones"][0:1, :], eb_row[:, :], start=True, stop=True)
                else:
                    raw = {"sq": sq_raw, "up": up_raw, "dn": dn_raw}[kind]
                    for k in range(n):
                        last = e.transpose(bk[:, k * P:(k + 1) * P], raw[:, a + k, :], m["ident"][:, :])
                last.then_inc(turned, 1)

            e.wait_ge(ident_done, 1)
            e.wait_ge(scan_in, 16 * 5)
            e.transpose(PD[:, 0:3], scan_rows[:, :], m["ident"][0:3, 0:3]).then_inc(cols_done, 1)
            e.wait_ge(cols_done, 2)
            steps([(0, turn_x), (1, delta_b)], weights)

        @block.vector
        def _(e):
            e.memset(wdelta_pad[:, :, :], 0.0).then_inc(zero_done, 1)
            e.memset(wb_pad[:, :, :], 0.0).then_inc(zero_done, 1)
            e.memset(m["wc_pad"][:, :, :], 0.0).then_inc(zero_done, 1)
            e.memset(ones[:, :], 1.0).then_inc(setup, 1)
            e.memset(clip[:, :, 0:1], 0.0).then_inc(setup, 1)
            e.memset(m["onesb"][:, :], 1.0).then_inc(setup, 1)
            e.wait_ge(cols_done, 1)
            e.tensor_copy(scol[:, :], PD[:, 0:3]).then_inc(cols_done, 1)
            e.wait_ge(s_a, 3)
            e.tensor_scalar(acol[:, 3:4], scol[:, 2:3], 0.0, None, ALU.max).then_inc(a_ready, 1)
            e.wait_ge(a_ready, 1)
            e.tensor_tensor(acol[:, 3:4], acol[:, 3:4], acol[:, 2:3], ALU.add).then_inc(a_ready, 1)
            e.wait_ge(a_ready, 2)
            e.tensor_scalar(acol[:, 3:4], acol[:, 3:4], -1.0, None, ALU.mult).then_inc(a_ready, 1)
            e.wait_ge(a_ready, 3)
            e.wait_ge(setup, 3)

            def copy_x(i):
                for k in range(2):
                    e.wait_ge(xt, 4 * i + k + 3)
                    at = 2 * i * GT + (k + 2) * 512
                    e.tensor_copy(A[:, at:at + 512], PT[2 + k][:, :]).then_inc(xe_dve, 1)

            def sums(i):
                e.wait_ge(s_abs, i + 1)
                e.tensor_scalar(pos[:, :], PD[:, :], scol[:, 0:1], 0.0, ALU.add, ALU.max).then_inc(s_pos, 1)
                e.wait_ge(s_pos, i + 1)
                e.wait_ge(s_ln, i + 1)
                e.tensor_tensor(delta[:, :], pos[:, :], lnd[:, :], ALU.add).then_inc(s_delta, 1)
                e.wait_ge(s_delta, i + 1)
                e.tensor_scalar(alog[:, :], delta[:, :], acol[:, 3:4], None, ALU.mult).then_inc(s_alog, 1)
                e.wait_ge(s_alog, i + 1)
                for g in range(2):
                    e.tensor_tensor_scan(cum[:, g * T:(g + 1) * T], ones[:, :], alog[:, g * T:(g + 1) * T], 0.0,
                                         ALU.mult, ALU.add).then_inc(s_cum, 1)
                e.wait_ge(db, 2 * i + 2)
                need(e, s_bsh, i)
                e.scalar_tensor_tensor(out=bbar[:, :], in0=PB[:, :], scalar=scol[:, 1:2], in1=delta[:, :],
                                       op0=ALU.add, op1=ALU.mult).then_inc(s_bbar, 1)
                e.wait_ge(s_cum, 2 * i + 2)
                need(e, s_en, i)
                need(e, s_ep, i)
                e.tensor_scalar(clip[:, :, 1:T + 1], cum[:, :].rearrange("p (g t) -> p g t", g=2), -20.0, 20.0,
                                ALU.max, ALU.min).then_inc(s_clip, 1)

            def second_sum(i):
                e.wait_ge(s_bsh, i + 1)
                need(e, s_h, i)
                for g in range(2):
                    e.tensor_tensor_scan(bcum[:, g * T:(g + 1) * T], ones[:, :], bsh[:, g * T:(g + 1) * T], 0.0,
                                         ALU.mult, ALU.add).then_inc(s_bcum, 1)

            def weights(g, kind, a, n):
                e.wait_ge(turned, g + 1)
                bk = bank[g % 2]
                bv = bk[:, 0:n * P].rearrange("p (a b) -> p a b", b=P)
                if kind == "cols":
                    ins = e.tensor_copy(m["cols"][:, :], bk[:, 0:len(ROWS)])
                elif kind == "gate":
                    ins = e.tensor_copy(m["gateT"][:, :], bk[:, 0:NE])
                elif kind == "ebias":
                    ins = e.tensor_copy(m["ebias"][:, :], bk[:, 0:NE])
                elif kind == "sq":
                    ins = e.tensor_copy(m["sqT"][:, a:a + n, :], bv)
                else:
                    e.wait_ge(evac_act, split_at[g])
                    ins = e.tensor_tensor(m[kind + "_lo"][:, a:a + n, :], bv,
                                          m[kind + "_hi"][:, a:a + n, :].bitcast(F32), ALU.subtract)
                ins.then_inc(evac_dve, 1)

            steps([(0, copy_x), (2, second_sum), (1, sums)], weights)
            e.wait_ge(masks, 8)
            e.tensor_copy(m["sel"][:, :, :].rearrange("p j c -> p (j c)"), wide[:, :]).then_inc(fixed, 1)
            e.tensor_copy(m["identb"][:, :], m["ident"][:, :]).then_inc(fixed, 1)
            e.tensor_copy(m["identr"][:, :], m["ident"][:, :]).then_inc(fixed, 1)
            e.wait_ge(wd_in, 16 * 6)
            e.tensor_tensor(m["wdI"][:, :], m["wdI"][:, :], m["ident"][:, :], ALU.add).then_inc(fixed, 1)
            e.wait_ge(evac_dve, 1)
            c = m["cols"]
            e.tensor_tensor(m["aux"][:, 0:1], c[:, COL["bc"]:COL["bc"] + 1], c[:, COL["bd"]:COL["bd"] + 1],
                            ALU.add).then_inc(fixed, 1)


class Norm:

    def __init__(self, ctx, nc, name):
        sb = lambda n, s: ctx.enter_context(nc.sbuf_tensor(f"{name}_{n}", s, F32))
        sem = lambda n: ctx.enter_context(nc.semaphore(f"{name}_{n}"))
        self.parts = [sb(f"parts{k}", [P, TT, 6]) for k in range(2)]
        self.mv = [sb(f"mv{k}", [P, TT, 2]) for k in range(2)]
        self.ve = [sb(f"ve{k}", [P, TT]) for k in range(2)]
        self.rstd = [sb(f"rstd{k}", [P, TT]) for k in range(2)]
        self.mr, self.nmr = ([sb(f"{n}{k}", [P, TT]) for k in range(2)] for n in ("mean_rstd", "minus_mean_rstd"))
        self.power, self.eps, self.minus = sb("power", [P, TT]), sb("eps", [P, TT]), sb("minus_one", [P, TT])
        self.mr_done, self.nmr_done = sem("mean_rstd_done"), sem("minus_mean_rstd_done")
        self.stats_done, self.mv_done = sem("stats_done"), sem("mv_done")
        self.ve_done, self.rstd_done, self.normed = sem("ve_done"), sem("rstd_done"), sem("normed")
        self.power_set, self.gate = sem("power_set"), sem("gate")

    def setup(self, pool):
        pool.memset(self.power[:, :], -0.5).then_inc(self.power_set, 1)
        pool.memset(self.eps[:, :], EPS).then_inc(self.power_set, 1)
        pool.memset(self.minus[:, :], -1.0).then_inc(self.power_set, 1)
        pool.wait_ge(self.power_set, 3)

    def stats(self, dve, c, par, src):
        for k in range(TT):
            dve.bn_stats(self.parts[par][:, k, :], src[:, k, :]).then_inc(self.stats_done, 1)
        dve.wait_ge(self.stats_done, TT * (c + 1))
        need(dve, self.normed, TT * c)
        dve.sem_inc(self.gate, 1)
        for k in range(TT):
            dve.bn_aggr(self.mv[par][:, k, :], self.parts[par][:, k, :]).then_inc(self.mv_done, 1)

    def root(self, pool, c, par):
        pool.wait_ge(self.mv_done, TT * (c + 1))
        pool.tensor_tensor(self.ve[par][:, :], self.mv[par][:, :, 1], self.eps[:, :], ALU.add).then_inc(self.ve_done, 1)
        pool.wait_ge(self.ve_done, c + 1)
        need(pool, self.normed, TT * c)
        pool.tensor_tensor(self.rstd[par][:, :], self.ve[par][:, :], self.power[:, :], ALU.pow).then_inc(self.rstd_done, 1)

    def shift(self, pool, c, par):
        pool.wait_ge(self.rstd_done, c + 1)
        pool.tensor_tensor(self.mr[par][:, :], self.mv[par][:, :, 0], self.rstd[par][:, :], ALU.mult).then_inc(self.mr_done, 1)
        pool.wait_ge(self.mr_done, c + 1)
        pool.tensor_tensor(self.nmr[par][:, :], self.mr[par][:, :], self.minus[:, :], ALU.mult).then_inc(self.nmr_done, 1)

    def apply_act(self, act, c, par, dst, src):
        act.wait_ge(self.nmr_done, c + 1)
        for k in range(TT):
            act.activation(dst[:, k, 0:D], src[:, k, :], ACT.Identity, bias=self.nmr[par][:, k:k + 1],
                           scale=self.rstd[par][:, k:k + 1]).then_inc(self.normed, 1)

    def apply(self, dve, c, par, dst, src):
        dve.wait_ge(self.mv_done, TT * (c + 1))
        dve.wait_ge(self.rstd_done, c + 1)
        for k in range(TT):
            dve.tensor_scalar(dst[:, k, 0:D], src[:, k, :], self.mv[par][:, k, 0:1], self.rstd[par][:, k:k + 1],
                              ALU.subtract, ALU.mult).then_inc(self.normed, 1)


def first_block(nc, t, m):
    with ExitStack() as ctx:
        sb = lambda n, s, d=F32: ctx.enter_context(nc.sbuf_tensor(n, s, d))
        sem = lambda n: ctx.enter_context(nc.semaphore(n))
        ps = lambda n: ctx.enter_context(nc.psum_tensor(n, [P, CH], F32))
        two = lambda n, s=(P, CH): [sb(f"{n}{k}", list(s)) for k in range(2)]
        YT, YK, X1, RP, KP, ZK, X2, GP = (ps(n) for n in ("y_ch", "y_tok", "x1_ch", "r_pre", "k_pre", "z_tok", "x2_ch", "gram_sum"))
        VP = RP
        yT, x1k = two("y_sb"), two("x1_tok", (P, TT, D))
        x1T = two("x1T", (P, BC, T + 1))
        diff, xr, xk, rr, kr, k2, vr, zT = (two(n) for n in ("diff", "xr", "xk", "r", "k_relu", "k_sq", "v_r", "zT"))
        x2k = two("x2_stage", (P, TT, D + 1))
        n1, n2 = Norm(ctx, nc, "norm1"), Norm(ctx, nc, "norm2")
        zrow = sb("zero_row", [1, P + 1])
        A, hT, aux, cols = m["act"], m["hT"], m["aux"], m["cols"]
        cc = lambda n: cols[:, COL[n]:COL[n] + 1]
        bv = lambda ap: ap.rearrange("p (b t) -> p b t", b=BC)
        tv = lambda ap: ap.rearrange("p (k c) -> p k c", k=TT)

        y_mm, y_sb, y_tok, x1_turned, x1_copied = sem("y_mm"), sem("y_sb_done"), sem("y_turned"), sem("x1_turned"), sem("x1_copied")
        s_diff, s_xr, s_xk, r_mm, k_mm = sem("diff_done"), sem("xr_done"), sem("xk_done"), sem("r_mm"), sem("k_mm")
        s_r, s_kr, s_k2, v_mm, s_vr, s_z = sem("r_done"), sem("krelu_done"), sem("ksq_done"), sem("v_mm"), sem("vr_done"), sem("z_done")
        z_turned, x2_turned, x2_copied, gram_mm, stored = sem("z_turned"), sem("x2_turned"), sem("x2_copied"), sem("gram_mm"), [sem("x2_stored0"), sem("x2_stored1")]
        setup, gram_out, zeroed = sem("first_setup"), sem("gram_out"), sem("gram_zeroed")
        block = ctx.enter_context(nc.Block())

        @block.tensor
        def _(e):
            e.wait_ge(setup, 5)
            e.matmul(GP[:, 0:P + 1], m["ones"][0:1, :], zrow[0:1, :], start=True, stop=False).then_inc(zeroed, 1)

            def attention(c, p):
                need(e, y_sb, c)
                e.matmul(YT[:, :], m["wdI"][:, :], A[:, bass.ds(c * CH, CH)], start=True, stop=False)
                for b in range(BC):
                    last = e.matmul(YT[:, b * T:(b + 1) * T], m["wc_pad"][:, BC * p + b, :],
                                    hT[:, bass.ds((c - p) * (T // 2), T)], start=False, stop=(b == BC - 1))
                last.then_inc(y_mm, 1)

            def value(c, p):
                e.wait_ge(s_k2, c + 1)
                e.wait_ge(s_r, c + 1)
                e.matmul(VP[:, :], m["sqT"][:, SQ.index("W_v"), :], k2[p][:, :], start=True, stop=True).then_inc(v_mm, 1)

            def receptance(c, p):
                e.wait_ge(s_xk, c + 1)
                need(e, s_kr, c)
                need(e, s_k2, c)
                e.matmul(KP[:, :], m["sqT"][:, SQ.index("W_k"), :], xk[p][:, :], start=True, stop=True).then_inc(k_mm, 1)
                e.wait_ge(s_xr, c + 1)
                need(e, s_vr, c)
                e.matmul(RP[:, :], m["sqT"][:, SQ.index("W_r"), :], xr[p][:, :], start=True, stop=True).then_inc(r_mm, 1)

            def turn_y(c, p):
                e.wait_ge(y_sb, c + 1)
                need(e, n1.normed, TT * c)
                for k in range(TT):
                    last = e.transpose(YK[:, k * P:(k + 1) * P], yT[p][:, k * P:(k + 1) * P], m["ident"][:, :])
                last.then_inc(y_tok, 1)

            def turn_z(c, p):
                e.wait_ge(s_z, c + 1)
                need(e, n2.normed, TT * c)
                for k in range(TT):
                    last = e.transpose(ZK[:, k * P:(k + 1) * P], zT[p][:, k * P:(k + 1) * P], m["ident"][:, :])
                last.then_inc(z_turned, 1)

            def turn_x1(c, p):
                e.wait_ge(n1.normed, TT * (c + 1))
                need(e, x1_copied, c)
                for k in range(TT):
                    last = e.transpose(X1[:, k * P:(k + 1) * P], x1k[p][:, k, :], m["ident"][:, :])
                last.then_inc(x1_turned, 1)

            def turn_x2(c, p):
                e.wait_ge(n2.normed, TT * (c + 1))
                need(e, x2_copied, c)
                for k in range(TT):
                    last = e.transpose(X2[:, k * P:(k + 1) * P], x2k[p][:, k, 0:D], m["ident"][:, :])
                last.then_inc(x2_turned, 1)
                for k in range(TT):
                    last = e.matmul(GP[:, 0:D + 1], x2k[p][:, k, 0:D], x2k[p][:, k, :], start=False,
                                    stop=False, skip_group_check=True)
                last.then_inc(gram_mm, 1)

            pipeline(e, [(0, attention), (3, value), (2, receptance), (0, turn_y), (3, turn_z), (1, turn_x1),
                         (4, turn_x2)], NCH, 4)
            e.matmul(GP[:, 0:P + 1], m["ones"][0:1, :], zrow[0:1, :], start=False, stop=True).then_inc(zeroed, 1)

        @block.scalar
        def _(e):
            def norm1(c, p):
                need(e, x1_turned, c - 1)
                n1.apply_act(e, c, p, x1k[p], tv(YK[:, :]))

            def copy_y(c, p):
                e.wait_ge(y_mm, c + 1)
                need(e, y_tok, c - 1)
                e.activation(yT[p][:, :], YT[:, :], ACT.Identity, bias=aux[:, 0:1]).then_inc(y_sb, 1)

            def norm2(c, p):
                need(e, x2_turned, c - 1)
                need(e, gram_mm, c - 1)
                need(e, stored[p], 8 * (c - p))
                n2.apply_act(e, c, p, x2k[p], tv(ZK[:, :]))

            def receptance(c, p):
                e.wait_ge(k_mm, c + 1)
                need(e, s_k2, c - 1)
                e.activation(kr[p][:, :], KP[:, :], ACT.Relu).then_inc(s_kr, 1)
                e.wait_ge(r_mm, c + 1)
                need(e, s_vr, c - 1)
                e.activation(rr[p][:, :], RP[:, :], ACT.Sigmoid).then_inc(s_r, 1)

            def copy_x1(c, p):
                e.wait_ge(x1_turned, c + 1)
                need(e, s_z, c - 1)
                need(e, s_xr, c - 1)
                need(e, s_xk, c - 1)
                e.activation(x1T[p][:, :, 1:T + 1], bv(X1[:, :]), ACT.Copy).then_inc(x1_copied, 1)

            def copy_x2(c, p):
                e.wait_ge(x2_turned, c + 1)
                e.activation(A[:, bass.ds(c * CH, CH)], X2[:, :], ACT.Copy).then_inc(x2_copied, 1)

            pipeline(e, [(1, norm1), (0, copy_y), (4, norm2), (2, receptance), (1, copy_x1), (4, copy_x2)], NCH, 4)

        @block.vector
        def _(e):
            e.memset(zrow[:, :], 0.0).then_inc(setup, 1)
            for k in range(2):
                e.memset(x1T[k][:, :, 0:1], 0.0).then_inc(setup, 1)
                e.memset(x2k[k][:, :, D:D + 1], 1.0).then_inc(setup, 1)

            def mix(c, p):
                e.wait_ge(x1_copied, c + 1)
                need(e, s_xr, c)
                e.tensor_tensor(bv(diff[p][:, :]), x1T[p][:, :, 1:T + 1], x1T[p][:, :, 0:T], ALU.subtract).then_inc(s_diff, 1)
                e.wait_ge(s_diff, c + 1)
                for mu, dst, done, used in (("mu_k", xk, s_xk, k_mm), ("mu_r", xr, s_xr, r_mm)):
                    need(e, used, c - 1)
                    e.scalar_tensor_tensor(out=bv(dst[p][:, :]), in0=bv(diff[p][:, :]), scalar=cc(mu),
                                           in1=x1T[p][:, :, 0:T], op0=ALU.mult, op1=ALU.add).then_inc(done, 1)

            def gate(c, p):
                e.wait_ge(v_mm, c + 1)
                e.wait_ge(s_r, c + 1)
                need(e, s_z, c - 1)
                e.tensor_tensor(vr[p][:, :], VP[:, :], rr[p][:, :], ALU.mult).then_inc(s_vr, 1)

            def square(c, p):
                e.wait_ge(s_kr, c + 1)
                need(e, v_mm, c - 1)
                e.scalar_tensor_tensor(out=k2[p][:, :], in0=KP[:, :], scalar=0.0, in1=kr[p][:, :],
                                       op0=ALU.max, op1=ALU.mult).then_inc(s_k2, 1)

            def stats1(c, p):
                e.wait_ge(y_tok, c + 1)
                n1.stats(e, c, p, tv(YK[:, :]))

            def stats2(c, p):
                e.wait_ge(z_turned, c + 1)
                n2.stats(e, c, p, tv(ZK[:, :]))

            pipeline(e, [(2, mix), (3, gate), (2, square), (0, stats1), (3, stats2)], NCH, 4)
            e.wait_ge(zeroed, 2)
            e.tensor_scalar(m["gram"][:, :], GP[:, 0:P + 1], 1.0 / NTOK, None, ALU.mult).then_inc(gram_out, 1)

        @block.gpsimd
        def _(e):
            n1.setup(e)
            n2.setup(e)
            e.wait_ge(setup, 5)

            def residual(c, p):
                e.wait_ge(s_vr, c + 1)
                need(e, z_turned, c - 1)
                e.tensor_tensor(bv(zT[p][:, :]), bv(vr[p][:, :]), x1T[p][:, :, 1:T + 1], ALU.add).then_inc(s_z, 1)

            def root1(c, p):
                n1.root(e, c, p)
                n1.shift(e, c, p)

            def root2(c, p):
                n2.root(e, c, p)
                n2.shift(e, c, p)

            pipeline(e, [(3, residual), (0, root1), (3, root2)], NCH, 4)

        @block.sync
        def _(e):
            def keep(c, p):
                e.wait_ge(n2.normed, TT * (c + 1))
                e.dma_start(m["tok"][:, bass.ds(c * TT, TT), :], x2k[p][:, :, 0:D]).then_inc(stored[p], 16)

            pipeline(e, [(4, keep)], NCH, 4)
            for s in stored:
                e.wait_ge(s, 8 * NCH)


def fold_block(nc, t, m):
    with ExitStack() as ctx:
        sb = lambda n, s, d=F32: ctx.enter_context(nc.sbuf_tensor(n, s, d))
        sem = lambda n: ctx.enter_context(nc.semaphore(n))
        ps = lambda n, d=F32: ctx.enter_context(nc.psum_tensor(n, [P, 512], d))
        GW, ST, TR, TB = ps("gram_w"), ps("bn_sums"), ps("v_turned"), ps("rows_turned", BF16)
        prod = sb("w_gram_w", [P, 3, P])
        st = sb("bn_columns", [P, 8, 3])
        half = sb("half_power", [P, 3])
        parts = sb("row_parts", [P, 2, 3], BF16)
        rest = sb("row_rest", [P, 2, 2])
        mm, dv, pw, pl = sem("fold_mm"), sem("fold_dve"), sem("fold_power"), sem("fold_pool")
        block = ctx.enter_context(nc.Block())
        WT = m["sqT"][:, SQ.index("Wq"):SQ.index("Wq") + 3, :]
        aux, cols = m["aux"], m["cols"]
        gam = cols[:, COL["gq"]:COL["gq"] + 6].rearrange("p (b k) -> p k b", k=2)

        @block.tensor
        def _(e):
            e.matmul(GW[:, 0:3 * P], m["gram"][:, 0:P], WT, start=True, stop=True).then_inc(mm, 1)
            e.wait_ge(dv, 1)
            for b in range(3):
                e.matmul(ST[:, b:b + 1], WT[:, b, :], m["gram"][:, P:P + 1], start=(b == 0), stop=True,
                         skip_group_check=True)
            for b in range(3):
                last = e.matmul(ST[:, 4 + b:5 + b], prod[:, b, :], m["ones"][:, 0:1], start=False, stop=True,
                                skip_group_check=True)
            last.then_inc(mm, 1)
            e.wait_ge(dv, 7)
            e.transpose(TR[:, 0:P], m["wv_nat"][:, :], m["ident"][:, :]).then_inc(mm, 1)
            e.wait_ge(dv, 12)
            e.transpose(TB[0:3, 0:P], parts[:, 0, :], m["identb"][:, :])
            e.transpose(TB[0:3, P:2 * P], parts[:, 1, :], m["identb"][:, :]).then_inc(mm, 1)

        @block.gpsimd
        def _(e):
            e.memset(half[:, :], -0.5).then_inc(pl, 1)
            e.wait_ge(pl, 1)
            e.wait_ge(dv, 4)
            e.tensor_tensor(st[:, 5, :], st[:, 4, :], half[:, :], ALU.pow).then_inc(pw, 1)

        @block.vector
        def _(e):
            n = [0]

            def done(ins):
                ins.then_inc(dv, 1)
                n[0] += 1
                e.wait_ge(dv, n[0])

            e.wait_ge(mm, 1)
            done(e.tensor_tensor(prod[:, :, :], GW[:, 0:3 * P].rearrange("p (b c) -> p b c", b=3), WT, ALU.mult))
            e.wait_ge(mm, 2)
            e.tensor_copy(st[:, 1, :], ST[:, 4:7])
            done(e.tensor_copy(st[:, 0, :], ST[:, 0:3]))
            done(e.tensor_tensor(st[:, 2, :], st[:, 0, :], st[:, 0, :], ALU.mult))
            e.scalar_tensor_tensor(out=st[:, 3, :], in0=st[:, 2, :], scalar=-1.0, in1=ST[:, 4:7],
                                   op0=ALU.mult, op1=ALU.add).then_inc(pl, 1)
            e.wait_ge(pl, 2)
            done(e.tensor_scalar(st[:, 4, :], st[:, 3, :], 0.0, EPS, ALU.max, ALU.add))
            e.wait_ge(pw, 1)
            done(e.scalar_tensor_tensor(out=st[:, 6, :], in0=st[:, 5, :], scalar=4.0, in1=gam[:, 0, :],
                                        op0=ALU.mult, op1=ALU.mult))
            done(e.tensor_tensor(st[:, 7, :], st[:, 0, :], st[:, 6, :], ALU.mult))
            e.tensor_copy(aux[:, 2:5], st[:, 6, :])
            done(e.tensor_scalar(m["wv_nat"][:, :], m["wv_nat"][:, :], st[:, 6, 2:3], None, ALU.mult))
            done(e.tensor_scalar(aux[:, 5:8], gam[:, 1, :], -V_TH, 4.0, ALU.add, ALU.mult))
            done(e.tensor_tensor(aux[:, 5:8], aux[:, 5:8], st[:, 7, :], ALU.subtract))
            src = m["brow"]
            e.tensor_copy(src[:, 0:1], aux[:, 7:8])
            done(e.tensor_copy(src[:, 1:2], cols[:, COL["bp"]:COL["bp"] + 1]))
            e.tensor_copy(parts[:, :, 0], src[:, :]).then_inc(pl, 1)
            e.wait_ge(pl, 3)
            e.tensor_tensor(rest[:, :, 0], src[:, :], parts[:, :, 0], ALU.subtract).then_inc(pl, 1)
            e.wait_ge(pl, 4)
            done(e.tensor_copy(parts[:, :, 1], rest[:, :, 0]))
            e.tensor_tensor(rest[:, :, 1], rest[:, :, 0], parts[:, :, 1], ALU.subtract).then_inc(pl, 1)
            e.wait_ge(pl, 5)
            done(e.tensor_copy(parts[:, :, 2], rest[:, :, 1]))
            e.wait_ge(mm, 3)
            done(e.tensor_copy(m["wvT"][:, :], TR[:, 0:P]))
            e.wait_ge(mm, 4)
            for k in range(TT):
                done(e.tensor_copy(m["vb3"][:, k, :], TB[0:3, 0:P]))
                done(e.tensor_copy(m["bp3"][:, k, :], TB[0:3, P:2 * P]))


def second_block(nc, t, m):
    with ExitStack() as ctx:
        sb = lambda n, s, d=F32: ctx.enter_context(nc.sbuf_tensor(n, s, d))
        sem = lambda n: ctx.enter_context(nc.semaphore(n))
        ps = lambda n, d=F32, w=CH: ctx.enter_context(nc.psum_tensor(n, [P, w], d))
        two = lambda n, s=(P, CH), d=F32: [sb(f"{n}{k}", list(s), d) for k in range(2)]
        QP, KP, VP, GM, MP, OP, X3, LG = (ps(n) for n in ("q_pre", "k2_pre", "v_pre", "vv_sum", "m_pre", "o_tok", "x3_ch", "logits"))
        CT = MP[:, :].bitcast(BF16)
        PT = 2 * TT
        x2s, q, k_, qk = two("x2_static"), two("q"), two("k"), two("qk")
        v = two("v_tok", (P, TT, D))
        vvm, mp = two("vv_masked", (P, BC, P)), two("m_mix", (P, BC, P))
        z, x3k, x3s = two("z_attn", (P, TT, D)), two("x3_tok", (P, TT, D)), two("x3_static")
        S = sb("scores", [P, NTOK // P, NE])
        sc = sb("biased", [P, PT, NE])
        hi2, lo2 = sb("pair_max", [P, PT * NE // 2]), sb("pair_min", [P, PT * NE // 2])
        g1, g2, g3 = (sb(n, [P, PT * NG]) for n in ("top1", "pair_max_min", "low_max"))
        gpad, grep = sb("group_padded", [P, PT, NG + TOPG]), sb("group_replaced", [P, PT, NG + TOPG])
        gm8 = sb("group_top", [P, PT, 8])
        gmask = sb("group_mask", [P, PT, NG])
        epad, erep = sb("expert_padded", [P, PT, NE + 2]), sb("expert_replaced", [P, PT, NE + 2])
        em8 = sb("expert_top", [P, PT, 8])
        w, wsum, wrec = sb("chosen", [P, PT, NE]), sb("chosen_sum", [P, PT]), sb("chosen_rec", [P, PT])
        cf, c1, c2 = sb("combine", [P, PT, NE]), sb("combine_rest1", [P, PT, NE]), sb("combine_rest2", [P, PT, NE])
        cs = sb("combine_parts", [P, PT, 3 * NE], BF16)
        n3 = Norm(ctx, nc, "norm3")
        A, aux = m["act"], m["aux"]
        tv = lambda ap: ap.rearrange("p (k c) -> p k c", k=TT)

        x2_in, x3_kept = [sem("x2_in0"), sem("x2_in1")], [sem("x3_kept0"), sem("x3_kept1")]
        q_mm, k_mm, v_mm, s_q, s_k, s_v, s_qk = (sem(n) for n in ("q_mm", "k2_mm", "v2_mm", "q_done", "k_done", "v_done", "qk_done"))
        vv_mm, s_vvm, m_mm, s_mp, o_mm, s_zz = (sem(n) for n in ("vv_mm", "vvm_done", "m_mm", "mp_done", "o_mm", "zz_done"))
        x3_turned, x3_static, lg_mm, s_S = (sem(n) for n in ("x3_turned", "x3_static_done", "logits_mm", "scores_done"))
        gate, rt, s_cf, pl, s_cs, c_turned, c_out, setup = (sem(n) for n in (
            "router_gate", "router_step", "combine_done", "parts_step", "parts_done", "combine_turned", "combine_out", "second_setup"))
        block = ctx.enter_context(nc.Block())

        @block.sync
        def _(e):
            def load(c, p):
                need(e, q_mm, c - 1)
                need(e, k_mm, c - 1)
                need(e, v_mm, c - 1)
                e.dma_start(x2s[p][:, :], A[:, bass.ds(c * CH, CH)]).then_inc(x2_in[p], 16)

            def keep(c, p):
                e.wait_ge(x3_static, c + 1)
                e.dma_start(A[:, bass.ds(c * CH, CH)], x3s[p][:, :]).then_inc(x3_kept[p], 16)

            pipeline(e, [(0, load), (3, keep)], NCH, 3)
            for s in x3_kept:
                e.wait_ge(s, 8 * NCH)

        @block.tensor
        def _(e):
            def logits(c, p):
                e.wait_ge(x3_static, c + 1)
                need(e, s_S, c)
                for k in range(TT):
                    last = e.matmul(LG[:, k * NE:(k + 1) * NE], x3s[p][:, k * P:(k + 1) * P], m["gateT"][:, :],
                                    start=True, stop=True)
                last.then_inc(lg_mm, 1)

            def gram(c, p):
                e.wait_ge(s_v, c + 1)
                need(e, s_vvm, c)
                for b in range(BC):
                    for k in range(2):
                        last = e.matmul(GM[:, b * P:(b + 1) * P], v[p][:, 2 * b + k, :], v[p][:, 2 * b + k, :],
                                        start=(k == 0), stop=(k == 1))
                last.then_inc(vv_mm, 1)

            def project(c, p):
                e.wait_ge(x2_in[p], 8 * (c - p) + 16)
                need(e, s_q, c)
                e.matmul(QP[:, :], m["sqT"][:, SQ.index("Wq"), :], x2s[p][:, :], start=True, stop=True).then_inc(q_mm, 1)
                need(e, s_k, c)
                e.matmul(KP[:, :], m["sqT"][:, SQ.index("Wk"), :], x2s[p][:, :], start=True, stop=True).then_inc(k_mm, 1)

            def mix(c, p):
                e.wait_ge(s_vvm, c + 1)
                need(e, s_mp, c)
                need(e, c_out, min(c - 7 + (1 - p), NCH) if isinstance(c, int) else c - 7 + (1 - p))
                for b in range(BC):
                    last = e.matmul(MP[:, b * P:(b + 1) * P], vvm[p][:, b, :], m["sqT"][:, SQ.index("Wp"), :],
                                    start=True, stop=True)
                last.then_inc(m_mm, 1)

            def project_v(c, p):
                need(e, s_v, c)
                e.matmul(VP[:, :], m["onesb"][:, :], m["vb3"][:, :, :].rearrange("p k c -> p (k c)"), start=True, stop=False)
                for k in range(TT):
                    last = e.matmul(VP[:, k * P:(k + 1) * P], x2s[p][:, k * P:(k + 1) * P], m["wvT"][:, :],
                                    start=False, stop=(k == TT - 1))
                last.then_inc(v_mm, 1)

            def attend(c, p):
                e.wait_ge(s_mp, c + 1)
                e.wait_ge(s_qk, c + 1)
                need(e, s_zz, c)
                e.matmul(OP[:, :], m["onesb"][:, :], m["bp3"][:, :, :].rearrange("p k c -> p (k c)"), start=True, stop=False)
                for k in range(TT):
                    last = e.matmul(OP[:, k * P:(k + 1) * P], qk[p][:, k * P:(k + 1) * P], mp[p][:, k // 2, :],
                                    start=False, stop=(k == TT - 1))
                last.then_inc(o_mm, 1)

            def turn_x3(c, p):
                e.wait_ge(n3.normed, TT * (c + 1))
                need(e, x3_static, c)
                for k in range(TT):
                    last = e.transpose(X3[:, k * P:(k + 1) * P], x3k[p][:, k, :], m["ident"][:, :])
                last.then_inc(x3_turned, 1)

            def turn_weights(c, p):
                if p == 0:
                    return
                e.wait_ge(s_cs, c + 1)
                need(e, c_out, c - 1)
                need(e, s_mp, min(c + 7, NCH) if isinstance(c, int) else c + 7)
                for k in range(PT):
                    last = e.transpose(CT[0:3 * NE, k * P:(k + 1) * P], cs[:, k, :], m["identb"][:, :])
                last.then_inc(c_turned, 2)

            pipeline(e, [(3, logits), (1, gram), (0, project), (1, mix), (0, project_v), (1, attend), (2, turn_x3),
                         (7, turn_weights)], NCH, 7)

        @block.scalar
        def _(e):
            def norm3(c, p):
                need(e, x3_turned, c - 1)
                n3.apply_act(e, c, p, x3k[p], z[p])

            def copy_weights(c, p):
                if p == 0:
                    return
                e.wait_ge(c_turned, c + 1)
                e.activation(m["cT"][:, bass.ds((c - 1) * CH, 2 * CH)], CT[0:3 * NE, 0:2 * CH], ACT.Copy).then_inc(c_out, 2)

            def scores(c, p):
                e.wait_ge(lg_mm, c + 1)
                e.activation(S[:, bass.ds(c * TT, TT), :], LG[:, 0:TT * NE].rearrange("p (k c) -> p k c", k=TT),
                             ACT.Sigmoid).then_inc(s_S, 1)

            def spikes(c, p):
                e.wait_ge(q_mm, c + 1)
                need(e, s_qk, c - 1)
                e.activation(q[p][:, :], QP[:, :], ACT.Sigmoid, bias=aux[:, 5:6], scale=aux[:, 2:3]).then_inc(s_q, 1)
                e.wait_ge(k_mm, c + 1)
                e.activation(k_[p][:, :], KP[:, :], ACT.Sigmoid, bias=aux[:, 6:7], scale=aux[:, 3:4]).then_inc(s_k, 1)

            def copy_m(c, p):
                e.wait_ge(m_mm, c + 1)
                need(e, o_mm, c - 1)
                e.activation(mp[p][:, :, :], MP[:, 0:BC * P].rearrange("p (b c) -> p b c", b=BC), ACT.Copy).then_inc(s_mp, 1)

            def spikes_v(c, p):
                e.wait_ge(v_mm, c + 1)
                need(e, vv_mm, c - 1)
                e.activation(v[p][:, :, :], tv(VP[:, :]), ACT.Sigmoid).then_inc(s_v, 1)

            def copy_x3(c, p):
                e.wait_ge(x3_turned, c + 1)
                need(e, lg_mm, c - 1)
                need(e, x3_kept[p], 8 * (c - p))
                e.activation(x3s[p][:, :], X3[:, :], ACT.Copy).then_inc(x3_static, 1)

            pipeline(e, [(8, copy_weights), (3, scores), (0, spikes), (1, copy_m), (2, norm3), (0, spikes_v),
                         (2, copy_x3)], NCH, 8)

        @block.gpsimd
        def _(e):
            n3.setup(e)
            PS = 4

            def parts(c, p):
                if p == 0:
                    return
                n = [0]

                def chain(ins):
                    ins.then_inc(pl, 2)
                    n[0] += 1
                    e.wait_ge(pl, PS * (c - 1) + 2 * n[0])

                e.wait_ge(s_cf, c + 1)
                need(e, c_turned, c - 1)
                chain(e.tensor_copy(cs[:, :, 0:NE], cf[:, :, :]))
                chain(e.tensor_tensor(c1[:, :, :], cf[:, :, :], cs[:, :, 0:NE], ALU.subtract))
                chain(e.tensor_copy(cs[:, :, NE:2 * NE], c1[:, :, :]))
                chain(e.tensor_tensor(c2[:, :, :], c1[:, :, :], cs[:, :, NE:2 * NE], ALU.subtract))
                assert n[0] == PS
                e.tensor_copy(cs[:, :, 2 * NE:3 * NE], c2[:, :, :]).then_inc(s_cs, 2)

            def product(c, p):
                e.wait_ge(s_q, c + 1)
                e.wait_ge(s_k, c + 1)
                need(e, o_mm, c - 1)
                e.tensor_tensor(qk[p][:, :], q[p][:, :], k_[p][:, :], ALU.mult).then_inc(s_qk, 1)

            def root(c, p):
                n3.root(e, c, p)
                n3.shift(e, c, p)

            pipeline(e, [(6, parts), (0, product), (1, root)], NCH, 6)

        @block.vector
        def _(e):
            e.memset(gpad[:, :, NG:], NEG).then_inc(setup, 1)
            e.memset(epad[:, :, NE:], NEG).then_inc(setup, 1)
            e.wait_ge(setup, 2)
            RT = 17
            R1 = 10

            def mask(c, p):
                e.wait_ge(vv_mm, c + 1)
                need(e, m_mm, c - 1)
                for b in range(BC):
                    last = e.scalar_tensor_tensor(out=vvm[p][:, b, :], in0=GM[:, b * P:(b + 1) * P],
                                                  scalar=float(HD) ** -0.5, in1=m["headmask"][:, :],
                                                  op0=ALU.mult, op1=ALU.mult)
                last.then_inc(s_vvm, 1)

            def residual(c, p):
                e.wait_ge(o_mm, c + 1)
                need(e, n3.normed, TT * (c - 1))
                e.tensor_tensor(z[p][:, :, :], tv(OP[:, :]), m["tok"][:, bass.ds(c * TT, TT), :], ALU.add).then_inc(s_zz, 1)
                e.wait_ge(s_zz, c + 1)
                n3.stats(e, c, p, z[p])

            def chainer(c, start):
                n = [start]

                def chain(ins, fixed=False):
                    ins.then_inc(rt, 2)
                    n[0] += 1
                    e.wait_ge(rt, RT * (c - 1) + 2 * n[0])
                    if fixed:
                        e.sem_inc(gate, 1)
                return chain, n

            def groups(c, p):
                if p == 0:
                    return
                chain, n = chainer(c, 0)
                e.wait_ge(s_S, c + 1)
                chain(e.tensor_tensor(sc[:, :, :], S[:, bass.ds((c - 1) * TT, PT), :],
                                      m["ebias"][:, :].rearrange("p (a c) -> p a c", a=1).broadcast_to([P, PT, NE]), ALU.add))
                pair = sc[:, :, :].rearrange("p k (g two) -> p (k g) two", two=2)
                e.tensor_tensor(hi2[:, :], pair[:, :, 0], pair[:, :, 1], ALU.max)
                chain(e.tensor_tensor(lo2[:, :], pair[:, :, 0], pair[:, :, 1], ALU.min))
                ph = hi2[:, :].rearrange("p (g two) -> p g two", two=2)
                pl_ = lo2[:, :].rearrange("p (g two) -> p g two", two=2)
                e.tensor_tensor(g1[:, :], ph[:, :, 0], ph[:, :, 1], ALU.max)
                e.tensor_tensor(g2[:, :], ph[:, :, 0], ph[:, :, 1], ALU.min)
                chain(e.tensor_tensor(g3[:, :], pl_[:, :, 0], pl_[:, :, 1], ALU.max))
                chain(e.tensor_tensor(g2[:, :], g2[:, :], g3[:, :], ALU.max))
                chain(e.tensor_tensor(gpad[:, :, 0:NG], g1[:, :].rearrange("p (k g) -> p k g", k=PT),
                                      g2[:, :].rearrange("p (k g) -> p k g", k=PT), ALU.add), fixed=True)
                for k in range(PT):
                    last = e.max(gm8[:, k, :], gpad[:, k, 0:NG])
                chain(last)
                chain(e.memset(gm8[:, :, TOPG:8], NEG), fixed=True)
                for k in range(PT):
                    last = e.match_replace(grep[:, k, :], gm8[:, k, :], gpad[:, k, :], TAKEN)
                chain(last)
                chain(e.tensor_scalar(gmask[:, :, :], grep[:, :, 0:NG], TAKEN, None, ALU.is_equal))
                chain(e.tensor_tensor(epad[:, :, 0:NE].rearrange("p k (g x) -> p k g x", g=NG),
                                      sc[:, :, :].rearrange("p k (g x) -> p k g x", g=NG),
                                      gmask[:, :, :].rearrange("p k (g x) -> p k g x", x=1).broadcast_to([P, PT, NG, GE]), ALU.mult))
                assert n[0] == R1

            def choose(c, p):
                if p == 0:
                    return
                chain, n = chainer(c, R1)
                e.wait_ge(rt, RT * (c - 1) + 2 * R1)
                e.sem_inc(gate, 1)
                for k in range(PT):
                    last = e.max(em8[:, k, :], epad[:, k, 0:NE])
                chain(last)
                chain(e.memset(em8[:, :, TOPK:8], NEG), fixed=True)
                for k in range(PT):
                    last = e.match_replace(erep[:, k, :], em8[:, k, :], epad[:, k, :], TAKEN)
                chain(last)
                chain(e.scalar_tensor_tensor(out=w[:, :, :], in0=erep[:, :, 0:NE], scalar=TAKEN,
                                             in1=S[:, bass.ds((c - 1) * TT, PT), :], op0=ALU.is_equal, op1=ALU.mult))
                chain(e.tensor_reduce(wsum[:, :], w[:, :, :], AX.X, ALU.add))
                chain(e.tensor_scalar(wsum[:, :], wsum[:, :], 1e-20, 1.0 / ROUTED_SCALE, ALU.add, ALU.mult))
                chain(e.reciprocal(wrec[:, :], wsum[:, :]))
                assert n[0] == RT
                need(e, s_cs, c - 1)
                e.tensor_tensor(cf[:, :, :], w[:, :, :],
                                wrec[:, :].rearrange("p (k x) -> p k x", x=1).broadcast_to([P, PT, NE]),
                                ALU.mult).then_inc(s_cf, 2)

            pipeline(e, [(1, mask), (4, groups), (5, choose), (1, residual)], NCH, 5)


def experts_block(nc, t, m, out):
    with ExitStack() as ctx:
        sb = lambda n, s, d=F32: ctx.enter_context(nc.sbuf_tensor(n, s, d))
        sem = lambda n: ctx.enter_context(nc.semaphore(n))
        ps = lambda n: ctx.enter_context(nc.psum_tensor(n, [P, CH], F32))
        U, C, O = [ps(f"up{k}") for k in range(3)], [ps(f"weight{k}") for k in range(2)], [ps(f"down{k}") for k in range(2)]
        TK = ps("out_tok")
        NR = 3
        r, tt, h = ([sb(f"{n}{k}", [P, CH]) for k in range(NR)] for n in ("relu", "relu_w", "hid"))
        hh, hl = ([sb(f"{n}{k}", [P, CH], F32R) for k in range(NR)] for n in ("hid_hi", "hid_lo"))
        xh, xl = ([sb(f"{n}{k}", [P, CH], F32R) for k in range(2)] for n in ("x3_hi", "x3_lo"))
        oT = [sb(f"outT{k}", [P, CH]) for k in range(2)]
        x4 = [sb(f"x4_tok{k}", [P, TT, D]) for k in range(2)]
        n4 = Norm(ctx, nc, "norm4")
        s_xh, s_xl, u_mm, c_mm, s_r, s_t, s_h, s_hh, s_hl, d_mm, o_mm, s_o, o_turned = (
            sem(n) for n in ("x_hi_done", "x_lo_done", "up_mm", "weight_mm", "relu_done", "relu_w_done", "hid_done",
                             "hid_hi_done", "hid_lo_done", "down_mm", "out_mm", "out_copied", "out_turned"))
        stored = [sem("x4_stored0"), sem("x4_stored1")]
        A = m["act"]
        tv = lambda ap: ap.rearrange("p (k c) -> p k c", k=TT)
        of = out.rearrange("b t c -> (b t) c")
        LAG, SLAG = 4, 2
        WL = 7
        block = ctx.enter_context(nc.Block())

        def chunks(eng, body, tail):
            body(0, 0)
            body(1, 1)
            with eng.Fori(1, NCH // 2 - 1) as i:
                body(2 * i, 0)
                body(2 * i + 1, 1)
            body(NCH - 2, 0)
            body(NCH - 1, 1)
            tail()

        @block.tensor
        def _(e):
            def up(c, p, j):
                g = c * NB + j
                if j == 0:
                    e.wait_ge(s_xl, c + 1)
                need(e, s_r, g - 2)
                uk = U[j % 3]
                e.matmul(uk[:, :], m["up_hi"][:, j, :], xh[p][:, :], start=True, stop=False)
                e.matmul(uk[:, :], m["up_hi"][:, j, :], xl[p][:, :], start=False, stop=False)
                e.matmul(uk[:, :], m["up_lo"][:, j, :], xh[p][:, :], start=False, stop=True).then_inc(u_mm, 1)
                if j < NRB:
                    need(e, s_t, c * NRB + j - 1)
                    e.matmul(C[j % 2][:, :], m["sel"][:, j, :], m["cT"][:, bass.ds(c * CH, CH)],
                             start=True, stop=True).then_inc(c_mm, 1)

            def down(c, p, j):
                g = c * NB + j
                if j == 0:
                    need(e, s_o, c - 1)
                    e.matmul(O[p][:, :], m["identr"][:, :], xh[p][:, :], start=True, stop=False)
                    e.matmul(O[p][:, :], m["identr"][:, :], xl[p][:, :], start=False, stop=False)
                e.wait_ge(s_hh, g + 1)
                e.matmul(O[p][:, :], m["dn_hi"][:, j, :], hh[j % NR][:, :], start=False, stop=False)
                e.matmul(O[p][:, :], m["dn_lo"][:, j, :], hh[j % NR][:, :], start=False, stop=False)
                e.wait_ge(s_hl, g + 1)
                last = e.matmul(O[p][:, :], m["dn_hi"][:, j, :], hl[j % NR][:, :], start=False, stop=(j == NB - 1))
                last.then_inc(d_mm, 1)

            def turn(c, p):
                e.wait_ge(s_o, c + 1)
                need(e, n4.normed, TT * c)
                for k in range(TT):
                    last = e.transpose(TK[:, k * P:(k + 1) * P], oT[p][:, k * P:(k + 1) * P], m["ident"][:, :])
                last.then_inc(o_turned, 1)

            def body(c, p):
                for j in range(NB):
                    up(c, p, j)
                    if j >= LAG:
                        down(c, p, j - LAG)
                    elif not (isinstance(c, int) and c == 0):
                        down(c - 1, 1 - p, NB - LAG + j)
                    if j == WL and not (isinstance(c, int) and c == 0):
                        turn(c - 1, 1 - p)

            def tail():
                for j in range(LAG):
                    down(NCH - 1, 1, NB - LAG + j)
                turn(NCH - 1, 1)
            chunks(e, body, tail)

        @block.scalar
        def _(e):
            def split(c, p):
                need(e, d_mm, NB * (c - 2 + 1))
                e.activation(xh[p][:, :], A[:, bass.ds(c * CH, CH)], ACT.Copy).then_inc(s_xh, 1)

            def relu(c, j):
                g = c * NB + j
                e.wait_ge(u_mm, g + 1)
                need(e, s_h, g - NR + 1)
                e.activation(r[j % NR][:, :], U[j % 3][:, :], ACT.Relu).then_inc(s_r, 1)

            def hi(c, j):
                g = c * NB + j
                e.wait_ge(s_h, g + 1)
                need(e, d_mm, g - NR + 1)
                e.activation(hh[j % NR][:, :], h[j % NR][:, :], ACT.Copy).then_inc(s_hh, 1)

            def outc(c, p):
                e.wait_ge(d_mm, NB * (c + 1))
                need(e, o_turned, c)
                e.activation(oT[p][:, :], O[p][:, :], ACT.Copy).then_inc(s_o, 1)

            def norm(c, p):
                e.wait_ge(stored[p], 8 * (c - p) + 16)
                n4.apply_act(e, c, p, x4[p], tv(TK[:, :]))

            def body(c, p):
                first = isinstance(c, int) and c == 0
                if first:
                    split(0, 0)
                for j in range(NB):
                    relu(c, j)
                    if j >= SLAG:
                        hi(c, j - SLAG)
                    elif not first:
                        hi(c - 1, NB - SLAG + j)
                    if j == LAG and not first:
                        outc(c - 1, 1 - p)
                    if j == WL + 5 and not first:
                        norm(c - 1, 1 - p)
                    if j == 9 and not (isinstance(c, int) and c == NCH - 1):
                        split(c + 1, 1 - p)

            def tail():
                for j in range(SLAG):
                    hi(NCH - 1, NB - SLAG + j)
                outc(NCH - 1, 1)
                norm(NCH - 1, 1)
            chunks(e, body, tail)

        @block.vector
        def _(e):
            def weigh(c, j):
                if j >= NRB:
                    return
                e.wait_ge(s_r, c * NB + j + 1)
                e.wait_ge(c_mm, c * NRB + j + 1)
                need(e, s_h, c * NB + j - NR + 1)
                e.tensor_tensor(tt[j % NR][:, :], C[j % 2][:, :], r[j % NR][:, :], ALU.mult).then_inc(s_t, 1)

            def lo(c, j):
                g = c * NB + j
                e.wait_ge(s_hh, g + 1)
                need(e, d_mm, g - NR + 1)
                e.tensor_tensor(hl[j % NR][:, :], h[j % NR][:, :], hh[j % NR][:, :].bitcast(F32), ALU.subtract).then_inc(s_hl, 1)

            def split(c, p):
                e.wait_ge(s_xh, c + 1)
                e.tensor_tensor(xl[p][:, :], A[:, bass.ds(c * CH, CH)], xh[p][:, :].bitcast(F32), ALU.subtract).then_inc(s_xl, 1)

            def norm(c, p):
                e.wait_ge(o_turned, c + 1)
                n4.stats(e, c, p, tv(TK[:, :]))

            def body(c, p):
                first = isinstance(c, int) and c == 0
                if first:
                    split(0, 0)
                for j in range(NB):
                    weigh(c, j)
                    if j >= SLAG:
                        lo(c, j - SLAG)
                    elif not first:
                        lo(c - 1, NB - SLAG + j)
                    if j == WL + 1 and not first:
                        norm(c - 1, 1 - p)
                    if j == 11 and not (isinstance(c, int) and c == NCH - 1):
                        split(c + 1, 1 - p)

            def tail():
                for j in range(SLAG):
                    lo(NCH - 1, NB - SLAG + j)
                norm(NCH - 1, 1)
            chunks(e, body, tail)

        @block.gpsimd
        def _(e):
            n4.setup(e)

            def square(c, j):
                g = c * NB + j
                e.wait_ge(s_r, g + 1)
                need(e, s_hl, g - NR + 1)
                if j < NRB:
                    e.wait_ge(s_t, c * NRB + j + 1)
                    e.tensor_tensor(h[j % NR][:, :], tt[j % NR][:, :], r[j % NR][:, :], ALU.mult).then_inc(s_h, 1)
                else:
                    e.tensor_tensor(h[j % NR][:, :], r[j % NR][:, :], r[j % NR][:, :], ALU.mult).then_inc(s_h, 1)

            def body(c, p):
                first = isinstance(c, int) and c == 0
                for j in range(NB):
                    square(c, j)
                    if j == WL + 1 and not first:
                        n4.root(e, c - 1, 1 - p)
                        n4.shift(e, c - 1, 1 - p)

            def tail():
                n4.root(e, NCH - 1, 1)
                n4.shift(e, NCH - 1, 1)
            chunks(e, body, tail)

        @block.sync
        def _(e):
            def store(c, p):
                e.wait_ge(n4.normed, TT * (c + 1))
                e.dma_start(of[bass.ds(c * CH, CH), :].rearrange("(k p) c -> p k c", p=P), x4[p][:, :, :]).then_inc(stored[p], 16)
            for s in stored:
                e.sem_inc(s, 16)
            chunks(e, store, lambda: [e.wait_ge(s, 8 * NCH + 16) for s in stored])


_INS = {
    "L0_attn_x": "x", "L0_attn_A": "A", "L0_attn_Wb": "Wb", "L0_attn_bb": "bb", "L0_attn_Wc": "Wc", "L0_attn_bc": "bc",
    "L0_attn_Wd": "Wd", "L0_attn_bd": "bd", "L0_attn_Wdelta": "Wdelta", "L0_attn_bdelta": "bdelta",
    "L0_ffn_W_r": "W_r", "L0_ffn_W_k": "W_k", "L0_ffn_W_v": "W_v", "L0_ffn_mu_r": "mu_r", "L0_ffn_mu_k": "mu_k",
    "L1_attn_Wq": "Wq", "L1_attn_gq": "gq", "L1_attn_bq": "bq", "L1_attn_Wk": "Wk", "L1_attn_gk": "gk",
    "L1_attn_bk": "bk", "L1_attn_Wv": "Wv", "L1_attn_gv": "gv", "L1_attn_bv": "bv", "L1_attn_Wp": "Wp",
    "L1_attn_bp": "bp", "L1_ffn_gate_w": "gate_w", "L1_ffn_e_bias": "e_bias", "L1_ffn_up_w": "up_w",
    "L1_ffn_down_w": "down_w", "L1_ffn_shared_up_w": "shared_up_w", "L1_ffn_shared_down_w": "shared_down_w",
}


def kernel(**inputs):
    import numpy as _np
    import concourse.bacc as _bacc
    from concourse import mybir as _mybir
    from concourse.bass_utils import run_bass_kernel_spmd as _run

    nc = _bacc.Bacc("TRN2", target_bir_lowering=False, num_devices=1)
    arrays, args = {}, {}
    for name, short in _INS.items():
        a = _np.ascontiguousarray(inputs[name])
        arrays[f"in_{name}_dram"] = a
        args[short] = nc.dram_tensor(f"in_{name}_dram", a.shape, _mybir.dt.from_np(a.dtype), kind="ExternalInput").ap()
    out = nc.dram_tensor("out_0_dram", (B, T, D), _mybir.dt.float32, kind="ExternalOutput").ap()
    build(nc, args, out)
    r = _run(nc, [arrays], core_ids=[0])
    return r.results[0]["out_0_dram"]
```

```python
from contextlib import ExitStack

import numpy as np
import concourse.bass as bass
from concourse import mybir

F32 = mybir.dt.float32
F32R = mybir.dt.float32r
BF16 = mybir.dt.bfloat16
ALU = mybir.AluOpType
ACT = mybir.ActivationFunctionType
AX = mybir.AxisListType

P = 128
B, T, D = 32, 256, 128
NTOK = B * T
CH = 512
NCH = NTOK // CH
TT = CH // P
BC = CH // T
HID = 32
NE, INTER, SHARED = 32, 64, 256
NG, GE = 8, 4
TOPG, TOPK = 4, 6
ROUTED_SCALE = 2.5
NRB = NE * INTER // P
NB = NRB + SHARED // P
EPS = 1e-5
NEG = -3.0e38
TAKEN = 3.0e38
HD = 8
V_TH = 1.0
LATE = 2

ROWS = ["bc", "bd", "mu_r", "mu_k", "gq", "bq", "gk", "bk", "gv", "bv"]
COL = {n: i for i, n in enumerate(ROWS)}
SQ = ["W_r", "W_k", "W_v", "Wq", "Wk", "Wv", "Wp"]


def need(eng, sem, n):
    if isinstance(n, int) and n <= 0:
        return
    eng.wait_ge(sem, n)


def pipeline(eng, stages, n, depth):
    first = depth + 2 + depth % 2
    last = n - n % 2

    def step(s, parity):
        for delay, fn in stages:
            c = s - delay
            if isinstance(s, int) and not 0 <= c < n:
                continue
            fn(c, (parity - delay) % 2)

    for s in range(first):
        step(s, s % 2)
    with eng.Fori(first // 2, last // 2) as i:
        for parity in (0, 1):
            step(2 * i + parity, parity)
    for s in range(last, n + depth):
        step(s, s % 2)


def build(nc, t, out):
    with ExitStack() as ctx:
        def sb(name, shape, dt=F32):
            return ctx.enter_context(nc.sbuf_tensor(name, shape, dt))

        m = {}
        m["act"] = sb("act_ch", [P, NTOK])
        m["tok"] = sb("x2_tok", [P, NTOK // P, D])
        m["hT"] = sb("scan_h", [P, NTOK // 4])
        m["cT"] = sb("combine_ch", [3 * NE, NTOK], BF16)
        for n in ("up_hi", "up_lo", "dn_hi", "dn_lo"):
            m[n] = sb(n, [P, NB, P], F32R)
        m["sqT"] = sb("square_T", [P, len(SQ), P])
        m["wv_nat"] = sb("wv_natural", [P, P])
        m["wdI"] = sb("wd_plus_identity", [P, P])
        m["wc_pad"] = sb("wc_padded", [P, 4, P])
        m["gateT"] = sb("gate_T", [P, NE])
        m["ebias"] = sb("e_bias_rows", [P, NE])
        m["bp"] = sb("bp_rows", [P, P])
        m["cols"] = sb("channel_columns", [P, len(ROWS)])
        m["aux"] = sb("derived_columns", [P, 16])
        m["ident"] = sb("identity", [P, P])
        m["identb"] = sb("identity_bf16", [P, P], BF16)
        m["ones"] = sb("ones", [P, P])
        m["onesb"] = sb("ones_bf16", [3, P], BF16)
        m["headmask"] = sb("head_mask", [P, P])
        m["sel"] = sb("expert_select", [3 * NE, NRB, P], BF16)
        m["gram"] = sb("gram", [P, P + 1])
        m["wvT"] = sb("wv_scaled_T", [P, P])
        m["vb3"] = sb("v_bias_rows", [3, TT, P], BF16)

        scan_block(nc, t, m)
        first_block(nc, t, m)
        R = Router(ctx, nc, m)
        second_block(nc, t, m, R)
        experts_block(nc, t, m, R, out)


def scan_block(nc, t, m):
    with ExitStack() as ctx:
        sb = lambda n, s, d=F32: ctx.enter_context(nc.sbuf_tensor(n, s, d))
        sem = lambda n: ctx.enter_context(nc.semaphore(n))
        ps = lambda n: ctx.enter_context(nc.psum_tensor(n, [P, 512], F32))
        NI = 4
        GT = 4 * T
        xin = [sb(f"x_in{k}", [P, GT // P, D]) for k in range(2)]
        PT = [ps(f"xT{k}") for k in range(4)]
        PD, PB = ps("delta_pre"), ps("b_pre")
        bank = [ps(f"weights_turned{k}") for k in range(2)]
        absd, expd, lnd, pos, delta = (sb(n, [P, 512]) for n in ("absd", "expd", "lnd", "posd", "delta"))
        alog, cum = sb("a_bar_log", [P, 512]), sb("cum", [P, 512])
        clip = sb("cum_clipped", [P, 2, T + 1])
        en, ep, bbar, bsh, bcum = (sb(n, [P, 512]) for n in ("exp_neg", "exp_pos", "b_bar", "b_shift", "b_cum"))
        ones = sb("ones_scan", [P, T])
        acol = sb("a_columns", [P, 4])
        wdelta_pad, wb_pad = sb("wdelta_padded", [P, 4, P + HID]), sb("wb_padded", [P, 4, P + HID])
        window = lambda w, k: w[:, :, :].rearrange("p k c -> p (k c)")[:, P * k:P * (k + 1)]
        later = m["tok"]
        up_raw, dn_raw = later[:, 0:NB, :], later[:, NB:2 * NB, :]
        wide = later[0:3 * NE, 2 * NB:2 * NB + NRB, :].rearrange("p a c -> p (a c)")
        sq_raw = sb("square_raw", [P, len(SQ), P])
        gate_raw = sb("gate_raw", [NE, P])
        scan_rows, rows = sb("scan_rows", [3, P]), sb("vector_rows", [len(ROWS), P])
        eb_row, bp_row = sb("e_bias_row", [1, NE]), sb("bp_row", [1, P])

        x_in = [sem("x_in_0"), sem("x_in_1")]
        xt, xe_act, xe_dve, db = sem("x_turned"), sem("x_evac_act"), sem("x_evac_dve"), sem("delta_b_ready")
        s_abs, s_exp, s_ln, s_pos, s_delta = sem("abs_done"), sem("exp_done"), sem("ln_done"), sem("pos_done"), sem("delta_done")
        s_alog, s_cum, s_clip, s_en, s_ep = sem("alog_done"), sem("cum_done"), sem("clip_done"), sem("exp_neg_done"), sem("exp_pos_done")
        s_bbar, s_bsh, s_bcum, s_h, setup = sem("bbar_done"), sem("bshift_done"), sem("bcum_done"), sem("h_done"), sem("scan_setup")
        s_a, a_ready = sem("a_softplus"), sem("a_columns_done")
        zero_done, ident_done, masks = sem("zero_done"), sem("ident_done"), sem("masks_step")
        scan_in, row_in, sq_in, wd_in, up_in, dn_in = (sem(n) for n in ("scan_weights_in", "rows_in", "square_in", "wd_in", "up_in", "down_in"))
        turned, evac_act, evac_dve, cols_done, fixed = (sem(n) for n in ("weights_turned", "weights_hi", "weights_lo", "scan_columns_done", "wd_identity"))
        xf = t["x"].rearrange("b t c -> (b t) c")
        A, hT = m["act"], m["hT"]
        scol = sb("scan_columns", [P, 3])
        row = lambda name: t[name].rearrange("(a c) -> a c", a=1)

        jobs = [("small", 0, 1)]
        jobs += [(kind, a, min(4, n - a)) for kind, n in (("sq", len(SQ)), ("up", NB), ("dn", NB)) for a in range(0, n, 4)]
        split_at = [sum(k in ("up", "dn") for k, _, _ in jobs[:g + 1]) for g in range(len(jobs))]

        def steps(order):
            left = list(range(len(jobs)))
            for s in range(NI + 2):
                for delay, fn in order:
                    if delay == "jobs":
                        for _ in range(2 if s >= 2 else 0):
                            if left:
                                g = left.pop(0)
                                fn(g, *jobs[g])
                    elif 0 <= s - delay < NI:
                        fn(s - delay)
            assert not left

        block = ctx.enter_context(nc.Block())

        @block.sync
        def _(e):
            def load(i, k):
                need(e, xt, 4 * (i - 1) + 2 * k + 2)
                src = xf[(2 * i + k) * GT:(2 * i + k + 1) * GT, :].rearrange("(a p) c -> p a c", p=P)
                e.dma_start(xin[k][:, :, :], src).then_inc(x_in[k], 16)

            load(0, 0)
            load(0, 1)
            e.wait_ge(zero_done, 2)
            for w, name in ((wdelta_pad, "Wdelta"), (wb_pad, "Wb")):
                e.dma_start(w[:, :, 0:HID], t[name].rearrange("p (k c) -> p k c", k=1).broadcast_to([P, 4, HID])).then_inc(scan_in, 16)
            load(1, 0)
            load(1, 1)
            e.dma_start(eb_row[:, :], row("e_bias")).then_inc(row_in, 16)
            e.dma_start(bp_row[:, :], row("bp")).then_inc(row_in, 16)
            e.dma_start(gate_raw[:, :], t["gate_w"]).then_inc(row_in, 16)
            for name in ROWS:
                e.dma_start(rows[COL[name]:COL[name] + 1, :], row(name)).then_inc(row_in, 16)
            for i, name in enumerate(SQ):
                e.dma_start(sq_raw[:, i, :], t[name]).then_inc(sq_in, 16)
            e.dma_start(up_raw[:, 0:NRB, :], t["up_w"].rearrange("(j e) i h -> (e i) j h", e=2)).then_inc(up_in, 16)
            e.dma_start(up_raw[:, NRB:NB, :], t["shared_up_w"].rearrange("(j p) h -> p j h", p=P)).then_inc(up_in, 16)
            load(2, 0)
            load(2, 1)
            for ee in range(2):
                e.dma_start(dn_raw[:, 0:NRB, INTER * ee:INTER * (ee + 1)],
                            t["down_w"].rearrange("(j e) h i -> e h j i", e=2)[ee]).then_inc(dn_in, 16)
            e.dma_start(dn_raw[:, NRB:NB, :], t["shared_down_w"].rearrange("h (j p) -> h j p", p=P)).then_inc(dn_in, 16)
            load(3, 0)
            load(3, 1)
            e.dma_start(m["wdI"][:, :], t["Wd"]).then_inc(wd_in, 16)
            e.dma_start(m["wv_nat"][:, :], t["Wv"]).then_inc(wd_in, 16)
            e.wait_ge(zero_done, 3)
            for k in range(4):
                e.dma_start(m["wc_pad"][HID * k:HID * (k + 1), k, :], t["Wc"]).then_inc(wd_in, 16)
            e.wait_ge(wd_in, 16 * 6)

        @block.scalar
        def _(e):
            for r, name in enumerate(("bdelta", "bb", "A")):
                e.dma_start(scan_rows[r:r + 1, :].rearrange("p (k c) -> p k c", k=4),
                            t[name].rearrange("(a k c) -> a k c", a=1, k=1).broadcast_to([1, 4, HID])).then_inc(scan_in, 16)

            def copy_x(i):
                for k in range(2):
                    e.wait_ge(xt, 4 * i + k + 1)
                    e.activation(A[:, 2 * i * GT + k * 512:2 * i * GT + (k + 1) * 512], PT[k][:, :], ACT.Copy).then_inc(xe_act, 1)

            def copy_later(i):
                if i > 0:
                    copy_x(i)

            def exponents(i):
                e.wait_ge(s_clip, i + 1)
                need(e, s_bsh, i)
                e.activation(en[:, :].rearrange("p (g t) -> p g t", g=2), clip[:, :, 0:T], ACT.Exp, scale=-1.0).then_inc(s_en, 1)
                need(e, s_h, i)
                e.activation(ep[:, :].rearrange("p (g t) -> p g t", g=2), clip[:, :, 1:T + 1], ACT.Exp).then_inc(s_ep, 1)

            def absolute(i):
                e.wait_ge(db, 2 * i + 1)
                e.activation(absd[:, :], PD[:, :], ACT.Abs, bias=scol[:, 0:1]).then_inc(s_abs, 1)

            def softplus(i):
                e.wait_ge(s_abs, i + 1)
                e.activation(expd[:, :], absd[:, :], ACT.Exp, scale=-1.0).then_inc(s_exp, 1)
                e.wait_ge(s_exp, i + 1)
                need(e, s_delta, i)
                e.activation(lnd[:, :], expd[:, :], ACT.Ln, bias=1.0).then_inc(s_ln, 1)

            def weights(g, kind, a, n):
                if kind in ("up", "dn"):
                    e.wait_ge(turned, g + 1)
                    e.activation(m[kind + "_hi"][:, a:a + n, :], bank[g % 2][:, 0:n * P].rearrange("p (a b) -> p a b", b=P),
                                 ACT.Copy).then_inc(evac_act, 1)

            copy_x(0)
            e.wait_ge(cols_done, 2)
            e.activation(acol[:, 0:1], scol[:, 2:3], ACT.Abs).then_inc(s_a, 1)
            e.wait_ge(s_a, 1)
            e.activation(acol[:, 1:2], acol[:, 0:1], ACT.Exp, scale=-1.0).then_inc(s_a, 1)
            e.wait_ge(s_a, 2)
            e.activation(acol[:, 2:3], acol[:, 1:2], ACT.Ln, bias=1.0).then_inc(s_a, 1)
            steps([("jobs", weights), (2, exponents), (1, absolute), ("jobs", weights), (1, softplus), (0, copy_later)])

        @block.gpsimd
        def _(e):
            e.memset(m["ident"][:, :], 0.0).then_inc(masks, 1)
            e.wait_ge(masks, 1)
            e.affine_select(out=m["ident"][:, :], in_=m["ident"][:, :], compare_op=ALU.not_equal, fill=1.0,
                            base=0, pattern=[[-1, P]], channel_multiplier=1).then_inc(ident_done, 1)
            e.memset(m["ones"][:, :], 1.0).then_inc(masks, 1)
            e.wait_ge(masks, 2)
            e.affine_select(out=m["headmask"][:, :].rearrange("p (a b) -> p a b", b=HD),
                            in_=m["ones"][:, :].rearrange("p (a b) -> p a b", b=HD),
                            compare_op=ALU.is_ge, fill=0.0, base=0, pattern=[[-HD, P // HD], [0, HD]],
                            channel_multiplier=1).then_inc(masks, 1)
            e.wait_ge(masks, 3)
            e.affine_select(out=m["headmask"][:, :].rearrange("p (a b) -> p a b", b=HD),
                            in_=m["headmask"][:, :].rearrange("p (a b) -> p a b", b=HD),
                            compare_op=ALU.is_ge, fill=0.0, base=HD - 1, pattern=[[HD, P // HD], [0, HD]],
                            channel_multiplier=-1).then_inc(masks, 1)
            e.memset(wide[:, :], 0.0).then_inc(masks, 1)
            for part in range(3):
                e.wait_ge(masks, 5 + part)
                w = wide[:, :].rearrange("p (j c) -> p j c", c=INTER)
                e.affine_select(out=w, in_=w, compare_op=ALU.not_equal, fill=1.0, base=-NE * part,
                                pattern=[[-1, NE], [0, INTER]], channel_multiplier=1).then_inc(masks, 1)

            def shifted(i):
                e.wait_ge(s_bbar, i + 1)
                e.wait_ge(s_en, i + 1)
                need(e, s_bcum, 2 * i)
                e.tensor_tensor(bsh[:, :], bbar[:, :], en[:, :], ALU.mult).then_inc(s_bsh, 1)
                e.wait_ge(s_bcum, 2 * i + 2)
                e.wait_ge(s_ep, i + 1)
                e.tensor_tensor(hT[:, i * 512:(i + 1) * 512], bcum[:, :], ep[:, :], ALU.mult).then_inc(s_h, 1)
            for i in range(NI):
                shifted(i)

        @block.tensor
        def _(e):
            def turn_x(i):
                for k in range(4):
                    if k % 2 == 0:
                        e.wait_ge(x_in[k // 2], 16 * (i + 1))
                    need(e, xe_act if k < 2 else xe_dve, 2 * (i - 1) + k % 2 + 1)
                    for a in range(4):
                        last = e.transpose(PT[k][:, a * P:(a + 1) * P], xin[k // 2][:, 4 * (k % 2) + a, :],
                                           m["ident"][:, :])
                    last.then_inc(xt, 1)

            def project(i, dst, w):
                for g in range(2):
                    for k in range(4):
                        at = (2 * i + g) * GT + k * T
                        last = e.matmul(dst[:, g * T:(g + 1) * T], window(w, k), A[:, at:at + T],
                                        start=(k == 0), stop=(k == 3))
                last.then_inc(db, 1)

            def delta(i):
                e.wait_ge(xe_act, 2 * (i + 1))
                e.wait_ge(xe_dve, 2 * (i + 1))
                need(e, s_pos, i)
                need(e, s_abs, i)
                project(i, PD, wdelta_pad)

            def b(i):
                need(e, s_bbar, i)
                project(i, PB, wb_pad)

            def weights(g, kind, a, n):
                if kind == "small":
                    e.wait_ge(row_in, 16 * (len(ROWS) + 3))
                    e.wait_ge(masks, 2)
                if kind in ("sq", "up", "dn"):
                    e.wait_ge(*{"sq": (sq_in, 16 * len(SQ)), "up": (up_in, 32), "dn": (dn_in, 48)}[kind])
                if g >= 2:
                    need(e, evac_act, split_at[g - 2])
                    need(e, evac_dve, g - 1)
                bk = bank[g % 2]
                if kind == "small":
                    e.transpose(bk[:, 0:len(ROWS)], rows[:, :], m["ident"][0:len(ROWS), 0:len(ROWS)])
                    e.transpose(bk[:, NE:2 * NE], gate_raw[:, :], m["ident"][0:NE, 0:NE])
                    e.matmul(bk[:, 2 * NE:3 * NE], m["ones"][0:1, :], eb_row[:, :], start=True, stop=True)
                    last = e.matmul(bk[:, P:2 * P], m["ones"][0:1, :], bp_row[:, :], start=True, stop=True)
                else:
                    raw = {"sq": sq_raw, "up": up_raw, "dn": dn_raw}[kind]
                    for k in range(n):
                        last = e.transpose(bk[:, k * P:(k + 1) * P], raw[:, a + k, :], m["ident"][:, :])
                last.then_inc(turned, 1)

            e.wait_ge(ident_done, 1)
            e.wait_ge(scan_in, 16 * 5)
            e.transpose(PD[:, 0:3], scan_rows[:, :], m["ident"][0:3, 0:3]).then_inc(cols_done, 1)
            e.wait_ge(cols_done, 2)
            steps([("jobs", weights), (1, delta), ("jobs", weights), (0, turn_x), (1, b)])

        @block.vector
        def _(e):
            e.memset(wdelta_pad[:, :, :], 0.0).then_inc(zero_done, 1)
            e.memset(wb_pad[:, :, :], 0.0).then_inc(zero_done, 1)
            e.memset(m["wc_pad"][:, :, :], 0.0).then_inc(zero_done, 1)
            e.memset(ones[:, :], 1.0).then_inc(setup, 1)
            e.memset(clip[:, :, 0:1], 0.0).then_inc(setup, 1)
            e.memset(m["onesb"][:, :], 1.0).then_inc(setup, 1)
            e.wait_ge(cols_done, 1)
            e.tensor_copy(scol[:, :], PD[:, 0:3]).then_inc(cols_done, 1)
            e.wait_ge(setup, 3)

            def copy_x(i):
                for k in range(2):
                    e.wait_ge(xt, 4 * i + k + 3)
                    at = 2 * i * GT + (k + 2) * 512
                    e.tensor_copy(A[:, at:at + 512], PT[2 + k][:, :]).then_inc(xe_dve, 1)

            def copy_later(i):
                if i > 0:
                    copy_x(i)

            def positive(i):
                e.wait_ge(s_abs, i + 1)
                e.tensor_scalar(pos[:, :], PD[:, :], scol[:, 0:1], 0.0, ALU.add, ALU.max).then_inc(s_pos, 1)

            def sums(i):
                e.wait_ge(s_pos, i + 1)
                e.wait_ge(s_ln, i + 1)
                e.tensor_tensor(delta[:, :], pos[:, :], lnd[:, :], ALU.add).then_inc(s_delta, 1)
                e.wait_ge(s_delta, i + 1)
                e.tensor_scalar(alog[:, :], delta[:, :], acol[:, 3:4], None, ALU.mult).then_inc(s_alog, 1)
                e.wait_ge(s_alog, i + 1)
                for g in range(2):
                    e.tensor_tensor_scan(cum[:, g * T:(g + 1) * T], ones[:, :], alog[:, g * T:(g + 1) * T], 0.0,
                                         ALU.mult, ALU.add).then_inc(s_cum, 1)
                e.wait_ge(db, 2 * i + 2)
                need(e, s_bsh, i)
                e.scalar_tensor_tensor(out=bbar[:, :], in0=PB[:, :], scalar=scol[:, 1:2], in1=delta[:, :],
                                       op0=ALU.add, op1=ALU.mult).then_inc(s_bbar, 1)
                e.wait_ge(s_cum, 2 * i + 2)
                need(e, s_en, i)
                need(e, s_ep, i)
                e.tensor_scalar(clip[:, :, 1:T + 1], cum[:, :].rearrange("p (g t) -> p g t", g=2), -20.0, 20.0,
                                ALU.max, ALU.min).then_inc(s_clip, 1)

            def second_sum(i):
                e.wait_ge(s_bsh, i + 1)
                need(e, s_h, i)
                for g in range(2):
                    e.tensor_tensor_scan(bcum[:, g * T:(g + 1) * T], ones[:, :], bsh[:, g * T:(g + 1) * T], 0.0,
                                         ALU.mult, ALU.add).then_inc(s_bcum, 1)

            def weights(g, kind, a, n):
                e.wait_ge(turned, g + 1)
                bk = bank[g % 2]
                bv = bk[:, 0:n * P].rearrange("p (a b) -> p a b", b=P)
                if kind == "small":
                    e.tensor_copy(m["cols"][:, :], bk[:, 0:len(ROWS)]).then_inc(fixed, 1)
                    e.tensor_copy(m["gateT"][:, :], bk[:, NE:2 * NE]).then_inc(fixed, 1)
                    e.tensor_copy(m["ebias"][:, :], bk[:, 2 * NE:3 * NE]).then_inc(fixed, 1)
                    ins = e.tensor_copy(m["bp"][:, :], bk[:, P:2 * P])
                elif kind == "sq":
                    ins = e.tensor_copy(m["sqT"][:, a:a + n, :], bv)
                else:
                    e.wait_ge(evac_act, split_at[g])
                    ins = e.tensor_tensor(m[kind + "_lo"][:, a:a + n, :], bv,
                                          m[kind + "_hi"][:, a:a + n, :].bitcast(F32), ALU.subtract)
                ins.then_inc(evac_dve, 1)

            copy_x(0)
            e.wait_ge(masks, 8)
            e.tensor_copy(m["sel"][:, :, :].rearrange("p j c -> p (j c)"), wide).then_inc(fixed, 1)
            e.tensor_copy(m["identb"][:, :], m["ident"][:, :]).then_inc(fixed, 1)
            e.wait_ge(s_a, 3)
            e.tensor_scalar(acol[:, 3:4], scol[:, 2:3], 0.0, None, ALU.max).then_inc(a_ready, 1)
            e.wait_ge(a_ready, 1)
            e.tensor_tensor(acol[:, 3:4], acol[:, 3:4], acol[:, 2:3], ALU.add).then_inc(a_ready, 1)
            e.wait_ge(a_ready, 2)
            e.tensor_scalar(acol[:, 3:4], acol[:, 3:4], -1.0, None, ALU.mult).then_inc(a_ready, 1)
            e.wait_ge(a_ready, 3)
            steps([("jobs", weights), (2, second_sum), (1, positive), ("jobs", weights), (0, copy_later), (1, sums)])
            e.wait_ge(wd_in, 16 * 6)
            e.tensor_tensor(m["wdI"][:, :], m["wdI"][:, :], m["ident"][:, :], ALU.add).then_inc(fixed, 1)
            e.wait_ge(fixed, 3)
            c = m["cols"]
            e.tensor_tensor(m["aux"][:, 0:1], c[:, COL["bc"]:COL["bc"] + 1], c[:, COL["bd"]:COL["bd"] + 1],
                            ALU.add).then_inc(fixed, 1)


class Norm:

    def __init__(self, ctx, nc, name):
        sb = lambda n, s: ctx.enter_context(nc.sbuf_tensor(f"{name}_{n}", s, F32))
        sem = lambda n: ctx.enter_context(nc.semaphore(f"{name}_{n}"))
        self.parts = [sb(f"parts{k}", [P, TT, 6]) for k in range(2)]
        self.mv = [sb(f"mv{k}", [P, TT, 2]) for k in range(2)]
        self.ve = [sb(f"ve{k}", [P, TT]) for k in range(2)]
        self.rstd = [sb(f"rstd{k}", [P, TT]) for k in range(2)]
        self.nm, self.nmr = ([sb(f"{n}{k}", [P, TT]) for k in range(2)] for n in ("minus_mean", "minus_mean_rstd"))
        self.power, self.eps, self.minus = sb("power", [P, TT]), sb("eps", [P, TT]), sb("minus_one", [P, TT])
        self.nm_done, self.nmr_done = sem("minus_mean_done"), sem("minus_mean_rstd_done")
        self.stats_done, self.mv_done = sem("stats_done"), sem("mv_done")
        self.ve_done, self.rstd_done, self.normed = sem("ve_done"), sem("rstd_done"), sem("normed")
        self.power_set, self.gate = sem("power_set"), sem("gate")

    def setup(self, pool):
        pool.memset(self.power[:, :], -0.5).then_inc(self.power_set, 1)
        pool.memset(self.eps[:, :], EPS).then_inc(self.power_set, 1)
        pool.memset(self.minus[:, :], -1.0).then_inc(self.power_set, 1)
        pool.wait_ge(self.power_set, 3)

    def stats(self, dve, c, par, src, tiles=range(TT)):
        for k in tiles:
            dve.bn_stats(self.parts[par][:, k, :], src[:, k, :]).then_inc(self.stats_done, 1)

    def aggregate(self, dve, c, par):
        dve.wait_ge(self.stats_done, TT * (c + 1))
        need(dve, self.normed, TT * c)
        dve.sem_inc(self.gate, 1)
        for k in range(TT):
            dve.bn_aggr(self.mv[par][:, k, :], self.parts[par][:, k, :]).then_inc(self.mv_done, 1)

    def root(self, pool, c, par):
        pool.wait_ge(self.mv_done, TT * (c + 1))
        pool.tensor_tensor(self.ve[par][:, :], self.mv[par][:, :, 1], self.eps[:, :], ALU.add).then_inc(self.ve_done, 1)
        pool.tensor_tensor(self.nm[par][:, :], self.mv[par][:, :, 0], self.minus[:, :], ALU.mult).then_inc(self.nm_done, 1)
        pool.wait_ge(self.ve_done, c + 1)
        need(pool, self.normed, TT * c)
        pool.tensor_tensor(self.rstd[par][:, :], self.ve[par][:, :], self.power[:, :], ALU.pow).then_inc(self.rstd_done, 1)

    def shift(self, pool, c, par):
        pool.wait_ge(self.nm_done, c + 1)
        pool.wait_ge(self.rstd_done, c + 1)
        pool.tensor_tensor(self.nmr[par][:, :], self.nm[par][:, :], self.rstd[par][:, :], ALU.mult).then_inc(self.nmr_done, 1)

    def apply_act(self, act, c, par, dst, src):
        act.wait_ge(self.nmr_done, c + 1)
        for k in range(TT):
            act.activation(dst[:, k, 0:D], src[:, k, :], ACT.Identity, bias=self.nmr[par][:, k:k + 1],
                           scale=self.rstd[par][:, k:k + 1]).then_inc(self.normed, 1)


def first_block(nc, t, m):
    with ExitStack() as ctx:
        sb = lambda n, s, d=F32: ctx.enter_context(nc.sbuf_tensor(n, s, d))
        sem = lambda n: ctx.enter_context(nc.semaphore(n))
        ps = lambda n: ctx.enter_context(nc.psum_tensor(n, [P, CH], F32))
        two = lambda n, s=(P, CH): [sb(f"{n}{k}", list(s)) for k in range(2)]
        YT, YK, X1, RP, KP, ZK, X2, GP = (ps(n) for n in ("y_ch", "y_tok", "x1_ch", "r_pre", "k_pre", "z_tok", "x2_ch", "gram_sum"))
        VP = RP
        yT, x1k = two("y_sb"), two("x1_tok", (P, TT, D))
        x1T = two("x1T", (P, BC, T + 1))
        diff, xr, xk, rr, kr, k2, vr, zT = (two(n) for n in ("diff", "xr", "xk", "r", "k_relu", "k_sq", "v_r", "zT"))
        x2k = two("x2_stage", (P, TT, D + 1))
        n1, n2 = Norm(ctx, nc, "norm1"), Norm(ctx, nc, "norm2")
        zrow = sb("zero_row", [1, P + 1])
        A, hT, aux, cols = m["act"], m["hT"], m["aux"], m["cols"]
        cc = lambda n: cols[:, COL[n]:COL[n] + 1]
        bv = lambda ap: ap.rearrange("p (b t) -> p b t", b=BC)
        tv = lambda ap: ap.rearrange("p (k c) -> p k c", k=TT)

        y_mm, y_sb, y_tok, x1_turned, x1_copied = sem("y_mm"), sem("y_sb_done"), sem("y_turned"), sem("x1_turned"), sem("x1_copied")
        s_diff, s_xr, s_xk, r_mm, k_mm = sem("diff_done"), sem("xr_done"), sem("xk_done"), sem("r_mm"), sem("k_mm")
        s_r, s_kr, s_k2, v_mm, s_vr, s_z = sem("r_done"), sem("krelu_done"), sem("ksq_done"), sem("v_mm"), sem("vr_done"), sem("z_done")
        z_turned, x2_turned, x2_copied, gram_mm, kept = sem("z_turned"), sem("x2_turned"), sem("x2_copied"), sem("gram_mm"), sem("x2_kept")
        setup, gram_out, zeroed = sem("first_setup"), sem("gram_out"), sem("gram_zeroed")
        block = ctx.enter_context(nc.Block())

        @block.tensor
        def _(e):
            e.wait_ge(setup, 5)
            e.matmul(GP[:, 0:P + 1], m["ones"][0:1, :], zrow[0:1, :], start=True, stop=False).then_inc(zeroed, 1)

            def attention(c, p):
                need(e, y_sb, c)
                e.matmul(YT[:, :], m["wdI"][:, :], A[:, bass.ds(c * CH, CH)], start=True, stop=False)
                for b in range(BC):
                    last = e.matmul(YT[:, b * T:(b + 1) * T], m["wc_pad"][:, BC * p + b, :],
                                    hT[:, bass.ds((c - p) * (T // 2), T)], start=False, stop=(b == BC - 1))
                last.then_inc(y_mm, 1)

            def value(c, p):
                e.wait_ge(s_k2, c + 1)
                e.wait_ge(s_r, c + 1)
                e.matmul(VP[:, :], m["sqT"][:, SQ.index("W_v"), :], k2[p][:, :], start=True, stop=True).then_inc(v_mm, 1)

            def receptance(c, p):
                e.wait_ge(s_xk, c + 1)
                need(e, s_kr, c)
                need(e, s_k2, c)
                e.matmul(KP[:, :], m["sqT"][:, SQ.index("W_k"), :], xk[p][:, :], start=True, stop=True).then_inc(k_mm, 1)
                e.wait_ge(s_xr, c + 1)
                need(e, s_vr, c)
                e.matmul(RP[:, :], m["sqT"][:, SQ.index("W_r"), :], xr[p][:, :], start=True, stop=True).then_inc(r_mm, 1)

            def turn_y(c, p):
                e.wait_ge(y_sb, c + 1)
                need(e, n1.normed, TT * c)
                for k in range(TT):
                    last = e.transpose(YK[:, k * P:(k + 1) * P], yT[p][:, k * P:(k + 1) * P], m["ident"][:, :])
                last.then_inc(y_tok, 1)

            def turn_z(c, p):
                e.wait_ge(s_z, c + 1)
                need(e, n2.normed, TT * c)
                for k in range(TT):
                    last = e.transpose(ZK[:, k * P:(k + 1) * P], zT[p][:, k * P:(k + 1) * P], m["ident"][:, :])
                last.then_inc(z_turned, 1)

            def turn_x1(c, p):
                e.wait_ge(n1.normed, TT * (c + 1))
                need(e, x1_copied, c)
                for k in range(TT):
                    last = e.transpose(X1[:, k * P:(k + 1) * P], x1k[p][:, k, :], m["ident"][:, :])
                last.then_inc(x1_turned, 1)

            def turn_x2(c, p):
                e.wait_ge(n2.normed, TT * (c + 1))
                need(e, x2_copied, c)
                for k in range(TT):
                    last = e.transpose(X2[:, k * P:(k + 1) * P], x2k[p][:, k, 0:D], m["ident"][:, :])
                last.then_inc(x2_turned, 1)
                for k in range(TT):
                    last = e.matmul(GP[:, 0:D + 1], x2k[p][:, k, 0:D], x2k[p][:, k, :], start=False,
                                    stop=False, skip_group_check=True)
                last.then_inc(gram_mm, 1)

            pipeline(e, [(0, attention), (4, turn_x2), (3, turn_z), (2, receptance), (0, turn_y), (1, turn_x1),
                         (2, value)], NCH, 4)
            e.matmul(GP[:, 0:P + 1], m["ones"][0:1, :], zrow[0:1, :], start=False, stop=True).then_inc(zeroed, 1)

        @block.scalar
        def _(e):
            def norm1(c, p):
                need(e, x1_turned, c - 1)
                n1.apply_act(e, c, p, x1k[p], tv(YK[:, :]))

            def copy_y(c, p):
                e.wait_ge(y_mm, c + 1)
                need(e, y_tok, c - 1)
                e.activation(yT[p][:, :], YT[:, :], ACT.Identity, bias=aux[:, 0:1]).then_inc(y_sb, 1)

            def norm2(c, p):
                need(e, x2_turned, c - 1)
                need(e, gram_mm, c - 1)
                need(e, kept, c - 1)
                n2.apply_act(e, c, p, x2k[p], tv(ZK[:, :]))

            def receptance(c, p):
                e.wait_ge(k_mm, c + 1)
                need(e, s_k2, c - 1)
                e.activation(kr[p][:, :], KP[:, :], ACT.Relu).then_inc(s_kr, 1)
                e.wait_ge(r_mm, c + 1)
                need(e, s_vr, c - 1)
                e.activation(rr[p][:, :], RP[:, :], ACT.Sigmoid).then_inc(s_r, 1)

            def copy_x1(c, p):
                e.wait_ge(x1_turned, c + 1)
                need(e, s_z, c - 1)
                need(e, s_xr, c - 1)
                need(e, s_xk, c - 1)
                e.activation(x1T[p][:, :, 1:T + 1], bv(X1[:, :]), ACT.Copy).then_inc(x1_copied, 1)

            def copy_x2(c, p):
                e.wait_ge(x2_turned, c + 1)
                e.activation(A[:, bass.ds(c * CH, CH)], X2[:, :], ACT.Copy).then_inc(x2_copied, 1)

            def copy_y_early(c, p):
                if isinstance(c, int) and c == 1:
                    copy_y(c, p)

            def copy_y_rest(c, p):
                if not (isinstance(c, int) and c == 1):
                    copy_y(c, p)

            pipeline(e, [(0, copy_y_early), (1, norm1), (0, copy_y_rest), (4, copy_x2), (2, receptance), (1, copy_x1), (3, norm2)], NCH, 4)

        @block.vector
        def _(e):
            e.memset(zrow[:, :], 0.0).then_inc(setup, 1)
            for k in range(2):
                e.memset(x1T[k][:, :, 0:1], 0.0).then_inc(setup, 1)
                e.memset(x2k[k][:, :, D:D + 1], 1.0).then_inc(setup, 1)

            def mix(c, p):
                e.wait_ge(x1_copied, c + 1)
                need(e, s_xr, c)
                e.tensor_tensor(bv(diff[p][:, :]), x1T[p][:, :, 1:T + 1], x1T[p][:, :, 0:T], ALU.subtract).then_inc(s_diff, 1)
                e.wait_ge(s_diff, c + 1)
                for mu, dst, done, used in (("mu_k", xk, s_xk, k_mm), ("mu_r", xr, s_xr, r_mm)):
                    need(e, used, c - 1)
                    e.scalar_tensor_tensor(out=bv(dst[p][:, :]), in0=bv(diff[p][:, :]), scalar=cc(mu),
                                           in1=x1T[p][:, :, 0:T], op0=ALU.mult, op1=ALU.add).then_inc(done, 1)

            def gate(c, p):
                e.wait_ge(v_mm, c + 1)
                e.wait_ge(s_r, c + 1)
                need(e, s_z, c - 1)
                e.tensor_tensor(vr[p][:, :], VP[:, :], rr[p][:, :], ALU.mult).then_inc(s_vr, 1)
                e.wait_ge(s_vr, c + 1)
                need(e, z_turned, c - 1)
                e.tensor_tensor(bv(zT[p][:, :]), bv(vr[p][:, :]), x1T[p][:, :, 1:T + 1], ALU.add).then_inc(s_z, 1)

            def square(c, p):
                e.wait_ge(s_kr, c + 1)
                need(e, v_mm, c - 1)
                e.scalar_tensor_tensor(out=k2[p][:, :], in0=KP[:, :], scalar=0.0, in1=kr[p][:, :],
                                       op0=ALU.max, op1=ALU.mult).then_inc(s_k2, 1)

            def stats1(c, p):
                e.wait_ge(y_tok, c + 1)
                n1.stats(e, c, p, tv(YK[:, :]))
                n1.aggregate(e, c, p)

            def stats2(c, p):
                e.wait_ge(z_turned, c + 1)
                n2.stats(e, c, p, tv(ZK[:, :]))
                n2.aggregate(e, c, p)

            pipeline(e, [(3, stats2), (2, square), (0, stats1), (2, gate), (1, mix)], NCH, 4)
            e.wait_ge(zeroed, 2)
            e.tensor_scalar(m["gram"][:, :], GP[:, 0:P + 1], 1.0 / NTOK, None, ALU.mult).then_inc(gram_out, 1)

        @block.gpsimd
        def _(e):
            n1.setup(e)
            n2.setup(e)
            e.wait_ge(setup, 5)

            def root1(c, p):
                n1.root(e, c, p)
                n1.shift(e, c, p)

            def root2(c, p):
                n2.root(e, c, p)
                n2.shift(e, c, p)

            def keep(c, p):
                e.wait_ge(n2.normed, TT * (c + 1))
                e.tensor_tensor(m["tok"][:, bass.ds(c * TT, TT), :], x2k[p][:, :, 0:D],
                                m["bp"][:, :].rearrange("p (k c) -> p k c", k=1).broadcast_to([P, TT, D]), ALU.add).then_inc(kept, 1)

            pipeline(e, [(3, root2), (0, root1), (4, keep)], NCH, 4)


class Router:
    PT = 2 * TT
    GA, GB, GC, CA, CB, RT = 5, 7, 9, 11, 13, 17

    def __init__(self, ctx, nc, m):
        sb = lambda n, s, d=F32: ctx.enter_context(nc.sbuf_tensor(n, s, d))
        sem = lambda n: ctx.enter_context(nc.semaphore(n))
        self.m, PT = m, self.PT
        self.S = sb("scores", [P, NTOK // P, NE])
        self.sc = sb("biased", [P, PT, NE])
        self.pmax, self.psum = sb("pair_max", [P, PT * NE // 2]), sb("pair_sum", [P, PT * NE // 2])
        self.across, self.within = (sb(n, [P, PT * NG]) for n in ("sum_across", "sum_within"))
        self.gpad, self.grep = sb("group_padded", [P, PT, NG + TOPG]), sb("group_replaced", [P, PT, NG + TOPG])
        self.gm8 = sb("group_top", [P, PT, 8])
        self.gmask = sb("group_mask", [P, PT, NG])
        self.epad, self.erep = sb("expert_padded", [P, PT, NE + 2]), sb("expert_replaced", [P, PT, NE + 2])
        self.em8 = sb("expert_top", [P, PT, 8])
        self.w, self.wsum, self.wrec = sb("chosen", [P, PT, NE]), sb("chosen_sum", [P, PT]), sb("chosen_rec", [P, PT])
        self.cf, self.c1, self.c2 = sb("combine", [P, PT, NE]), sb("combine_rest1", [P, PT, NE]), sb("combine_rest2", [P, PT, NE])
        self.cs = sb("combine_parts", [P, PT, 3 * NE], BF16)
        (self.s_S, self.gate, self.rt, self.s_rec, self.s_cf, self.s_p1, self.s_r1, self.s_p2, self.s_r2, self.s_cs,
         self.c_turned, self.c_out, self.setup) = (sem(n) for n in (
            "scores_done", "router_gate", "router_step", "reciprocal_done", "combine_done", "part1_done", "rest1_done",
            "part2_done", "rest2_done", "parts_done", "combine_turned", "combine_out", "router_setup"))

    def chained(self, e, c, k, fixed=False):
        e.wait_ge(self.rt, self.RT * (c - 1) + 2 * k)
        if fixed:
            e.sem_inc(self.gate, 1)

    def groups_scores(self, e, c):
        e.wait_ge(self.s_S, c + 1)
        e.tensor_tensor(self.sc[:, :, :], self.S[:, bass.ds((c - 1) * TT, self.PT), :],
                        self.m["ebias"][:, :].rearrange("p (a c) -> p a c", a=1).broadcast_to([P, self.PT, NE]), ALU.add).then_inc(self.rt, 2)
        pair = self.sc[:, :, :].rearrange("p k (g two) -> p (k g) two", two=2)
        self.chained(e, c, 1)
        e.tensor_tensor(self.pmax[:, :], pair[:, :, 0], pair[:, :, 1], ALU.max).then_inc(self.rt, 2)
        e.tensor_tensor(self.psum[:, :], pair[:, :, 0], pair[:, :, 1], ALU.add).then_inc(self.rt, 2)
        both = lambda ap: ap.rearrange("p (g two) -> p g two", two=2)
        self.chained(e, c, 2)
        e.tensor_tensor(self.across[:, :], both(self.pmax[:, :])[:, :, 0], both(self.pmax[:, :])[:, :, 1], ALU.add).then_inc(self.rt, 2)
        self.chained(e, c, 3)
        e.tensor_tensor(self.within[:, :], both(self.psum[:, :])[:, :, 0], both(self.psum[:, :])[:, :, 1], ALU.max).then_inc(self.rt, 2)

    def groups_top(self, e, c):
        self.chained(e, c, self.GA)
        e.tensor_tensor(self.gpad[:, :, 0:NG], self.across[:, :].rearrange("p (k g) -> p k g", k=self.PT),
                        self.within[:, :].rearrange("p (k g) -> p k g", k=self.PT), ALU.max).then_inc(self.rt, 2)
        self.chained(e, c, self.GA + 1, fixed=True)
        for k in range(self.PT):
            last = e.max(self.gm8[:, k, :], self.gpad[:, k, 0:NG])
        last.then_inc(self.rt, 2)
        assert self.GB == self.GA + 2

    def groups_found(self, e, c):
        self.chained(e, c, self.GB)
        e.memset(self.gm8[:, :, TOPG:8], NEG).then_inc(self.rt, 2)
        self.chained(e, c, self.GB + 1, fixed=True)
        for k in range(self.PT):
            last = e.match_replace(self.grep[:, k, :], self.gm8[:, k, :], self.gpad[:, k, :], TAKEN)
        last.then_inc(self.rt, 2)
        assert self.GC == self.GB + 2
        self.chained(e, c, self.GC)
        e.tensor_scalar(self.gmask[:, :, :], self.grep[:, :, 0:NG], TAKEN, None, ALU.is_equal).then_inc(self.rt, 2)

    def groups_kept(self, e, c):
        self.chained(e, c, self.GC + 1)
        e.tensor_tensor(self.epad[:, :, 0:NE].rearrange("p k (g x) -> p k g x", g=NG),
                        self.sc[:, :, :].rearrange("p k (g x) -> p k g x", g=NG),
                        self.gmask[:, :, :].rearrange("p k (g x) -> p k g x", x=1).broadcast_to([P, self.PT, NG, GE]),
                        ALU.mult).then_inc(self.rt, 2)
        assert self.CA == self.GC + 2

    def choose_top(self, e, c):
        self.chained(e, c, self.CA, fixed=True)
        for k in range(self.PT):
            last = e.max(self.em8[:, k, :], self.epad[:, k, 0:NE])
        last.then_inc(self.rt, 2)
        self.chained(e, c, self.CA + 1)
        e.memset(self.em8[:, :, TOPK:8], NEG).then_inc(self.rt, 2)
        assert self.CB == self.CA + 2

    def choose_found(self, e, c):
        self.chained(e, c, self.CB, fixed=True)
        for k in range(self.PT):
            last = e.match_replace(self.erep[:, k, :], self.em8[:, k, :], self.epad[:, k, :], TAKEN)
        last.then_inc(self.rt, 2)

    def choose_scores(self, e, c):
        self.chained(e, c, self.CB + 1)
        e.scalar_tensor_tensor(out=self.w[:, :, :], in0=self.erep[:, :, 0:NE], scalar=TAKEN,
                               in1=self.S[:, bass.ds((c - 1) * TT, self.PT), :], op0=ALU.is_equal, op1=ALU.mult).then_inc(self.rt, 2)
        self.chained(e, c, self.CB + 2)
        e.tensor_reduce(self.wsum[:, :], self.w[:, :, :], AX.X, ALU.add).then_inc(self.rt, 2)

    def choose_sum(self, e, c):
        self.chained(e, c, self.CB + 3)
        e.tensor_scalar(self.wsum[:, :], self.wsum[:, :], 1e-20, 1.0 / ROUTED_SCALE, ALU.add, ALU.mult).then_inc(self.rt, 2)
        assert self.RT == self.CB + 4

    def choose_weights(self, e, c):
        self.chained(e, c, self.RT)
        e.reciprocal(self.wrec[:, :], self.wsum[:, :]).then_inc(self.s_rec, 2)
        e.wait_ge(self.s_rec, c + 1)
        need(e, self.s_cs, c - 1)
        e.tensor_tensor(self.cf[:, :, :], self.w[:, :, :],
                        self.wrec[:, :].rearrange("p (k x) -> p k x", x=1).broadcast_to([P, self.PT, NE]),
                        ALU.mult).then_inc(self.s_cf, 2)

    def part1(self, e, c):
        e.wait_ge(self.s_cf, c + 1)
        need(e, self.c_turned, c - 1)
        e.activation(self.cs[:, :, 0:NE], self.cf[:, :, :], ACT.Copy).then_inc(self.s_p1, 2)

    def part2(self, e, c):
        e.wait_ge(self.s_r1, c + 1)
        e.activation(self.cs[:, :, NE:2 * NE], self.c1[:, :, :], ACT.Copy).then_inc(self.s_p2, 2)

    def part3(self, e, c):
        e.wait_ge(self.s_r2, c + 1)
        e.activation(self.cs[:, :, 2 * NE:3 * NE], self.c2[:, :, :], ACT.Copy).then_inc(self.s_cs, 2)

    def rest1(self, e, c):
        e.wait_ge(self.s_p1, c + 1)
        need(e, self.s_p2, c - 1)
        e.tensor_tensor(self.c1[:, :, :], self.cf[:, :, :], self.cs[:, :, 0:NE], ALU.subtract).then_inc(self.s_r1, 2)

    def rest2(self, e, c):
        e.wait_ge(self.s_r1, c + 1)
        e.wait_ge(self.s_p2, c + 1)
        need(e, self.s_cs, c - 1)
        e.tensor_tensor(self.c2[:, :, :], self.c1[:, :, :], self.cs[:, :, NE:2 * NE], ALU.subtract).then_inc(self.s_r2, 2)

    def turn_weights(self, e, c, bank):
        e.wait_ge(self.s_cs, c + 1)
        need(e, self.c_out, c - 1)
        for k in range(self.PT):
            last = e.transpose(bank[0:3 * NE, k * P:(k + 1) * P], self.cs[:, k, :], self.m["identb"][:, :])
        last.then_inc(self.c_turned, 2)

    def copy_weights(self, e, c, bank):
        e.wait_ge(self.c_turned, c + 1)
        e.activation(self.m["cT"][:, bass.ds((c - 1) * CH, 2 * CH)], bank[0:3 * NE, 0:2 * CH], ACT.Copy).then_inc(self.c_out, 2)


def second_block(nc, t, m, R):
    with ExitStack() as ctx:
        sb = lambda n, s, d=F32: ctx.enter_context(nc.sbuf_tensor(n, s, d))
        sem = lambda n: ctx.enter_context(nc.semaphore(n))
        ps = lambda n, d=F32, w=CH: ctx.enter_context(nc.psum_tensor(n, [P, w], d))
        two = lambda n, s=(P, CH), d=F32: [sb(f"{n}{k}", list(s), d) for k in range(2)]
        QP, KP, VP, GM, MP, OP, X3, LG = (ps(n) for n in ("q_pre", "k2_pre", "v_pre", "vv_sum", "m_pre", "o_tok", "x3_ch", "logits"))
        CT = MP[:, :].bitcast(BF16)
        GW, ST, TR, TB = GM, OP, X3, LG[:, :].bitcast(BF16)
        x2s, q, k_, qk = two("x2_static"), two("q"), two("k"), two("qk")
        v = two("v_tok", (P, TT, D))
        vvm, mp = two("vv_masked", (P, BC, P)), two("m_mix", (P, BC, P))
        z, x3k, x3s = two("z_attn", (P, TT, D)), two("x3_tok", (P, TT, D)), two("x3_static")
        n3 = Norm(ctx, nc, "norm3")
        prod = sb("w_gram_w", [P, 3, P])
        st = sb("bn_columns", [P, 8, 3])
        half = sb("half_power", [P, 3])
        vparts, vrest = sb("bias_parts", [P, 3], BF16), sb("bias_rest", [P, 2])
        mm, dv, pw, half_set = sem("bn_mm"), sem("bn_step"), sem("bn_rstd"), sem("half_power_set")
        WT = m["sqT"][:, SQ.index("Wq"):SQ.index("Wq") + 3, :]
        cols = m["cols"]
        gam = cols[:, COL["gq"]:COL["gq"] + 6].rearrange("p (b k) -> p k b", k=2)
        A, aux = m["act"], m["aux"]
        tv = lambda ap: ap.rearrange("p (k c) -> p k c", k=TT)

        x2_in, x3_kept = [sem("x2_in0"), sem("x2_in1")], [sem("x3_kept0"), sem("x3_kept1")]
        q_mm, k_mm, v_mm, s_q, s_k, s_v, s_qk = (sem(n) for n in ("q_mm", "k2_mm", "v2_mm", "q_done", "k_done", "v_done", "qk_done"))
        vv_mm, s_vvm, m_mm, s_mp, o_mm, s_zz = (sem(n) for n in ("vv_mm", "vvm_done", "m_mm", "mp_done", "o_mm", "zz_done"))
        x3_turned, x3_static, lg_mm = (sem(n) for n in ("x3_turned", "x3_static_done", "logits_mm"))

        def pairs(e, fn, *args):
            def stage(c, p):
                if p == 1 and not (isinstance(c, int) and c >= NCH - 2 * LATE):
                    fn(e, c, *args)
            return stage

        DV_V, DV_BIAS, DV_PARTS, DV_END = 8, 10, 15, 17
        block = ctx.enter_context(nc.Block())

        @block.sync
        def _(e):
            def load(c, p):
                need(e, q_mm, c - 1)
                need(e, k_mm, c - 1)
                need(e, v_mm, c - 1)
                e.dma_start(x2s[p][:, :], A[:, bass.ds(c * CH, CH)]).then_inc(x2_in[p], 16)

            def keep(c, p):
                e.wait_ge(x3_static, c + 1)
                e.dma_start(A[:, bass.ds(c * CH, CH)], x3s[p][:, :]).then_inc(x3_kept[p], 16)

            pipeline(e, [(0, load), (3, keep)], NCH, 3)
            for s in x3_kept:
                e.wait_ge(s, 8 * NCH)

        @block.tensor
        def _(e):
            def bn_sums():
                e.matmul(GW[:, 0:3 * P], m["gram"][:, 0:P], WT, start=True, stop=True).then_inc(mm, 1)
                for b in range(3):
                    e.matmul(ST[:, b:b + 1], WT[:, b, :], m["gram"][:, P:P + 1], start=(b == 0), stop=True,
                             skip_group_check=True)
                e.wait_ge(dv, 1)
                for b in range(3):
                    last = e.matmul(ST[:, 4 + b:5 + b], prod[:, b, :], m["ones"][:, 0:1], start=False, stop=True,
                                    skip_group_check=True)
                last.then_inc(mm, 1)

            def bn_values():
                e.wait_ge(dv, DV_V)
                e.transpose(TR[:, 0:P], m["wv_nat"][:, :], m["ident"][:, :]).then_inc(mm, 1)
                e.wait_ge(dv, DV_PARTS)
                e.transpose(TB[0:3, 0:P], vparts[:, :], m["identb"][:, :]).then_inc(mm, 1)
                e.wait_ge(dv, DV_END)

            def logits(c, p):
                e.wait_ge(x3_static, c + 1)
                need(e, R.s_S, c)
                for k in range(TT):
                    last = e.matmul(LG[:, k * NE:(k + 1) * NE], x3s[p][:, k * P:(k + 1) * P], m["gateT"][:, :],
                                    start=True, stop=True)
                last.then_inc(lg_mm, 1)

            def gram(c, p):
                e.wait_ge(s_v, c + 1)
                need(e, s_vvm, c)
                for b in range(BC):
                    for k in range(2):
                        last = e.matmul(GM[:, b * P:(b + 1) * P], v[p][:, 2 * b + k, :], v[p][:, 2 * b + k, :],
                                        start=(k == 0), stop=(k == 1))
                last.then_inc(vv_mm, 1)

            def project(c, p):
                first = isinstance(c, int) and c == 0
                if first:
                    bn_sums()
                project_qk(c, p)
                if first:
                    bn_values()

            def project_qk(c, p):
                e.wait_ge(x2_in[p], 8 * (c - p) + 16)
                need(e, s_q, c)
                e.matmul(QP[:, :], m["sqT"][:, SQ.index("Wq"), :], x2s[p][:, :], start=True, stop=True).then_inc(q_mm, 1)
                need(e, s_k, c)
                e.matmul(KP[:, :], m["sqT"][:, SQ.index("Wk"), :], x2s[p][:, :], start=True, stop=True).then_inc(k_mm, 1)

            def mix(c, p):
                e.wait_ge(s_vvm, c + 1)
                need(e, s_mp, c)
                need(e, R.c_out, min(c - 7 + (1 - p), NCH) if isinstance(c, int) else c - 7 + (1 - p))
                for b in range(BC):
                    last = e.matmul(MP[:, b * P:(b + 1) * P], vvm[p][:, b, :], m["sqT"][:, SQ.index("Wp"), :],
                                    start=True, stop=True)
                last.then_inc(m_mm, 1)

            def project_v(c, p):
                need(e, s_v, c)
                e.matmul(VP[:, :], m["onesb"][:, :], m["vb3"][:, :, :].rearrange("p k c -> p (k c)"), start=True, stop=False)
                for k in range(TT):
                    last = e.matmul(VP[:, k * P:(k + 1) * P], x2s[p][:, k * P:(k + 1) * P], m["wvT"][:, :],
                                    start=False, stop=(k == TT - 1))
                last.then_inc(v_mm, 1)

            def attend(c, p):
                e.wait_ge(s_mp, c + 1)
                e.wait_ge(s_qk, c + 1)
                need(e, s_zz, c)
                for k in range(TT):
                    last = e.matmul(OP[:, k * P:(k + 1) * P], qk[p][:, k * P:(k + 1) * P], mp[p][:, k // 2, :],
                                    start=True, stop=True)
                last.then_inc(o_mm, 1)

            def turn_x3(c, p):
                e.wait_ge(n3.normed, TT * (c + 1))
                need(e, x3_static, c)
                for k in range(TT):
                    last = e.transpose(X3[:, k * P:(k + 1) * P], x3k[p][:, k, :], m["ident"][:, :])
                last.then_inc(x3_turned, 1)

            turn_pair = pairs(e, R.turn_weights, CT)

            def turn_weights(c, p):
                if p == 1:
                    need(e, s_mp, min(c + 7, NCH) if isinstance(c, int) else c + 7)
                turn_pair(c, p)

            pipeline(e, [(3, turn_x3), (1, gram), (8, turn_weights), (0, project), (1, mix), (0, project_v),
                         (3, logits), (1, attend)], NCH, 8)

        @block.scalar
        def _(e):
            def norm3(c, p):
                need(e, x3_turned, c - 1)
                n3.apply_act(e, c, p, x3k[p], z[p])

            def scores(c, p):
                e.wait_ge(lg_mm, c + 1)
                e.activation(R.S[:, bass.ds(c * TT, TT), :], LG[:, 0:TT * NE].rearrange("p (k c) -> p k c", k=TT),
                             ACT.Sigmoid).then_inc(R.s_S, 1)

            def spikes(c, p):
                e.wait_ge(q_mm, c + 1)
                need(e, s_qk, c - 1)
                e.activation(q[p][:, :], QP[:, :], ACT.Sigmoid, bias=aux[:, 5:6], scale=aux[:, 2:3]).then_inc(s_q, 1)
                e.wait_ge(k_mm, c + 1)
                e.activation(k_[p][:, :], KP[:, :], ACT.Sigmoid, bias=aux[:, 6:7], scale=aux[:, 3:4]).then_inc(s_k, 1)

            def copy_m(c, p):
                e.wait_ge(m_mm, c + 1)
                need(e, o_mm, c - 1)
                e.activation(mp[p][:, :, :], MP[:, 0:BC * P].rearrange("p (b c) -> p b c", b=BC), ACT.Copy).then_inc(s_mp, 1)

            def spikes_v(c, p):
                e.wait_ge(v_mm, c + 1)
                need(e, vv_mm, c - 1)
                e.activation(v[p][:, :, :], tv(VP[:, :]), ACT.Sigmoid).then_inc(s_v, 1)

            def copy_x3(c, p):
                e.wait_ge(x3_turned, c + 1)
                need(e, lg_mm, c - 1)
                need(e, x3_kept[p], 8 * (c - p))
                e.activation(x3s[p][:, :], X3[:, :], ACT.Copy).then_inc(x3_static, 1)

            e.wait_ge(dv, DV_BIAS)
            pipeline(e, [(3, copy_x3), (8, pairs(e, R.copy_weights, CT)), (6, pairs(e, R.part1)), (0, spikes), (1, copy_m), (2, norm3),
                         (7, pairs(e, R.part3)), (0, spikes_v), (3, scores), (6, pairs(e, R.part2))], NCH, 8)

        @block.gpsimd
        def _(e):
            n3.setup(e)
            e.memset(half[:, :], -0.5).then_inc(half_set, 1)
            e.wait_ge(half_set, 1)
            e.wait_ge(dv, 5)
            e.tensor_tensor(st[:, 5, :], st[:, 4, :], half[:, :], ALU.pow).then_inc(pw, 1)

            def product(c, p):
                e.wait_ge(s_q, c + 1)
                e.wait_ge(s_k, c + 1)
                need(e, o_mm, c - 1)
                e.tensor_tensor(qk[p][:, :], q[p][:, :], k_[p][:, :], ALU.mult).then_inc(s_qk, 1)

            def root(c, p):
                n3.root(e, c, p)
                n3.shift(e, c, p)

            pipeline(e, [(7, pairs(e, R.rest2)), (6, pairs(e, R.rest1)), (0, product), (1, root)], NCH, 7)

        @block.vector
        def _(e):
            e.memset(R.gpad[:, :, NG:], NEG).then_inc(R.setup, 1)
            e.memset(R.epad[:, :, NE:], NEG).then_inc(R.setup, 1)
            e.wait_ge(R.setup, 2)
            n = [0]

            def done(ins):
                ins.then_inc(dv, 1)
                n[0] += 1
                e.wait_ge(dv, n[0])

            e.wait_ge(mm, 1)
            done(e.tensor_tensor(prod[:, :, :], GW[:, 0:3 * P].rearrange("p (b c) -> p b c", b=3), WT, ALU.mult))
            e.wait_ge(mm, 2)
            done(e.tensor_copy(st[:, 0, :], ST[:, 0:3]))
            done(e.tensor_tensor(st[:, 2, :], st[:, 0, :], st[:, 0, :], ALU.mult))
            done(e.scalar_tensor_tensor(out=st[:, 3, :], in0=st[:, 2, :], scalar=-1.0, in1=ST[:, 4:7],
                                        op0=ALU.mult, op1=ALU.add))
            done(e.tensor_scalar(st[:, 4, :], st[:, 3, :], 0.0, EPS, ALU.max, ALU.add))
            e.wait_ge(pw, 1)
            done(e.scalar_tensor_tensor(out=st[:, 6, :], in0=st[:, 5, :], scalar=4.0, in1=gam[:, 0, :],
                                        op0=ALU.mult, op1=ALU.mult))
            done(e.tensor_tensor(st[:, 7, :], st[:, 0, :], st[:, 6, :], ALU.mult))
            e.tensor_copy(aux[:, 2:5], st[:, 6, :])
            done(e.tensor_scalar(m["wv_nat"][:, :], m["wv_nat"][:, :], st[:, 6, 2:3], None, ALU.mult))
            done(e.tensor_scalar(aux[:, 5:8], gam[:, 1, :], -V_TH, 4.0, ALU.add, ALU.mult))
            done(e.tensor_tensor(aux[:, 5:8], aux[:, 5:8], st[:, 7, :], ALU.subtract))
            assert n[0] == DV_BIAS
            bias = aux[:, 7:8]
            done(e.tensor_copy(vparts[:, 0:1], bias))
            done(e.tensor_tensor(vrest[:, 0:1], bias, vparts[:, 0:1], ALU.subtract))
            done(e.tensor_copy(vparts[:, 1:2], vrest[:, 0:1]))
            done(e.tensor_tensor(vrest[:, 1:2], vrest[:, 0:1], vparts[:, 1:2], ALU.subtract))
            done(e.tensor_copy(vparts[:, 2:3], vrest[:, 1:2]))
            assert n[0] == DV_PARTS
            e.wait_ge(mm, 3)
            done(e.tensor_copy(m["wvT"][:, :], TR[:, 0:P]))
            e.wait_ge(mm, 4)
            done(e.tensor_copy(m["vb3"][:, :, :], TB[0:3, 0:P].rearrange("p (k c) -> p k c", k=1).broadcast_to([3, TT, P])))
            assert n[0] == DV_END
            def mask(c, p):
                e.wait_ge(vv_mm, c + 1)
                need(e, m_mm, c - 1)
                for b in range(BC):
                    last = e.scalar_tensor_tensor(out=vvm[p][:, b, :], in0=GM[:, b * P:(b + 1) * P],
                                                  scalar=float(HD) ** -0.5, in1=m["headmask"][:, :],
                                                  op0=ALU.mult, op1=ALU.mult)
                last.then_inc(s_vvm, 1)

            def residual(c, p):
                e.wait_ge(o_mm, c + 1)
                need(e, n3.normed, TT * (c - 1))
                e.tensor_tensor(z[p][:, :, :], tv(OP[:, :]), m["tok"][:, bass.ds(c * TT, TT), :], ALU.add).then_inc(s_zz, 1)

            def stats(c, p):
                e.wait_ge(s_zz, c + 1)
                n3.stats(e, c, p, z[p])

            def aggregate(c, p):
                n3.aggregate(e, c, p)

            r = lambda fn: pairs(e, fn)
            pipeline(e, [(4, r(R.groups_scores)), (5, r(R.choose_top)), (4, r(R.groups_top)),
                         (5, r(R.choose_found)), (4, r(R.groups_found)), (5, r(R.choose_scores)), (1, residual),
                         (4, r(R.groups_kept)), (5, r(R.choose_sum)), (1, stats), (5, r(R.choose_weights)),
                         (0, mask), (1, aggregate)], NCH, 5)


def experts_block(nc, t, m, R, out):
    with ExitStack() as ctx:
        sb = lambda n, s, d=F32: ctx.enter_context(nc.sbuf_tensor(n, s, d))
        sem = lambda n: ctx.enter_context(nc.semaphore(n))
        ps = lambda n: ctx.enter_context(nc.psum_tensor(n, [P, CH], F32))
        U, C, O = [ps(f"up{k}") for k in range(3)], [ps(f"weight{k}") for k in range(2)], [ps(f"down{k}") for k in range(2)]
        TK = ps("out_tok")
        CT = TK[:, :].bitcast(BF16)
        late_dve = {(0, 1): R.groups_scores, (0, 4): R.groups_top, (0, 7): R.groups_found, (0, 10): R.groups_kept,
                    (0, 16): R.choose_top, (1, 0): R.choose_found, (1, 2): R.choose_scores, (1, 5): R.choose_sum,
                    (1, 6): R.choose_weights}
        late_act = {(1, 8): R.part1, (1, 11): R.part2, (1, 14): R.part3,
                    (1, NB - 1): lambda e, c: R.copy_weights(e, c, CT)}
        late_pool = {(1, 9): R.rest1, (1, 12): R.rest2}

        def late(e, pieces, c, j):
            if isinstance(c, int) and c < 2 * LATE and (c % 2, j) in pieces:
                pieces[c % 2, j](e, NCH - 2 * LATE + c // 2 * 2 + 1)
        NR = 3
        r, tt, h = ([sb(f"{n}{k}", [P, CH]) for k in range(NR)] for n in ("relu", "relu_w", "hid"))
        hh, hl = ([sb(f"{n}{k}", [P, CH], F32R) for k in range(NR)] for n in ("hid_hi", "hid_lo"))
        xh, xl = ([sb(f"{n}{k}", [P, CH], F32R) for k in range(2)] for n in ("x3_hi", "x3_lo"))
        oT = [sb(f"outT{k}", [P, CH]) for k in range(2)]
        x4 = [sb(f"x4_tok{k}", [P, TT, D]) for k in range(2)]
        n4 = Norm(ctx, nc, "norm4")
        s_xh, s_xl, u_mm, c_mm, s_r, s_t, s_h, s_hs, s_hh, s_hl, d_mm, s_o, o_turned = (
            sem(n) for n in ("x_hi_done", "x_lo_done", "up_mm", "weight_mm", "relu_done", "relu_w_done", "hid_done", "shared_hid_done",
                             "hid_hi_done", "hid_lo_done", "down_mm", "out_copied", "out_turned"))
        stored = [sem("x4_stored0"), sem("x4_stored1")]
        A = m["act"]
        tv = lambda ap: ap.rearrange("p (k c) -> p k c", k=TT)
        of = out.rearrange("b t c -> (b t) c")
        LAG, SLAG = 4, 2
        WL = 7
        block = ctx.enter_context(nc.Block())

        def hid_done(eng, c, j):
            if j < 0:
                c, j = c - 1, j + NB
            if isinstance(c, int) and c < 0:
                return
            if j < NRB:
                eng.wait_ge(s_h, NRB * c + j + 1)
            else:
                eng.wait_ge(s_hs, (NB - NRB) * c + j - NRB + 1)

        def chunks(eng, body, tail):
            for c in range(2 * LATE):
                body(c, c % 2)
            with eng.Fori(LATE, NCH // 2 - 1) as i:
                body(2 * i, 0)
                body(2 * i + 1, 1)
            body(NCH - 2, 0)
            body(NCH - 1, 1)
            tail()

        @block.tensor
        def _(e):
            def up(c, p, j):
                g = c * NB + j
                if j == 0:
                    e.wait_ge(s_xl, c + 1)
                need(e, s_r, g - 2)
                uk = U[j % 3]
                e.matmul(uk[:, :], m["up_hi"][:, j, :], xh[p][:, :], start=True, stop=False)
                e.matmul(uk[:, :], m["up_hi"][:, j, :], xl[p][:, :], start=False, stop=False)
                e.matmul(uk[:, :], m["up_lo"][:, j, :], xh[p][:, :], start=False, stop=True).then_inc(u_mm, 1)
                if j < NRB:
                    need(e, s_t, c * NRB + j - 1)
                    e.matmul(C[j % 2][:, :], m["sel"][:, j, :], m["cT"][:, bass.ds(c * CH, CH)],
                             start=True, stop=True).then_inc(c_mm, 1)

            def down(c, p, j):
                g = c * NB + j
                if j == 0:
                    need(e, s_o, c - 1)
                e.wait_ge(s_hh, g + 1)
                e.matmul(O[p][:, :], m["dn_hi"][:, j, :], hh[j % NR][:, :], start=(j == 0), stop=False)
                e.matmul(O[p][:, :], m["dn_lo"][:, j, :], hh[j % NR][:, :], start=False, stop=False)
                e.wait_ge(s_hl, g + 1)
                last = e.matmul(O[p][:, :], m["dn_hi"][:, j, :], hl[j % NR][:, :], start=False, stop=(j == NB - 1))
                last.then_inc(d_mm, 1)

            def turn(c, p):
                e.wait_ge(s_o, c + 1)
                need(e, n4.normed, TT * c)
                e.wait_ge(R.c_out, NCH - 2 * LATE + (c + 1) // 2 * 2 if isinstance(c, int) and c < 2 * LATE else NCH)
                for k in range(TT):
                    last = e.transpose(TK[:, k * P:(k + 1) * P], oT[p][:, k * P:(k + 1) * P], m["ident"][:, :])
                last.then_inc(o_turned, 1)

            def body(c, p):
                for j in range(NB):
                    up(c, p, j)
                    if j >= LAG:
                        down(c, p, j - LAG)
                    elif not (isinstance(c, int) and c == 0):
                        down(c - 1, 1 - p, NB - LAG + j)
                    if j == WL and not (isinstance(c, int) and c == 0):
                        turn(c - 1, 1 - p)
                    if isinstance(c, int) and c < 2 * LATE and (c % 2, j) == (1, NB - 1):
                        e.wait_ge(n4.normed, TT * c)
                        R.turn_weights(e, NCH - 2 * LATE + c, CT)

            def tail():
                for j in range(LAG):
                    down(NCH - 1, 1, NB - LAG + j)
                turn(NCH - 1, 1)
            chunks(e, body, tail)

        @block.scalar
        def _(e):
            def split(c, p):
                need(e, d_mm, NB * (c - 2 + 1))
                e.activation(xh[p][:, :], A[:, bass.ds(c * CH, CH)], ACT.Copy).then_inc(s_xh, 1)

            def relu(c, j):
                e.wait_ge(u_mm, c * NB + j + 1)
                hid_done(e, c, j - NR)
                e.activation(r[j % NR][:, :], U[j % 3][:, :], ACT.Relu).then_inc(s_r, 1)

            def hi(c, j):
                g = c * NB + j
                hid_done(e, c, j)
                need(e, d_mm, g - NR + 1)
                e.activation(hh[j % NR][:, :], h[j % NR][:, :], ACT.Copy).then_inc(s_hh, 1)

            def norm(c, p):
                e.wait_ge(stored[p], 8 * (c - p) + 16)
                n4.apply_act(e, c, p, x4[p], tv(TK[:, :]))

            def body(c, p):
                first = isinstance(c, int) and c == 0
                if first:
                    split(0, 0)
                for j in range(NB):
                    relu(c, j)
                    if j >= SLAG:
                        hi(c, j - SLAG)
                    elif not first:
                        hi(c - 1, NB - SLAG + j)
                    if j == WL + 8 and not first:
                        norm(c - 1, 1 - p)
                    late(e, late_act, c, j)
                    if j == 9 and not (isinstance(c, int) and c == NCH - 1):
                        split(c + 1, 1 - p)

            def tail():
                for j in range(SLAG):
                    hi(NCH - 1, NB - SLAG + j)
                norm(NCH - 1, 1)
            chunks(e, body, tail)

        @block.vector
        def _(e):
            def weigh(c, j):
                e.wait_ge(s_r, c * NB + j + 1)
                if j >= NRB:
                    need(e, s_hl, c * NB + j - NR + 1)
                    e.tensor_tensor(h[j % NR][:, :], r[j % NR][:, :], r[j % NR][:, :], ALU.mult).then_inc(s_hs, 1)
                    return
                e.wait_ge(c_mm, c * NRB + j + 1)
                need(e, s_h, c * NRB + max(j - NR + 1, 0))
                e.tensor_tensor(tt[j % NR][:, :], C[j % 2][:, :], r[j % NR][:, :], ALU.mult).then_inc(s_t, 1)

            def lo(c, j):
                g = c * NB + j
                e.wait_ge(s_hh, g + 1)
                need(e, d_mm, g - NR + 1)
                e.tensor_tensor(hl[j % NR][:, :], h[j % NR][:, :], hh[j % NR][:, :].bitcast(F32), ALU.subtract).then_inc(s_hl, 1)

            def split(c, p):
                e.wait_ge(s_xh, c + 1)
                e.tensor_tensor(xl[p][:, :], A[:, bass.ds(c * CH, CH)], xh[p][:, :].bitcast(F32), ALU.subtract).then_inc(s_xl, 1)

            def residual(c, p):
                e.wait_ge(d_mm, NB * (c + 1))
                need(e, o_turned, c)
                e.tensor_tensor(oT[p][:, :], O[p][:, :], A[:, bass.ds(c * CH, CH)], ALU.add).then_inc(s_o, 1)

            def stats(c, p, k):
                e.wait_ge(o_turned, c + 1)
                n4.stats(e, c, p, tv(TK[:, :]), range(k, k + 1))

            def body(c, p):
                first = isinstance(c, int) and c == 0
                if first:
                    split(0, 0)
                for j in range(NB):
                    weigh(c, j)
                    if j >= SLAG:
                        lo(c, j - SLAG)
                    elif not first:
                        lo(c - 1, NB - SLAG + j)
                    late(e, late_dve, c, j)
                    if j == LAG and not first:
                        residual(c - 1, 1 - p)
                    if 0 < j - WL <= TT and not first:
                        stats(c - 1, 1 - p, j - WL - 1)
                    if j == WL + TT + 1 and not first:
                        n4.aggregate(e, c - 1, 1 - p)
                    if j == WL + TT + 2 and not (isinstance(c, int) and c == NCH - 1):
                        split(c + 1, 1 - p)

            def tail():
                for j in range(SLAG):
                    lo(NCH - 1, NB - SLAG + j)
                residual(NCH - 1, 1)
                for k in range(TT):
                    stats(NCH - 1, 1, k)
                n4.aggregate(e, NCH - 1, 1)
            chunks(e, body, tail)

        @block.gpsimd
        def _(e):
            n4.setup(e)

            def square(c, j):
                if j >= NRB:
                    return
                e.wait_ge(s_r, c * NB + j + 1)
                need(e, s_hl, c * NB + j - NR + 1)
                e.wait_ge(s_t, c * NRB + j + 1)
                e.tensor_tensor(h[j % NR][:, :], tt[j % NR][:, :], r[j % NR][:, :], ALU.mult).then_inc(s_h, 1)

            def body(c, p):
                first = isinstance(c, int) and c == 0
                for j in range(NB):
                    square(c, j)
                    late(e, late_pool, c, j)
                    if j == WL + 6 and not first:
                        n4.root(e, c - 1, 1 - p)
                        n4.shift(e, c - 1, 1 - p)

            def tail():
                n4.root(e, NCH - 1, 1)
                n4.shift(e, NCH - 1, 1)
            chunks(e, body, tail)

        @block.sync
        def _(e):
            def store(c, p):
                e.wait_ge(n4.normed, TT * (c + 1))
                e.dma_start(of[bass.ds(c * CH, CH), :].rearrange("(k p) c -> p k c", p=P), x4[p][:, :, :]).then_inc(stored[p], 16)
            for s in stored:
                e.sem_inc(s, 16)
            chunks(e, store, lambda: [e.wait_ge(s, 8 * NCH + 16) for s in stored])


_INS = {
    "L0_attn_x": "x", "L0_attn_A": "A", "L0_attn_Wb": "Wb", "L0_attn_bb": "bb", "L0_attn_Wc": "Wc", "L0_attn_bc": "bc",
    "L0_attn_Wd": "Wd", "L0_attn_bd": "bd", "L0_attn_Wdelta": "Wdelta", "L0_attn_bdelta": "bdelta",
    "L0_ffn_W_r": "W_r", "L0_ffn_W_k": "W_k", "L0_ffn_W_v": "W_v", "L0_ffn_mu_r": "mu_r", "L0_ffn_mu_k": "mu_k",
    "L1_attn_Wq": "Wq", "L1_attn_gq": "gq", "L1_attn_bq": "bq", "L1_attn_Wk": "Wk", "L1_attn_gk": "gk",
    "L1_attn_bk": "bk", "L1_attn_Wv": "Wv", "L1_attn_gv": "gv", "L1_attn_bv": "bv", "L1_attn_Wp": "Wp",
    "L1_attn_bp": "bp", "L1_ffn_gate_w": "gate_w", "L1_ffn_e_bias": "e_bias", "L1_ffn_up_w": "up_w",
    "L1_ffn_down_w": "down_w", "L1_ffn_shared_up_w": "shared_up_w", "L1_ffn_shared_down_w": "shared_down_w",
}


def kernel(**inputs):
    import numpy as _np
    import concourse.bacc as _bacc
    from concourse import mybir as _mybir
    from concourse.bass_utils import run_bass_kernel_spmd as _run

    nc = _bacc.Bacc("TRN2", target_bir_lowering=False, num_devices=1)
    arrays, args = {}, {}
    for name, short in _INS.items():
        a = _np.ascontiguousarray(inputs[name])
        arrays[f"in_{name}_dram"] = a
        args[short] = nc.dram_tensor(f"in_{name}_dram", a.shape, _mybir.dt.from_np(a.dtype), kind="ExternalInput").ap()
    out = nc.dram_tensor("out_0_dram", (B, T, D), _mybir.dt.float32, kind="ExternalOutput").ap()
    build(nc, args, out)
    r = _run(nc, [arrays], core_ids=[0])
    return r.results[0]["out_0_dram"]
```
